# Optimizing a Trainium2 kernel written in Bass

```python
import numpy as np
import jax
import jax.numpy as jnp

def _softmax(x, axis=-1):
    return jax.nn.softmax(x, axis=axis)

def _gelu(x):
    return jax.nn.gelu(x, approximate=True)

def _silu(x):
    return jax.nn.silu(x)

def _sigmoid(x):
    return jax.nn.sigmoid(x)

def _layernorm(x, axis=-1, eps=1e-05):
    m = jnp.mean(x, axis=axis, keepdims=True)
    v = jnp.var(x, axis=axis, keepdims=True)
    return (x - m) / jnp.sqrt(v + eps)

def _scatter_add(tgt, idx, src, axis=0):
    return tgt.at[idx].add(src)

def _segment_sum(src, seg, n):
    return jax.ops.segment_sum(src, seg, n)
kernel_name = 'mk_flamingo_gated_d2_seqx_r8_5a418d'

def setup_inputs(seed: int=0):
    np.random.seed(seed)
    _w = jnp.asarray

    def _rec_inputs():
        import jax
        import jax.numpy as jnp
        _rk = jax.random.key(seed)
        x = -0.0002928 + 1 * jax.random.normal(jax.random.fold_in(_rk, 1), (64, 64, 128), jnp.float32)
        _lenS = 64 - jax.random.randint(jax.random.fold_in(_rk, 7), (64,), 0, max(1, 64 // 4) + 1, jnp.int32)
        _lenS2 = 64 - jax.random.randint(jax.random.fold_in(_rk, 8), (64,), 0, max(1, 64 // 4) + 1, jnp.int32)
        _ctx_1024P = jax.random.normal(jax.random.fold_in(_rk, 11), (64, 16, 128), jnp.float32)
        _ctx_1024c = jax.random.dirichlet(jax.random.fold_in(_rk, 511), 0.3 * jnp.ones((16,), jnp.float32), (64, 64))
        _ctx_1024t = jnp.einsum('bsk,bkd->bsd', _ctx_1024c, _ctx_1024P)
        _ctx_1024t = _ctx_1024t * jax.lax.rsqrt(jnp.mean(jnp.square(_ctx_1024t)) + 1e-12) * 0.953939
        ctx_1024 = -1.39393e-06 + 0.999914 * (_ctx_1024t + 0.3 * jax.random.normal(jax.random.fold_in(_rk, 611), (64, 64, 128), jnp.float32))
        _validS = jnp.arange(64)[None, :] < _lenS[:, None]
        _validS2 = jnp.arange(64)[None, :] < _lenS2[:, None]
        _causal = jnp.tril(jnp.ones((64, 64), dtype=bool))
        mask_BxSxS2_ik1 = jnp.where(jnp.broadcast_to(_validS2[:, None, :], (64, 64, 64)), 1, 0).astype(jnp.int32)
        _g = jax.random.normal(jax.random.fold_in(_rk, 9001), (2, 2), jnp.float32)
        _g = jnp.sign(_g) * jnp.maximum(jnp.abs(_g), 1.0) + (_g == 0) * 1.0
        g_xattn = _g[0]
        g_ffn = _g[1]
        return (x, ctx_1024, mask_BxSxS2_ik1, g_xattn, g_ffn)
    x, ctx_1024, mask_BxSxS2_ik1, g_xattn, g_ffn = _rec_inputs()

    def _L0_xattn_setup():
        import jax, jax.numpy as jnp
        import numpy as np
        H = 16
        D_MODEL = 128
        D_K = D_MODEL // H
        key = jax.random.key(seed)
        ks = jax.random.split(key, 12)
        B, S = (2, 256)
        scale = 1.0 / np.sqrt(D_MODEL)
        inp = {'query': jax.random.normal(ks[0], (B, S, D_MODEL), jnp.float32), 'key': jax.random.normal(ks[1], (B, S, D_MODEL), jnp.float32), 'value': jax.random.normal(ks[2], (B, S, D_MODEL), jnp.float32), 'mask': jax.random.randint(ks[3], (B, S, S), 0, 2, jnp.int32), 'w_q': jax.random.normal(ks[4], (D_MODEL, D_MODEL), jnp.float32) * scale, 'b_q': jnp.zeros((D_MODEL,), jnp.float32), 'w_k': jax.random.normal(ks[5], (D_MODEL, D_MODEL), jnp.float32) * scale, 'b_k': jnp.zeros((D_MODEL,), jnp.float32), 'w_v': jax.random.normal(ks[6], (D_MODEL, D_MODEL), jnp.float32) * scale, 'b_v': jnp.zeros((D_MODEL,), jnp.float32), 'w_o': jax.random.normal(ks[7], (D_MODEL, D_MODEL), jnp.float32) * scale, 'b_o': jnp.zeros((D_MODEL,), jnp.float32)}
        return inp
    _L0_xattn_all = _L0_xattn_setup()
    _L0_xattn_in = {k: v for k, v in _L0_xattn_all.items() if k in ('w_q', 'b_q', 'w_k', 'b_k', 'w_v', 'b_v', 'w_o', 'b_o')}
    del _L0_xattn_all

    def _L0_ffn_setup():
        import jax, jax.numpy as jnp
        import numpy as np
        DIM, HIDDEN, E = (128, 512, 8)
        B, L = (2, 256)
        key = jax.random.key(seed)
        ks = jax.random.split(key, 6)
        s_in = 1.0 / np.sqrt(DIM)
        s_h = 1.0 / np.sqrt(HIDDEN)
        return {'x': jax.random.normal(ks[0], (B, L, DIM), dtype=jnp.float32), 'Wg': jax.random.uniform(ks[1], (E, DIM), jnp.float32, -s_in, s_in), 'W1': jax.random.uniform(ks[2], (E, DIM, HIDDEN), jnp.float32, -s_in, s_in), 'b1': jax.random.uniform(ks[3], (E, HIDDEN), jnp.float32, -s_in, s_in), 'W2': jax.random.uniform(ks[4], (E, HIDDEN, DIM), jnp.float32, -s_h, s_h), 'b2': jax.random.uniform(ks[5], (E, DIM), jnp.float32, -s_h, s_h)}
    _L0_ffn_all = _L0_ffn_setup()
    _L0_ffn_in = {k: v for k, v in _L0_ffn_all.items() if k in ('Wg', 'W1', 'b1', 'W2', 'b2')}
    del _L0_ffn_all

    def _L1_xattn_setup():
        import jax, jax.numpy as jnp
        import numpy as np
        B, S, D, H = (2, 256, 128, 16)
        key = jax.random.key(seed)
        ks = jax.random.split(key, 7)
        scale_in = (6.0 / (D + 3 * D)) ** 0.5
        scale_out = (6.0 / (D + D)) ** 0.5
        return {'query': jax.random.normal(ks[0], (B, S, D), jnp.float32), 'key': jax.random.normal(ks[1], (B, S, D), jnp.float32), 'value': jax.random.normal(ks[2], (B, S, D), jnp.float32), 'in_proj_weight': jax.random.uniform(ks[3], (D, 3 * D), jnp.float32, -scale_in, scale_in), 'in_proj_bias': jnp.zeros((3 * D,), jnp.float32), 'out_proj_weight': jax.random.uniform(ks[4], (D, D), jnp.float32, -scale_out, scale_out), 'out_proj_bias': jnp.zeros((D,), jnp.float32), 'num_heads': H}
    _L1_xattn_all = _L1_xattn_setup()
    _L1_xattn_in = {k: v for k, v in _L1_xattn_all.items() if k in ('in_proj_weight', 'in_proj_bias', 'out_proj_weight', 'out_proj_bias')}
    del _L1_xattn_all

    def _L1_ffn_setup():
        import jax, jax.numpy as jnp
        import numpy as np
        E = 16
        K = 2
        LOAD = 1.0

        def _dispatch(xb, pb, cap):
            T, C = xb.shape
            top_k_probs, ei = jax.lax.top_k(pb, K)
            flat = ei.swapaxes(0, 1).ravel()
            one_hot = jax.nn.one_hot(flat, E, dtype=jnp.int32)
            pos = jnp.cumsum(one_hot, axis=0) * one_hot
            pos = pos.reshape(K, T, E).swapaxes(0, 1)
            pos = jnp.max(pos, axis=-1) - 1
            ei2 = flat.reshape(K, T).swapaxes(0, 1)
            xr = jnp.repeat(xb, K, axis=0)
            buf = jnp.zeros((E, cap, C), xb.dtype)
            buf = buf.at[ei2.ravel(), pos.ravel()].set(xr, mode='drop')
            return (top_k_probs, pos, ei2, buf)

        def _collect(eo_b, ei_b, pos_b, tk_b):
            out = eo_b[ei_b, pos_b]
            return jnp.sum(tk_b[..., None] * out, axis=1)
        key = jax.random.key(seed)
        k1, k2, k3, k4, k5 = jax.random.split(key, 5)
        B, T, C, H = (8, 512, 128, 64)
        n_layer = 12
        x = jax.random.normal(k1, (B, T, C), dtype=jnp.float32)
        w_router = jax.random.normal(k2, (C, E), dtype=jnp.float32) * 0.02
        w_fc = jax.random.normal(k3, (E, C, H), dtype=jnp.float32) * 0.02
        w_gate = jax.random.normal(k4, (E, C, H), dtype=jnp.float32) * 0.02
        w_proj = jax.random.normal(k5, (E, H, C), dtype=jnp.float32) * (0.02 * (2 * n_layer) ** (-0.5))
        return {'x': x, 'w_router': w_router, 'w_fc': w_fc, 'w_gate': w_gate, 'w_proj': w_proj}
    _L1_ffn_all = _L1_ffn_setup()
    _L1_ffn_in = {k: v for k, v in _L1_ffn_all.items() if k in ('w_router', 'w_fc', 'w_gate', 'w_proj')}
    del _L1_ffn_all
    return {'x': x, 'ctx_1024': ctx_1024, 'mask_BxSxS2_ik1': mask_BxSxS2_ik1, 'g_xattn': g_xattn, 'g_ffn': g_ffn, 'L0_xattn_w_q': _L0_xattn_in['w_q'], 'L0_xattn_b_q': _L0_xattn_in['b_q'], 'L0_xattn_w_k': _L0_xattn_in['w_k'], 'L0_xattn_b_k': _L0_xattn_in['b_k'], 'L0_xattn_w_v': _L0_xattn_in['w_v'], 'L0_xattn_b_v': _L0_xattn_in['b_v'], 'L0_xattn_w_o': _L0_xattn_in['w_o'], 'L0_xattn_b_o': _L0_xattn_in['b_o'], 'L0_ffn_Wg': _L0_ffn_in['Wg'], 'L0_ffn_W1': _L0_ffn_in['W1'], 'L0_ffn_b1': _L0_ffn_in['b1'], 'L0_ffn_W2': _L0_ffn_in['W2'], 'L0_ffn_b2': _L0_ffn_in['b2'], 'L1_xattn_in_proj_weight': _L1_xattn_in['in_proj_weight'], 'L1_xattn_in_proj_bias': _L1_xattn_in['in_proj_bias'], 'L1_xattn_out_proj_weight': _L1_xattn_in['out_proj_weight'], 'L1_xattn_out_proj_bias': _L1_xattn_in['out_proj_bias'], 'L1_ffn_w_router': _L1_ffn_in['w_router'], 'L1_ffn_w_fc': _L1_ffn_in['w_fc'], 'L1_ffn_w_gate': _L1_ffn_in['w_gate'], 'L1_ffn_w_proj': _L1_ffn_in['w_proj']}

def reference(x, ctx_1024, mask_BxSxS2_ik1, g_xattn, g_ffn, L0_xattn_w_q, L0_xattn_b_q, L0_xattn_w_k, L0_xattn_b_k, L0_xattn_w_v, L0_xattn_b_v, L0_xattn_w_o, L0_xattn_b_o, L0_ffn_Wg, L0_ffn_W1, L0_ffn_b1, L0_ffn_W2, L0_ffn_b2, L1_xattn_in_proj_weight, L1_xattn_in_proj_bias, L1_xattn_out_proj_weight, L1_xattn_out_proj_bias, L1_ffn_w_router, L1_ffn_w_fc, L1_ffn_w_gate, L1_ffn_w_proj):
    import jax
    import jax.numpy as jnp

    def _L0_xattn_ref(query, key, value, mask, w_q, b_q, w_k, b_k, w_v, b_v, w_o, b_o):
        import jax, jax.numpy as jnp
        import numpy as np
        H = 16
        D_MODEL = 128
        D_K = D_MODEL // H
        B, S, _ = query.shape
        q = query @ w_q.T + b_q
        k = key @ w_k.T + b_k
        v = value @ w_v.T + b_v
        q = q.reshape(B, S, H, D_K).transpose(0, 2, 1, 3)
        k = k.reshape(B, S, H, D_K).transpose(0, 2, 1, 3)
        v = v.reshape(B, S, H, D_K).transpose(0, 2, 1, 3)
        scores = jnp.einsum('bhqd,bhkd->bhqk', q, k)
        m = mask[:, None, :, :]
        scores = jnp.where(m == 0, jnp.float32(-1000000000.0), scores)
        scores = scores / jnp.sqrt(jnp.float32(D_K))
        attn = jax.nn.softmax(scores, axis=-1)
        ctx = jnp.einsum('bhqk,bhkd->bhqd', attn, v)
        ctx = ctx.transpose(0, 2, 1, 3).reshape(B, S, H * D_K)
        return ctx @ w_o.T + b_o

    def _L0_ffn_ref(x, Wg, W1, b1, W2, b2):
        import jax, jax.numpy as jnp
        import numpy as np
        DIM, HIDDEN, E = (128, 512, 8)
        B, L = (2, 256)
        gate_logits = jnp.einsum('bld,ed->ble', x, Wg)
        top1 = jnp.argmax(gate_logits, axis=-1)
        out = jnp.zeros_like(x)
        for e in range(E):
            mask = (top1 == e)[..., None]
            h = jax.nn.gelu(jnp.einsum('bld,dh->blh', x, W1[e]) + b1[e], approximate=False)
            y = jnp.einsum('blh,hd->bld', h, W2[e]) + b2[e]
            out = jnp.where(mask, y, out)
        return out

    def _L1_xattn_ref(query, key, value, in_proj_weight, in_proj_bias, out_proj_weight, out_proj_bias, num_heads):
        import jax, jax.numpy as jnp
        import numpy as np
        B, S, D, H = (2, 256, 128, 16)
        qbs, qss, qds = query.shape
        b, s, d = value.shape
        qw, kw, vw = jnp.split(in_proj_weight, 3, axis=-1)
        qb, kb, vb = jnp.split(in_proj_bias, 3, axis=-1)
        q = (query @ qw + qb).reshape(qbs, qss, num_heads, -1)
        k = (key @ kw + kb).reshape(b, s, num_heads, -1)
        v = (value @ vw + vb).reshape(b, s, num_heads, -1)
        scale = q.shape[-1] ** (-0.5)
        scores = jnp.einsum('bqhd,bkhd->bhqk', q * scale, k)
        attn = jax.nn.softmax(scores, axis=-1)
        out = jnp.einsum('bhqk,bkhd->bqhd', attn, v)
        return out.reshape(qbs, qss, qds) @ out_proj_weight + out_proj_bias

    def _L1_ffn_ref(x, w_router, w_fc, w_gate, w_proj):
        import jax, jax.numpy as jnp
        import numpy as np
        E = 16
        K = 2
        LOAD = 1.0

        def _dispatch(xb, pb, cap):
            T, C = xb.shape
            top_k_probs, ei = jax.lax.top_k(pb, K)
            flat = ei.swapaxes(0, 1).ravel()
            one_hot = jax.nn.one_hot(flat, E, dtype=jnp.int32)
            pos = jnp.cumsum(one_hot, axis=0) * one_hot
            pos = pos.reshape(K, T, E).swapaxes(0, 1)
            pos = jnp.max(pos, axis=-1) - 1
            ei2 = flat.reshape(K, T).swapaxes(0, 1)
            xr = jnp.repeat(xb, K, axis=0)
            buf = jnp.zeros((E, cap, C), xb.dtype)
            buf = buf.at[ei2.ravel(), pos.ravel()].set(xr, mode='drop')
            return (top_k_probs, pos, ei2, buf)

        def _collect(eo_b, ei_b, pos_b, tk_b):
            out = eo_b[ei_b, pos_b]
            return jnp.sum(tk_b[..., None] * out, axis=1)
        B, T, C = x.shape
        cap = int(LOAD * K * max(1, T / E))
        g = jnp.einsum('btc,ce->bte', x, w_router)
        gate_probs = jax.nn.softmax(g, axis=-1)
        top_k_probs, positions, indices, expert_inputs = jax.vmap(lambda xb, pb: _dispatch(xb, pb, cap))(x, gate_probs)
        expert_inputs = jnp.swapaxes(expert_inputs, 0, 1).reshape(E, B * cap, C)
        gg = jnp.einsum('enc,ech->enh', expert_inputs, w_gate)
        h = jnp.einsum('enc,ech->enh', expert_inputs, w_fc)
        h = jax.nn.silu(gg) * h
        o = jnp.einsum('enh,ehc->enc', h, w_proj)
        expert_outputs = jnp.swapaxes(o.reshape(E, B, cap, C), 0, 1)
        y = jax.vmap(_collect)(expert_outputs, indices, positions, top_k_probs)
        return y
    x = x + jnp.tanh(g_xattn[0]) * _L0_xattn_ref(_layernorm(x, axis=-1), ctx_1024, ctx_1024, mask_BxSxS2_ik1, L0_xattn_w_q, L0_xattn_b_q, L0_xattn_w_k, L0_xattn_b_k, L0_xattn_w_v, L0_xattn_b_v, L0_xattn_w_o, L0_xattn_b_o)
    x = x + jnp.tanh(g_ffn[0]) * _L0_ffn_ref(_layernorm(x, axis=-1), L0_ffn_Wg, L0_ffn_W1, L0_ffn_b1, L0_ffn_W2, L0_ffn_b2)
    x = x + jnp.tanh(g_xattn[1]) * _L1_xattn_ref(_layernorm(x, axis=-1), ctx_1024, ctx_1024, L1_xattn_in_proj_weight, L1_xattn_in_proj_bias, L1_xattn_out_proj_weight, L1_xattn_out_proj_bias, 16)
    x = x + jnp.tanh(g_ffn[1]) * _L1_ffn_ref(_layernorm(x, axis=-1), L1_ffn_w_router, L1_ffn_w_fc, L1_ffn_w_gate, L1_ffn_w_proj)
    return x

_drawn_inputs = setup_inputs


def setup_inputs(seed=0):
    import zlib

    import numpy as np

    out = dict(_drawn_inputs(seed))
    spreads = {'g_ffn': (-1.0, 0.6),
     'L0_xattn_b_q': (0.0, 0.291),
     'L0_xattn_b_k': (0.0, 0.8),
     'L0_xattn_b_v': (0.0, 0.1),
     'L0_xattn_b_o': (0.0, 0.1),
     'L1_xattn_in_proj_bias': (0.0, 0.1),
     'L1_xattn_out_proj_bias': (0.0, 0.1)}
    factors = {'L0_ffn_b1': 4.673,
     'L0_ffn_b2': 3.334,
     'L1_ffn_w_router': 8.0,
     'L1_ffn_w_fc': 8.0,
     'L1_ffn_w_gate': 8.0,
     'L1_ffn_w_proj': 8.0}
    for name, (base, spread) in spreads.items():
        noise = np.random.default_rng([zlib.crc32(name.encode()), seed]).standard_normal(out[name].shape)
        drawn = base * np.exp(spread * noise) if base else spread * noise
        out[name] = jnp.asarray(drawn.astype(out[name].dtype))
    for name, factor in factors.items():
        out[name] = (out[name] * factor).astype(out[name].dtype)
    return out
```

```python
from contextlib import ExitStack

import concourse.bass as bass
from concourse import mybir

F32 = mybir.dt.float32
BF16 = mybir.dt.bfloat16
I32 = mybir.dt.int32
U32 = mybir.dt.uint32
ALU = mybir.AluOpType
ACT = mybir.ActivationFunctionType
X = mybir.AxisListType.X

B, S, D = 64, 64, 128
H, DK = 16, 8
HP = H // 2
P = 128
NT = B * S // P
E0, HID0 = 8, 512
NC0 = HID0 // P
REGION = B * S + P
MAX_TILES = NT + E0 - 1
ROWS = E0 * REGION + (MAX_TILES - NT) * P
E1, HID1 = 16, 64
CAP = 2 * S // E1
SLOTS = E1 * CAP
EPS = 1e-5
SCALE = DK ** -0.5
MASKED = -1e9
ALL_MASKED = -2.0 ** 100


class Tile:

    def __init__(self, t, par, half):
        self.t, self.par, self.half = t, par, half


def number(t):
    return Tile(t, t % 2, t // 2)


def pipeline(eng, steps, count):
    most = max(skew for _, skew in steps)
    least = min(0, min(skew for _, skew in steps))
    first = most + 2 + most % 2
    last = count + least
    last -= (last - first) % 2

    def alone(n):
        for step, skew in steps:
            if 0 <= n - skew < count:
                step(number(n - skew))

    for n in range(least, first):
        alone(n)
    with eng.Fori(0, (last - first) // 2) as i:
        for u in range(2):
            for step, skew in steps:
                c = first + u - skew
                step(Tile(i * 2 + c, c % 2, i + c // 2))
    for n in range(last, count + most):
        alone(n)


def wait(eng, sem, value):
    if not (isinstance(value, int) and value <= 0):
        eng.wait_ge(sem, value)


def apart(eng):
    eng.nop(nofuse=True)


class Chain:

    def __init__(self, eng, sem, t, n):
        self.eng, self.sem, self.base, self.n, self.k = eng, sem, t * n, n, 0

    def __call__(self, ins, alone=False):
        self.k += 1
        assert self.k <= self.n
        ins.then_inc(self.sem, 1)
        self.eng.wait_ge(self.sem, self.base + self.k)
        if alone:
            apart(self.eng)


def attention(nc, layer, x_all, w, dram, hooks):
    with ExitStack() as ctx:
        def sb(name, shape, dt=F32):
            return ctx.enter_context(nc.sbuf_tensor(f"{name}_{layer}", shape, dt))

        def ps(name, shape, dt=F32):
            return ctx.enter_context(nc.psum_tensor(f"{name}_{layer}", shape, dt))

        def sem(name):
            return ctx.enter_context(nc.semaphore(f"{name}_{layer}"))

        masked = layer == 0
        ctx_in = sb("ctx_in", [P, 2, D])
        mask_in = sb("mask_in", [P, 2, S], I32)
        mask_zero = sb("mask_zero", [P, S])
        mask_all = sb("mask_all", [P, 2])
        mask_bias = sb("mask_bias", [P, 2, S], BF16)
        stats = sb("stats", [P, 6])
        mv = sb("mv", [P, 2, 2])
        rstd = sb("rstd", [P, 2])
        xn = sb("xn", [P, 2, D])
        xnT = sb("xnT", [P, 2, P])
        ctxT = sb("ctxT", [P, 2, 2, 2, S])
        qT = sb("qT", [P, 2, P])
        kT = sb("kT", [P, 2, P])
        k_blk = sb("k_blk", [P, 2, 2, H, S])
        v_blk = sb("v_blk", [P, 2, 2, HP, 32])
        prob = sb("prob", [P, 2, H, S])
        probT = sb("probT", [P, HP, P])
        rden = sb("rden", [P, 2, P])
        avT = sb("avT", [P, 2, P])
        x_bo = sb("x_bo", [P, 2, D])
        maxes = sb("maxes", [P, 2, H])

        S_ps = [ps("S_ps0", [P, HP, S]), ps("S_ps1", [P, HP, S])]
        T_ps = [ps("T_ps0", [P, 4, P]), ps("T_ps1", [P, 4, P])]
        A_ps = ps("A_ps", [P, 4, P])
        V_ps = ps("V_ps", [P, 2, HP, 2, DK])
        O_ps = ps("O_ps", [P, 2, 2, P])
        Y_ps = ps("Y_ps", [P, 512])

        loaded = [sem("loaded0"), sem("loaded1")]
        x_ready = sem("x_ready")
        mask_biased = sem("mask_biased")
        ln_stats = sem("ln_stats")
        ln_rstd = sem("ln_rstd")
        xn_ready = sem("xn_ready")
        xo_ready = sem("xo_ready")
        turned = sem("turned")
        turned_out = sem("turned_out")
        qk_ready = sem("qk_ready")
        qk_out = sem("qk_out")
        v_ready = sem("v_ready")
        v_out = sem("v_out")
        kblk_ready = sem("kblk_ready")
        scored = sem("scored")
        shifted = sem("shifted")
        exp_ready = sem("exp_ready")
        probs_turned = sem("probs_turned")
        probT_ready = sem("probT_ready")
        av_ready = sem("av_ready")
        av_out = sem("av_out")
        y_ready = sem("y_ready")
        y_out = sem("y_out")
        a_chain = sem("a_chain")
        m_chain = sem("m_chain")
        b_chain = sem("b_chain")
        c_chain = sem("c_chain")
        zeroed = sem("zeroed")

        block = ctx.enter_context(nc.Block())
        env = dict(ctx=ctx, sb=sb, ps=ps, sem=sem, x_all=x_all, Y_ps=Y_ps, y_ready=y_ready, y_out=y_out, x_ready=x_ready)
        hook = hooks(env)
        LOADS = 48 if masked else 16

        @block.sync
        def _(sp):
            def load(T):
                wait(sp, turned, T.t - 1)
                sp.dma_start(ctx_in[:, T.par, :], dram["ctx"][bass.ds(T.t * P, P), :]).then_inc(loaded[T.par], 16)
                if masked:
                    wait(sp, mask_biased, T.t - 1)
                    sp.dma_start(x_all[:, bass.ds(T.t * D, D)], dram["x"][bass.ds(T.t * P, P), :]).then_inc(loaded[T.par], 16)
                    sp.dma_start(mask_in[:, T.par, :], dram["mask"][bass.ds(T.t * P, P), :]).then_inc(loaded[T.par], 16)

            pipeline(sp, [(load, 0)] + hook["sync"], NT)
            pass

        @block.gpsimd
        def _(pool):
            nc.gpsimd.memset(v_blk[:, :, :, :, :], 0.0).then_inc(zeroed, 1)

            def std(T):
                pool.wait_ge(ln_stats, T.t + 1)
                nc.gpsimd.tensor_tensor(rstd[:, T.par:T.par + 1], mv[:, T.par, 1:2], w["minus_half"][:, 0:1],
                                        ALU.pow).then_inc(ln_rstd, 1)

            def residual(T):
                pool.wait_ge(xn_ready, T.t + 1)
                wait(pool, y_out, T.t - 1)
                nc.gpsimd.tensor_tensor(x_bo[:, T.par, :], x_all[:, bass.ds(T.t * D, D)], w["bo"][:, :],
                                        ALU.add).then_inc(xo_ready, 1)

            def blocks(T):
                pool.wait_ge(qk_out, 2 * T.t + 2)
                wait(pool, scored, 2 * T.t - 2)
                for b in range(2):
                    last = nc.gpsimd.tensor_tensor(
                        k_blk[:, T.par, b, :, :],
                        kT[:, T.par, b * S:(b + 1) * S].unsqueeze(1).to_broadcast([P, H, S]),
                        w["head_rows"][:, :].unsqueeze(2).to_broadcast([P, H, S]), ALU.mult)
                last.then_inc(kblk_ready, 1)

            pipeline(pool, hook["pool_first"] + [(std, 0), (blocks, 0), (residual, 1)] + hook["pool"], NT)
            hook["pool_end"](pool)

        @block.scalar
        def _(act):
            def turn_out(T):
                act.wait_ge(turned, T.t + 1)
                wait(act, qk_ready, T.t - 1)
                wait(act, v_ready, T.t - 1)
                nc.scalar.copy(ctxT[:, T.par, :, :, :], A_ps[:, 1, :].rearrange("p (b k) -> p b k", b=2)
                               .unsqueeze(2).to_broadcast([P, 2, 2, S])).then_inc(turned_out, 1)
                nc.scalar.copy(xnT[:, T.par, :], A_ps[:, 0, :]).then_inc(turned_out, 1)

            def qk(T):
                act.wait_ge(qk_ready, T.t + 1)
                wait(act, scored, 2 * T.t - 2)
                nc.scalar.activation(qT[:, T.par, :], A_ps[:, 2, :], ACT.Identity, bias=w["bq"][:, 0:1]).then_inc(qk_out, 1)
                nc.scalar.activation(kT[:, T.par, :], A_ps[:, 3, :], ACT.Identity, bias=w["bk"][:, 0:1]).then_inc(qk_out, 1)

            def exps(T):
                for g in range(2):
                    act.wait_ge(shifted, 2 * T.t + g + 1)
                    part = prob[:, T.par, g * HP:(g + 1) * HP, :]
                    nc.scalar.activation(part, part, ACT.Exp, scale=SCALE).then_inc(exp_ready, 1)

            def probs_out(T):
                for g in range(2):
                    act.wait_ge(probs_turned, 2 * T.t + g + 1)
                    wait(act, av_ready, T.t)
                    nc.scalar.copy(probT[:, 4 * g:4 * g + 4, :], T_ps[g][:, :, :]).then_inc(probT_ready, 1)

            pipeline(act, hook["act0"] + [(turn_out, 0)] + hook["act1"] + [(qk, 0), (probs_out, 2)] + hook["act"] + [(exps, 1)], NT)

        @block.vector
        def _(dve):
            def stat(T):
                if masked:
                    dve.wait_ge(loaded[T.par], (T.half + 1) * LOADS)
                else:
                    hook["before_norm"](dve, T)
                step = Chain(dve, a_chain, T.t, 2)
                step(nc.vector.bn_stats(stats[:, :], x_all[:, bass.ds(T.t * D, D)]), alone=True)
                step(nc.vector.bn_aggr(mv[:, T.par, :], stats[:, :]))
                nc.vector.tensor_scalar(mv[:, T.par, 1:2], mv[:, T.par, 1:2], EPS, None, ALU.add).then_inc(ln_stats, 1)

            def norm(T):
                dve.wait_ge(ln_rstd, T.t + 1)
                wait(dve, turned, T.t - 1)
                nc.vector.tensor_scalar(xn[:, T.par, :], x_all[:, bass.ds(T.t * D, D)], mv[:, T.par, 0:1],
                                        rstd[:, T.par:T.par + 1], ALU.subtract, ALU.mult).then_inc(xn_ready, 1)

            def mask(T):
                step = Chain(dve, m_chain, T.t, 3)
                step(nc.vector.tensor_scalar(mask_zero[:, :], mask_in[:, T.par, :], 0.0, None, ALU.is_equal))
                step(nc.vector.tensor_reduce(mask_all[:, 0:1], mask_zero[:, :], X, ALU.min))
                step(nc.vector.tensor_scalar(mask_all[:, 1:2], mask_all[:, 0:1], ALL_MASKED, MASKED, ALU.mult, ALU.add))
                wait(dve, scored, 2 * T.t - 2)
                nc.vector.tensor_scalar(mask_bias[:, T.par, :], mask_zero[:, :], mask_all[:, 1:2], None,
                                        ALU.mult).then_inc(mask_biased, 1)

            def values(T):
                dve.wait_ge(v_ready, T.t + 1)
                if isinstance(T.t, int) and T.t == 0:
                    dve.wait_ge(zeroed, 1)
                wait(dve, av_ready, T.t - 1)
                for r in range(2):
                    half = slice(r * S, (r + 1) * S)
                    last = nc.vector.tensor_tensor(
                        v_blk[half, T.par, :, :, r * DK:(r + 1) * DK], V_ps[half, :, :, r, :],
                        w["bv"][half, :].rearrange("p (a r d) -> p a r d", a=HP, r=2)[:, :, r, :]
                        .unsqueeze(1).to_broadcast([S, 2, HP, DK]), ALU.add)
                last.then_inc(v_out, 1)

            def softmax(T):
                step = Chain(dve, b_chain, T.t, 2)
                for g in range(2):
                    heads = slice(g * HP, (g + 1) * HP)
                    dve.wait_ge(scored, 2 * T.t + g + 1)
                    step(nc.vector.tensor_reduce(maxes[:, T.par, heads], S_ps[g][:, :, :], X, ALU.max))
                    wait(dve, probs_turned, 2 * T.t - 2)
                    nc.vector.tensor_tensor(
                        prob[:, T.par, heads, :], S_ps[g][:, :, :],
                        maxes[:, T.par, heads].unsqueeze(2).to_broadcast([P, HP, S]), ALU.subtract).then_inc(shifted, 1)

            def divide(T):
                step = Chain(dve, c_chain, T.t, 1)
                dve.wait_ge(av_ready, T.t + 1)
                step(nc.vector.reciprocal(rden[:, :, :], O_ps[:, 1, :, :]))
                wait(dve, y_ready, T.t)
                nc.vector.tensor_tensor(avT[:, :, :], O_ps[:, 0, :, :], rden[:, :, :], ALU.mult).then_inc(av_out, 1)

            def add(T):
                dve.wait_ge(y_ready, T.t + 1)
                dve.wait_ge(xo_ready, T.t + 1)
                nc.vector.tensor_tensor(x_all[:, bass.ds(T.t * D, D)], Y_ps[:, 0:D], x_bo[:, T.par, :],
                                        ALU.add).then_inc(y_out, 1)

            pipeline(dve, hook["dve_first"] + [(stat, 0), (norm, 0)] + ([(mask, 0)] if masked else []) + hook["dve0"] + [(softmax, 1), (values, 0)]
                     + hook["dve1"] + [(divide, 2), (add, 2)] + hook["dve2"], NT)

        @block.tensor
        def _(pe):
            ident = w["ident"]

            def turn(T):
                pe.wait_ge(xn_ready, T.t + 1)
                wait(pe, qk_out, 2 * T.t)
                pe.wait_ge(loaded[T.par], (T.half + 1) * LOADS)
                nc.tensor.transpose(A_ps[:, 1, :], ctx_in[:, T.par, :], ident[:, :])
                nc.tensor.transpose(A_ps[:, 0, :], xn[:, T.par, :], ident[:, :]).then_inc(turned, 1)

            def project(T):
                pe.wait_ge(turned_out, 2 * T.t + 2)
                nc.tensor.matmul(A_ps[:, 2, :], w["wq"][:, :], xnT[:, T.par, :], start=True, stop=True)
                nc.tensor.matmul(A_ps[:, 3, :], w["wk"][:, :], ctxT[:, T.par, :, 0, :], start=True, stop=True).then_inc(qk_ready, 1)

            def project_v(T):
                wait(pe, v_out, T.t)
                for b in range(2):
                    last = nc.tensor.matmul(V_ps[:, b, :, :, :].rearrange("p a r d -> p (a r d)"),
                                            ctxT[:, T.par, b, :, :].rearrange("p r k -> p (r k)"),
                                            w["wv"][:, :], start=True, stop=True)
                last.then_inc(v_ready, 1)

            def score(T):
                pe.wait_ge(kblk_ready, T.t + 1)
                if masked:
                    pe.wait_ge(mask_biased, T.t + 1)
                for g in range(2):
                    wait(pe, shifted, 2 * T.t + g - 1)
                    if masked:
                        nc.tensor.matmul(S_ps[g][:, :, :], w["ident_bf"][:, :],
                                         mask_bias[:, T.par, :].unsqueeze(1).to_broadcast([P, HP, S]),
                                         start=True, stop=False, skip_group_check=True)
                    for b in range(2):
                        last = nc.tensor.matmul(S_ps[g][b * S:(b + 1) * S, :, :], qT[:, T.par, b * S:(b + 1) * S],
                                                k_blk[:, T.par, b, g * HP:(g + 1) * HP, :],
                                                start=not masked, stop=True, skip_group_check=True)
                    last.then_inc(scored, 1)

            def turn_probs(T):
                for g in range(2):
                    pe.wait_ge(exp_ready, 2 * T.t + g + 1)
                    wait(pe, probT_ready, 2 * T.t + g - 1)
                    for j in range(4):
                        pair = prob[:, T.par, 8 * g + 2 * j:8 * g + 2 * j + 2, :].rearrange("p r k -> p (r k)")
                        last = nc.tensor.transpose(T_ps[g][:, j, :], pair, ident[:, :])
                    last.then_inc(probs_turned, 1)

            def attend(T):
                pe.wait_ge(v_out, T.t + 1)
                wait(pe, av_out, T.t)
                for g in range(2):
                    pe.wait_ge(probT_ready, 2 * T.t + g + 1)
                    for b in range(2):
                        for j in range(4):
                            nc.tensor.matmul(O_ps[32 * j:32 * j + 32, 0, g, b * S:(b + 1) * S],
                                             v_blk[:, T.par, b, 4 * g + j, :], probT[:, 4 * g + j, b * S:(b + 1) * S],
                                             start=True, stop=True, skip_group_check=True)
                    for j in range(4):
                        last = nc.tensor.matmul(O_ps[32 * j:32 * j + 32, 1, g, :], w["ones_blk"][:, :],
                                                probT[:, 4 * g + j, :], start=True, stop=True, skip_group_check=True)
                last.then_inc(av_ready, 1)

            def output(T):
                pe.wait_ge(av_out, T.t + 1)
                wait(pe, y_out, T.t)
                wait(pe, hook["y_bank_free"], T.t)
                for g in range(2):
                    last = nc.tensor.matmul(Y_ps[:, 0:D], avT[:, g, :], w["wo"][:, g, :],
                                            start=g == 0, stop=g == 1)
                last.then_inc(y_ready, 1)

            pipeline(pe, hook["pe0"] + [(turn, 0)] + hook["pe1"] + [(score, 1)] + hook["pe2"]
                     + [(project, 0), (project_v, 0), (turn_probs, 2), (attend, 2)] + hook["pe3"] + [(output, 2)], NT)


def router(nc, env, layer, r):
    sb, sem = env["sb"], env["sem"]
    x_all, Y_ps, y_out = env["x_all"], env["Y_ps"], env["y_out"]
    E = E0 if layer == 0 else E1
    stats = sb("r_stats", [P, 6])
    mv = sb("r_mv", [P, 2, 2])
    rstd = sb("r_rstd", [P, 2])
    xn = sb("r_xn", [P, 2, D])
    xnT = sb("r_xnT", [P, P])
    logits = sb("r_logits", [P, E])
    top = sb("r_top", [P, 8])
    top_at = sb("r_top_at", [P, 8], U32)
    expert = sb("r_expert", [P, 2])
    chosen = sb("r_chosen", [P, 2, E], BF16)
    product = sb("r_product", [P, E])
    place = sb("r_place", [P, E])
    rank = sb("r_rank", [P, 2])
    LOG = Y_ps[:, 0:E]
    RANK = Y_ps[:, 32:32 + (2 * E if layer else E)]
    COUNT = Y_ps[:, 64:64 + E]
    XT = Y_ps[:, 128:256]

    r_stats = sem("r_stats_ready")
    r_rstd = sem("r_rstd_ready")
    r_xn = sem("r_xn_ready")
    r_turned = sem("r_turned")
    r_xnT = sem("r_xnT_ready")
    r_logits = sem("r_logits_ready")
    r_chosen = sem("r_chosen_ready")
    r_ranked = sem("r_ranked")
    r_done = sem("r_done")
    s_chain = sem("r_s_chain")
    t_chain = sem("r_t_chain")
    p_chain = sem("r_p_chain")
    h = {k: [] for k in ("sync", "pool_first", "pool", "act0", "act1", "act", "dve_first", "dve0", "dve1", "dve2",
                         "pe0", "pe1", "pe2", "pe3")}
    h["y_bank_free"] = r_done
    vec, pool, act, pe = nc.vector, nc.gpsimd, nc.scalar, nc.tensor

    def stat(T):
        step = Chain(vec, s_chain, T.t, 2)
        vec.wait_ge(y_out, T.t + 1)
        apart(vec)
        step(vec.bn_stats(stats[:, :], x_all[:, bass.ds(T.t * D, D)]), alone=True)
        step(vec.bn_aggr(mv[:, T.par, :], stats[:, :]))
        vec.tensor_scalar(mv[:, T.par, 1:2], mv[:, T.par, 1:2], EPS, None, ALU.add).then_inc(r_stats, 1)

    def std(T):
        pool.wait_ge(r_stats, T.t + 1)
        pool.tensor_tensor(rstd[:, T.par:T.par + 1], mv[:, T.par, 1:2], r["minus_half"][:, 0:1], ALU.pow).then_inc(r_rstd, 1)

    def norm(T):
        vec.wait_ge(r_rstd, T.t + 1)
        if layer == 0:
            wait(vec, scattered[T.par], T.half * 16)
        vec.tensor_scalar(xn[:, T.par, :], x_all[:, bass.ds(T.t * D, D)], mv[:, T.par, 0:1], rstd[:, T.par:T.par + 1],
                          ALU.subtract, ALU.mult).then_inc(r_xn, 1)

    def turn(T):
        pe.wait_ge(r_xn, T.t + 1)
        pe.transpose(XT, xn[:, T.par, :], r["ident"][:, :]).then_inc(r_turned, 1)

    def turn_out(T):
        act.wait_ge(r_turned, T.t + 1)
        act.copy(xnT[:, :], XT).then_inc(r_xnT, 1)

    def logit(T):
        pe.wait_ge(r_xnT, T.t + 1)
        pe.matmul(LOG, xnT[:, :], r["router"][:, :], start=True, stop=True).then_inc(r_logits, 1)

    def choose(T):
        step = Chain(vec, t_chain, T.t, 4)
        vec.wait_ge(r_logits, T.t + 1)
        step(vec.tensor_copy(logits[:, :], LOG), alone=True)
        step(vec.max(top[:, :], logits[:, :]), alone=True)
        if layer:
            wait(vec, e_done, T.t)
            vec.tensor_scalar(shift[:, :], top[:, 0:1], -1.0, None, ALU.mult).then_inc(shift_ready, 1)
        step(vec.max_index(top_at[:, :], top[:, :], logits[:, :]))
        step(vec.tensor_copy(expert[:, :], top_at[:, 0:2]))
        for k in range(layer + 1):
            last = vec.tensor_scalar(chosen[:, k, :], r["iota"][:, 0:E], expert[:, k:k + 1], None, ALU.is_equal)
        last.then_inc(r_chosen, 1)

    def ranks(T):
        pe.wait_ge(r_chosen, T.t + 1)
        if layer == 0:
            pe.matmul(RANK, r["before"][:, :], chosen[:, 0, :], start=True, stop=True)
            pe.matmul(COUNT, r["ones"][:, :], chosen[:, 0, :], start=True, stop=True).then_inc(r_ranked, 1)
        else:
            pe.matmul(RANK, r["before"][:, :], chosen[:, :, :], start=True, stop=False, skip_group_check=True)
            pe.matmul(RANK[:, E:2 * E], r["ones"][:, :], chosen[:, 0, :], start=False, stop=True,
                      skip_group_check=True).then_inc(r_ranked, 1)

    h["dve_first"] = [(norm, 3)]
    h["dve0"] = [(choose, 3)]
    h["dve2"] = [(stat, 2)]
    h["act0"] = [(turn_out, 3)]
    h["pe0"] = [(turn, 3)]
    h["pe1"] = [(logit, 3)]
    h["pe2"] = [(ranks, 3)]

    if layer == 0:
        row = sb("r_row", [P, 2], I32)
        scattered = [sem("r_scattered0"), sem("r_scattered1")]
        row_ready = sem("r_row_ready")

        def rows(T):
            step = Chain(vec, p_chain, T.t, 2)
            vec.wait_ge(r_ranked, T.t + 1)
            step(vec.tensor_tensor(place[:, :], RANK, r["start"][:, :], ALU.add))
            step(vec.tensor_tensor_reduce(product[:, :], place[:, :], chosen[:, 0, :], 1.0, 0.0, ALU.mult, ALU.add,
                                          rank[:, 0:1]))
            vec.tensor_tensor(r["start"][:, :], r["start"][:, :], COUNT, ALU.add).then_inc(r_done, 1)
            wait(vec, scattered[T.par], T.half * 16)
            vec.tensor_copy(row[:, T.par:T.par + 1], rank[:, 0:1]).then_inc(row_ready, 1)
            vec.tensor_copy(r["row_all"][:, bass.ds(T.t, 1)], rank[:, 0:1]).then_inc(row_ready, 1)

        def scatter(T):
            pool.wait_ge(row_ready, 2 * T.t + 1)
            apart(pool)
            pool.indirect_dma_start(r["sorted"], bass.IndirectOffsetOnAxis(ap=row[:, T.par:T.par + 1], axis=0),
                                    xn[:, T.par, :], None).then_inc(scattered[T.par], 16)

        def end(eng):
            for s in scattered:
                eng.wait_ge(s, 16 * NT // 2)

        h["dve1"] = [(rows, 3)]
        h["pool"] = [(std, 2), (scatter, 3)]
        h["pool_end"] = end
        return h

    shift = sb("r_shift", [P, 1])
    e_all = sb("r_e_all", [P, E])
    e_top = sb("r_e_top", [P, 2])
    e_sum = sb("r_e_sum", [P, 1])
    r_sum = sb("r_r_sum", [P, 1])
    prob = sb("r_prob", [P, 2])
    base = sb("r_base", [P, 2])
    slot = sb("r_slot", [P, 2])
    sent = sb("r_sent", [P, 2])
    over = sb("r_over", [P, 2])
    part = sb("r_part", [P, 4, 2 * SLOTS])
    dispatch = sb("r_dispatch", [P, 2 * SLOTS])
    combine = sb("r_combine", [P, 2 * SLOTS])
    shift_ready = sem("r_shift_ready")
    e_done = sem("r_e_done")
    matrices = sem("r_matrices")
    to_slots = sem("r_to_slots")

    def exps(T):
        act.wait_ge(shift_ready, T.t + 1)
        wait(act, matrices, T.t)
        act.activation(e_all[:, :], logits[:, :], ACT.Exp, bias=shift[:, 0:1], accum_out=e_sum[:, 0:1])
        act.activation(e_top[:, :], top[:, 0:2], ACT.Exp, bias=shift[:, 0:1]).then_inc(e_done, 1)

    def place_all(T):
        step = Chain(vec, p_chain, T.t, 10)
        vec.wait_ge(e_done, T.t + 1)
        step(vec.reciprocal(r_sum[:, :], e_sum[:, :]))
        step(vec.tensor_scalar(prob[:, :], e_top[:, :], r_sum[:, 0:1], None, ALU.mult))
        vec.wait_ge(r_ranked, T.t + 1)
        for k in range(2):
            step(vec.tensor_tensor_reduce(product[:, :], RANK[:, k * E:(k + 1) * E], chosen[:, k, :], 1.0, 0.0,
                                          ALU.mult, ALU.add, rank[:, k:k + 1]))
        step(vec.tensor_scalar(base[:, :], expert[:, :], float(CAP), r["batch_slot"][:, 0:1], ALU.mult, ALU.add))
        step(vec.scalar_tensor_tensor(slot[:, :], rank[:, :], float(CAP - 1), base[:, :], ALU.min, ALU.add))
        step(vec.tensor_scalar(over[:, :], rank[:, :], float(CAP), 4.0 * SLOTS, ALU.is_ge, ALU.mult))
        step(vec.tensor_tensor(sent[:, :], over[:, :], slot[:, :], ALU.add))
        wait(vec, to_slots, T.t)
        step(vec.tensor_scalar(part[:, 0, :], r["iota"][:, :], sent[:, 0:1], None, ALU.is_equal))
        vec.scalar_tensor_tensor(dispatch[:, :], r["iota"][:, :], sent[:, 1:2], part[:, 0, :], ALU.is_equal, ALU.add)
        vec.tensor_scalar(part[:, 1, :], r["iota"][:, :], slot[:, 0:1], prob[:, 0:1], ALU.is_equal, ALU.mult)
        step(vec.tensor_scalar(part[:, 2, :], r["iota"][:, :], slot[:, 1:2], prob[:, 1:2], ALU.is_equal, ALU.mult))
        vec.tensor_tensor(combine[:, :], part[:, 1, :], part[:, 2, :], ALU.add).then_inc(matrices, 1)

    def slots(T):
        pe.wait_ge(matrices, T.t + 1)
        pe.matmul(Y_ps[:, 256:512], xn[:, T.par, :], dispatch[:, :], start=True, stop=True)
        for b in range(2):
            last = pe.transpose(Y_ps[:, b * P:(b + 1) * P], combine[:, b * SLOTS:(b + 1) * SLOTS], r["ident"][:, :])
        last.then_inc(to_slots, 1)

    def slots_out(T):
        act.wait_ge(to_slots, T.t + 1)
        act.copy(r["slotsT"][:, :, bass.ds(T.t * 2, 2), :].rearrange("p e b s -> p b e s"),
                 Y_ps[:, 256:512].rearrange("p (b e s) -> p b e s", b=2, e=E1))
        act.copy(r["combineT"][:, bass.ds(T.t * 2 * P, 2 * P)], Y_ps[:, 0:256]).then_inc(r_done, 1)

    h["act1"] = [(exps, 3)]
    h["act"] = [(slots_out, 3)]
    h["dve1"] = [(place_all, 3)]
    h["pe3"] = [(slots, 3)]
    h["pool"] = [(std, 2)]
    h["pool_end"] = lambda eng: None
    return h


def experts0(nc, r, f):
    with ExitStack() as ctx:
        def sb(name, shape, dt=F32):
            return ctx.enter_context(nc.sbuf_tensor("f0_" + name, shape, dt))

        def ps(name, shape, dt=F32):
            return ctx.enter_context(nc.psum_tensor("f0_" + name, shape, dt))

        def sem(name):
            return ctx.enter_context(nc.semaphore("f0_" + name))

        w1 = sb("w1", [P, E0, HID0])
        w2 = sb("w2", [P, E0, NC0, D])
        b1 = sb("b1", [P, E0, NC0])
        b2 = sb("b2", [P, E0, D])
        zeros = sb("zeros", [P, D])
        counts = sb("counts", [P, E0])
        filled = sb("filled", [P, E0], I32)
        over = sb("over", [P, E0, NT])
        tiles = sb("tiles", [P, E0])
        ends = sb("ends", [P, E0])
        ends_of = sb("ends_of", [P, E0, E0])
        passed = sb("passed", [P, MAX_TILES, E0])
        behind = sb("behind", [P, MAX_TILES, E0])
        n_passed = sb("n_passed", [P, MAX_TILES])
        n_behind = sb("n_behind", [P, MAX_TILES])
        first = sb("first", [P, MAX_TILES])
        row_tab = sb("row_tab", [P, MAX_TILES], I32)
        expert_tab = sb("expert_tab", [P, MAX_TILES], I32)
        closer = sb("closer", [P, E0])
        beyond = sb("beyond", [P, NT, E0 - 1])
        moved = sb("moved", [P, NT])
        weights_in = sem("weights_in")
        table = sem("table")
        chain = sem("chain")
        zeroed = sem("zeroed")
        rows_zeroed = sem("rows_zeroed")
        rows = sb("rows", [P, 2, D])
        rowsT = sb("rowsT", [P, 2, P])
        w1_now = sb("w1_now", [P, 2, HID0])
        hid = sb("hid", [P, 2, NC0, P])
        done = sb("done", [P, 2, D])
        T_ps = [ps(f"T_ps{n}", [P, 512]) for n in range(2)]
        H_ps = [ps(f"H_ps{n}", [P, NC0, P]) for n in range(2)]
        Y_ps = [ps(f"Y_ps{n}", [P, 512]) for n in range(2)]
        rows_in = [sem("rows_in0"), sem("rows_in1")]
        turned = sem("turned")
        turned_out = sem("turned_out")
        w1_ready = sem("w1_ready")
        hidden = sem("hidden")
        biased = sem("biased")
        gelu_done = sem("gelu_done")
        y_ready = sem("y_ready")
        y_out = sem("y_out")
        stored = [sem("stored0"), sem("stored1")]
        vec, pool, act, pe, sp = nc.vector, nc.gpsimd, nc.scalar, nc.tensor, nc.sync
        block = ctx.enter_context(nc.Block())

        @block.vector
        def _(dve):
            step = Chain(dve, chain, 0, 20)
            vec.memset(zeros[:, :], 0.0).then_inc(zeroed, 1)
            step(vec.tensor_copy(filled[:, :], r["start"][:, :]))
            step(vec.tensor_tensor(counts[:, :], r["start"][:, :], r["region"][:, :], ALU.subtract))
            step(vec.tensor_tensor(over[:, :, :], counts[:, :].unsqueeze(2).to_broadcast([P, E0, NT]),
                                   r["edges"][:, :].unsqueeze(1).to_broadcast([P, E0, NT]), ALU.is_gt))
            step(vec.tensor_reduce(tiles[:, :], over[:, :, :], X, ALU.add))
            step(vec.tensor_tensor(ends_of[:, :, :], tiles[:, :].unsqueeze(1).to_broadcast([P, E0, E0]),
                                   r["upto"][:, :].rearrange("p (a b) -> p a b", a=E0), ALU.mult))
            step(vec.tensor_reduce(ends[:, :], ends_of[:, :, :], X, ALU.add))
            step(vec.tensor_tensor(passed[:, :, :], r["tile_no"][:, :].unsqueeze(2).to_broadcast([P, MAX_TILES, E0]),
                                   ends[:, :].unsqueeze(1).to_broadcast([P, MAX_TILES, E0]), ALU.is_ge))
            step(vec.tensor_tensor(behind[:, :, :], passed[:, :, :],
                                   tiles[:, :].unsqueeze(1).to_broadcast([P, MAX_TILES, E0]), ALU.mult))
            step(vec.tensor_reduce(n_passed[:, :], passed[:, :, :], X, ALU.add))
            step(vec.tensor_reduce(n_behind[:, :], behind[:, :, :], X, ALU.add))
            step(vec.tensor_tensor(first[:, :], r["tile_no"][:, :], n_behind[:, :], ALU.subtract))
            step(vec.tensor_scalar(first[:, :], first[:, :], float(P), None, ALU.mult))
            step(vec.scalar_tensor_tensor(first[:, :], n_passed[:, :], float(REGION), first[:, :], ALU.mult, ALU.add))
            step(vec.tensor_copy(row_tab[:, :], first[:, :]))
            step(vec.tensor_scalar(expert_tab[:, :], n_passed[:, :], float(E0 - 1), None, ALU.min))
            step(vec.tensor_scalar(closer[:, :], tiles[:, :], float(P), -float(REGION), ALU.mult, ALU.add))
            step(vec.tensor_tensor(beyond[:, :, :], r["row_all"][:, :].unsqueeze(2).to_broadcast([P, NT, E0 - 1]),
                                   r["region"][:, 1:E0].unsqueeze(1).to_broadcast([P, NT, E0 - 1]), ALU.is_ge))
            step(vec.tensor_tensor(beyond[:, :, :], beyond[:, :, :],
                                   closer[:, 0:E0 - 1].unsqueeze(1).to_broadcast([P, NT, E0 - 1]), ALU.mult))
            step(vec.tensor_reduce(moved[:, :], beyond[:, :, :], X, ALU.add))
            vec.tensor_tensor(r["row_all"][:, :], r["row_all"][:, :], moved[:, :], ALU.add).then_inc(table, 1)


            def bias(T):
                e = dve.value_load(expert_tab[0:1, bass.ds(T.t, 1)], min_val=0, max_val=E0 - 1)
                dve.wait_ge(hidden, T.t + 1)
                wait(dve, y_ready, T.t - 1)
                vec.tensor_tensor(hid[:, T.par, :, :], H_ps[T.par][:, :, :],
                                  b1[:, bass.ds(e, 1), :].rearrange("p a c -> p (a c)").unsqueeze(2).to_broadcast([P, NC0, P]),
                                  ALU.add).then_inc(biased, 1)

            def finish(T):
                e = dve.value_load(expert_tab[0:1, bass.ds(T.t, 1)], min_val=0, max_val=E0 - 1)
                dve.wait_ge(y_ready, T.t + 1)
                wait(dve, stored[T.par], T.half * 16)
                vec.tensor_tensor(done[:, T.par, :], Y_ps[T.par][:, 0:D],
                                  b2[:, bass.ds(e, 1), :].rearrange("p a c -> p (a c)"), ALU.add).then_inc(y_out, 1)

            dve.wait_ge(weights_in, 16 * 4)
            pipeline(dve, [(bias, 0), (finish, 1)], MAX_TILES)

        @block.sync
        def _(sp):
            for to, what in ((w1, f["W1"].rearrange("e d h -> d e h")), (b1, f["b1"]), (b2, f["b2"].partition_broadcast(P)),
                             (w2, f["W2"].rearrange("e (c p) d -> p e c d", p=P))):
                sp.dma_start(to[:], what).then_inc(weights_in, 16)
            sp.wait_ge(zeroed, 1)
            sp.wait_ge(table, 1)
            for e in range(E0):
                row = sp.value_load(filled[0:1, e:e + 1], min_val=0, max_val=ROWS - P)
                sp.dma_start(r["sorted"][bass.ds(row, P), :], zeros[:, :]).then_inc(rows_zeroed, 16)
            for n in range(MAX_TILES - NT):
                sp.dma_start(r["sorted"][E0 * REGION + n * P:E0 * REGION + (n + 1) * P, :], zeros[:, :]).then_inc(rows_zeroed, 16)
            sp.wait_ge(rows_zeroed, 16 * (E0 + MAX_TILES - NT))

            def load(T):
                row = sp.value_load(row_tab[0:1, bass.ds(T.t, 1)], min_val=0, max_val=ROWS - P)
                wait(sp, turned, T.t - 1)
                sp.dma_start(rows[:, T.par, :], r["sorted"][bass.ds(row, P), :]).then_inc(rows_in[T.par], 16)

            def store(T):
                sp.wait_ge(y_out, T.t + 1)
                sp.dma_start(r["expert_out"][bass.ds(T.t * P, P), :], done[:, T.par, :]).then_inc(stored[T.par], 16)

            pipeline(sp, [(load, 0), (store, 2)], MAX_TILES)
            sp.wait_ge(stored[0], 16 * ((MAX_TILES + 1) // 2))
            sp.wait_ge(stored[1], 16 * (MAX_TILES // 2))

        @block.gpsimd
        def _(pool):
            def weights(T):
                e = pool.value_load(expert_tab[0:1, bass.ds(T.t, 1)], min_val=0, max_val=E0 - 1)
                wait(pool, hidden, T.t - 1)
                pool.tensor_copy(w1_now[:, T.par, :], w1[:, bass.ds(e, 1), :].rearrange("p a c -> p (a c)")).then_inc(w1_ready, 1)

            pool.wait_ge(table, 1)
            pool.wait_ge(weights_in, 16 * 4)
            pipeline(pool, [(weights, 0)], MAX_TILES)

        @block.scalar
        def _(act):
            def turn_out(T):
                act.wait_ge(turned, T.t + 1)
                wait(act, hidden, T.t - 1)
                nc.scalar.copy(rowsT[:, T.par, :], T_ps[T.par][:, 0:P]).then_inc(turned_out, 1)

            def gelu(T):
                act.wait_ge(biased, T.t + 1)
                nc.scalar.activation(hid[:, T.par, :, :], hid[:, T.par, :, :], ACT.Gelu).then_inc(gelu_done, 1)

            pipeline(act, [(turn_out, 0), (gelu, 1)], MAX_TILES)

        @block.tensor
        def _(pe):
            def turn(T):
                pe.wait_ge(rows_in[T.par], (T.half + 1) * 16)
                wait(pe, turned_out, T.t - 1)
                nc.tensor.transpose(T_ps[T.par][:, 0:P], rows[:, T.par, :], r["ident"][:, :]).then_inc(turned, 1)

            def up(T):
                pe.wait_ge(turned_out, T.t + 1)
                pe.wait_ge(w1_ready, T.t + 1)
                wait(pe, biased, T.t - 1)
                for n in range(NC0):
                    last = nc.tensor.matmul(H_ps[T.par][:, n, :], w1_now[:, T.par, n * P:(n + 1) * P], rowsT[:, T.par, :],
                                            start=True, stop=True)
                last.then_inc(hidden, 1)

            def down(T):
                e = pe.value_load(expert_tab[0:1, bass.ds(T.t, 1)], min_val=0, max_val=E0 - 1)
                pe.wait_ge(gelu_done, T.t + 1)
                wait(pe, y_out, T.t - 1)
                for n in range(NC0):
                    last = nc.tensor.matmul(Y_ps[T.par][:, 0:D], hid[:, T.par, n, :],
                                            w2[:, bass.ds(e, 1), n, :].rearrange("p a c -> p (a c)"),
                                            start=n == 0, stop=n == NC0 - 1)
                last.then_inc(y_ready, 1)

            pe.wait_ge(table, 1)
            pe.wait_ge(weights_in, 16 * 4)
            pipeline(pe, [(turn, 0), (up, 0), (down, 1)], MAX_TILES)


def experts1(nc, r, f, outT):
    N = B * CAP
    with ExitStack() as ctx:
        def sb(name, shape, dt=F32):
            return ctx.enter_context(nc.sbuf_tensor("f1_" + name, shape, dt))

        def sem(name):
            return ctx.enter_context(nc.semaphore("f1_" + name))

        gate = sb("gate", [P, E1, HID1])
        fc = sb("fc", [P, E1, HID1])
        proj = sb("proj", [P, E1, D])
        silu = sb("silu", [P, 2, N])
        hid = sb("hid", [P, 2, N])
        G_ps = [ctx.enter_context(nc.psum_tensor(f"f1_G_ps{n}", [P, N], F32)) for n in range(2)]
        F_ps = [ctx.enter_context(nc.psum_tensor(f"f1_F_ps{n}", [P, N], F32)) for n in range(2)]
        O_ps = [ctx.enter_context(nc.psum_tensor(f"f1_O_ps{n}", [P, N], F32)) for n in range(2)]
        weights_in = sem("weights_in")
        zeroed = sem("zeroed")
        up = sem("up")
        silu_done = sem("silu_done")
        hid_ready = sem("hid_ready")
        down = sem("down")
        out_done = sem("out_done")
        block = ctx.enter_context(nc.Block())
        PAIRS = E1 // 2

        @block.sync
        def _(sp):
            sp.dma_start(gate[:, :, :], f["w_gate"].rearrange("e d h -> d e h")).then_inc(weights_in, 16)
            sp.dma_start(fc[:, :, :], f["w_fc"].rearrange("e d h -> d e h")).then_inc(weights_in, 16)
            sp.wait_ge(zeroed, 1)
            for half in range(2):
                sp.dma_start(proj[half * HID1:(half + 1) * HID1, half:E1:2, :],
                             f["w_proj"].rearrange("(a two) h d -> two h a d", two=2)[half]).then_inc(weights_in, 16)

        @block.vector
        def _(dve):
            nc.vector.memset(proj[:, :, :], 0.0).then_inc(zeroed, 1)
            for q in range(PAIRS):
                dve.wait_ge(silu_done, q + 1)
                wait(dve, down, 2 * (q - 1))
                nc.vector.tensor_tensor(hid[:, q % 2, :], F_ps[q % 2][:, :], silu[:, q % 2, :], ALU.mult).then_inc(hid_ready, 1)

        @block.scalar
        def _(act):
            def out(e):
                act.wait_ge(down, e + 1)
                nc.scalar.copy(outT[:, :, e, :], O_ps[e % 2][:, :].rearrange("p (b s) -> p b s", s=CAP)).then_inc(out_done, 1)

            for q in range(PAIRS + 1):
                if q < PAIRS:
                    act.wait_ge(up, q + 1)
                    wait(act, hid_ready, q - 1)
                    nc.scalar.activation(silu[:, q % 2, :], G_ps[q % 2][:, :], ACT.Silu).then_inc(silu_done, 1)
                if q > 0:
                    out(2 * q - 2)
                    out(2 * q - 1)

        @block.tensor
        def _(pe):
            pe.wait_ge(weights_in, 64)
            for q in range(PAIRS + 1):
                if q < PAIRS:
                    wait(pe, hid_ready, q - 1)
                    for w, to in ((gate, G_ps), (fc, F_ps)):
                        for half in range(2):
                            last = nc.tensor.matmul(to[q % 2][half * HID1:(half + 1) * HID1, :], w[:, 2 * q + half, :],
                                                    r["slotsT"][:, 2 * q + half, :, :].rearrange("p b s -> p (b s)"), start=True, stop=True,
                                                    skip_group_check=True)
                    last.then_inc(up, 1)
                if q > 0:
                    pe.wait_ge(hid_ready, q)
                    for e in (2 * q - 2, 2 * q - 1):
                        wait(pe, out_done, e - 1)
                        nc.tensor.matmul(O_ps[e % 2][:, :], proj[:, e, :], hid[:, (q - 1) % 2, :], start=True,
                                         stop=True).then_inc(down, 1)


def collect(nc, r, tg, x_all, outT, out):
    with ExitStack() as ctx:
        def sb(name, shape, dt=F32):
            return ctx.enter_context(nc.sbuf_tensor("c_" + name, shape, dt))

        def sem(name):
            return ctx.enter_context(nc.semaphore("c_" + name))

        slots_now = sb("slots_now", [P, 2, 2 * SLOTS])
        combine_now = sb("combine_now", [P, 2, 2, P])
        slots = sb("slots", [P, 2, 2, D])
        final = sb("final", [P, 2, D])
        T_ps = [ctx.enter_context(nc.psum_tensor(f"c_T_ps{n}", [P, 512], F32)) for n in range(2)]
        Y_ps = [ctx.enter_context(nc.psum_tensor(f"c_Y_ps{n}", [P, 512], F32)) for n in range(2)]
        staged = sem("staged")
        turned = sem("turned")
        turned_out = sem("turned_out")
        y_ready = sem("y_ready")
        y_out = sem("y_out")
        stored = [sem("stored0"), sem("stored1")]
        block = ctx.enter_context(nc.Block())

        @block.gpsimd
        def _(pool):
            def stage(T):
                wait(pool, y_ready, T.t - 1)
                nc.gpsimd.tensor_copy(slots_now[:, T.par, :], outT[:, bass.ds(2 * T.t, 2), :, :].rearrange("p b e s -> p (b e s)"))
                nc.gpsimd.tensor_copy(combine_now[:, T.par, :, :].rearrange("p b k -> p (b k)"), r["combineT"][:, bass.ds(T.t * 2 * P, 2 * P)]).then_inc(staged, 1)

            pipeline(pool, [(stage, 0)], NT)

        @block.scalar
        def _(act):
            def turn_out(T):
                act.wait_ge(turned, T.t + 1)
                wait(act, y_ready, T.t - 1)
                nc.scalar.copy(slots[:, T.par, :, :].rearrange("p b k -> p (b k)"), T_ps[T.par][:, 0:256]).then_inc(turned_out, 1)

            pipeline(act, [(turn_out, 0)], NT)

        @block.tensor
        def _(pe):
            def turn(T):
                pe.wait_ge(staged, T.t + 1)
                wait(pe, turned_out, T.t - 1)
                for b in range(2):
                    last = nc.tensor.transpose(T_ps[T.par][:, b * P:(b + 1) * P], slots_now[:, T.par, b * P:(b + 1) * P],
                                               r["ident"][:, :])
                last.then_inc(turned, 1)

            def weigh(T):
                pe.wait_ge(turned_out, T.t + 1)
                wait(pe, y_out, T.t - 1)
                for b in range(2):
                    last = nc.tensor.matmul(Y_ps[T.par][:, 0:D], combine_now[:, T.par, b, :], slots[:, T.par, b, :],
                                            start=b == 0, stop=b == 1)
                last.then_inc(y_ready, 1)

            pipeline(pe, [(turn, 0), (weigh, 1)], NT)

        @block.vector
        def _(dve):
            def add(T):
                dve.wait_ge(y_ready, T.t + 1)
                wait(dve, stored[T.par], T.half * 16)
                nc.vector.scalar_tensor_tensor(final[:, T.par, :], Y_ps[T.par][:, 0:D], tg[:, 3:4],
                                               x_all[:, bass.ds(T.t * D, D)], ALU.mult, ALU.add).then_inc(y_out, 1)

            pipeline(dve, [(add, 0)], NT)

        @block.sync
        def _(sp):
            def store(T):
                sp.wait_ge(y_out, T.t + 1)
                sp.dma_start(out[bass.ds(T.t * P, P), :], final[:, T.par, :]).then_inc(stored[T.par], 16)

            pipeline(sp, [(store, 0)], NT)
            for s in stored:
                sp.wait_ge(s, 16 * NT // 2)


def setup(nc, ctx, d, tg, w0, w1):
    with ExitStack() as own:
        def sem(name):
            return own.enter_context(nc.semaphore(name))

        gates = own.enter_context(nc.sbuf_tensor("gates", [P, 4], F32))
        gates_in = sem("gates_in")
        loaded = sem("weights_in")
        tanh_done = sem("tanh_done")
        wo_zeroed = sem("wo_zeroed")
        casts = sem("casts")
        block = own.enter_context(nc.Block())
        loads = []
        for w, q in ((w0, "L0"), (w1, "L1")):
            loads += [(w["wq"][:, :], d[q + "wq"]), (w["wk"][:, :], d[q + "wk"]), (w["wv"][:, :], d[q + "wv"]),
                      (w["bq"][:, :], d[q + "bq"]), (w["bk"][:, :], d[q + "bk"]),
                      (w["bv"][:, :], d[q + "bv"].partition_broadcast(P)), (w["bo"][:, :], d[q + "bo"].partition_broadcast(P))]
            for j in range(4):
                loads.append((w["wo"][32 * j:32 * j + 16, :, :],
                              d[q + "wo"].rearrange("(g j r) o -> j r g o", g=2, j=4)[j]))
        loads += [(w0["ident"][:, :], d["ident"]), (w0["head_rows"][:, :], d["head_rows"]), (w0["ones_blk"][:, :], d["ones_blk"])]
        loads += d["more_loads"]

        @block.sync
        def _(sp):
            sp.dma_start(gates[:, 0:2], d["g_xattn"].partition_broadcast(P)).then_inc(gates_in, 16)
            sp.dma_start(gates[:, 2:4], d["g_ffn"].partition_broadcast(P)).then_inc(gates_in, 16)
            sp.wait_ge(wo_zeroed, 2)
            for to, what in loads:
                sp.dma_start(to, what).then_inc(loaded, 16)

        @block.scalar
        def _(act):
            act.wait_ge(gates_in, 32)
            nc.scalar.activation(tg[:, :], gates[:, :], ACT.Tanh).then_inc(tanh_done, 1)

        @block.vector
        def _(dve):
            nc.vector.memset(w0["wo"][:, :, :], 0.0).then_inc(wo_zeroed, 1)
            nc.vector.memset(w1["wo"][:, :, :], 0.0).then_inc(wo_zeroed, 1)
            nc.vector.memset(w0["minus_half"][:, :], -0.5)
            nc.vector.memset(d["ones_bf"][:, :], 1.0)
            dve.wait_ge(loaded, 16 * len(loads))
            dve.wait_ge(tanh_done, 1)
            for n, w in enumerate((w0, w1)):
                nc.vector.tensor_scalar(w["wo"][:, :, :], w["wo"][:, :, :], tg[:, n:n + 1], None, ALU.mult)
                nc.vector.tensor_scalar(w["bo"][:, :], w["bo"][:, :], tg[:, n:n + 1], None, ALU.mult)
            for to, what in d["casts"]:
                nc.vector.tensor_copy(to, what)


def program(nc, d, out):
    with ExitStack() as ctx:
        def sb(name, shape, dt=F32):
            return ctx.enter_context(nc.sbuf_tensor(name, shape, dt))

        x_all = sb("x_all", [P, NT * D])
        tg = sb("tg", [P, 4])
        w0, w1 = {}, {}
        for q, w in (("L0", w0), ("L1", w1)):
            for name, shape in (("wq", [P, D]), ("wk", [P, D]), ("wv", [P, D]), ("wo", [P, 2, D]),
                                ("bq", [P, 1]), ("bk", [P, 1]), ("bv", [P, D]), ("bo", [P, D])):
                w[name] = sb(q + name, shape)
        for name, shape, dt in (("ident", [P, P], F32), ("head_rows", [P, H], F32), ("ones_blk", [P, 32], F32),
                                ("minus_half", [P, 1], F32), ("ident_bf", [P, P], BF16)):
            w0[name] = w1[name] = sb(name, shape, dt)
        r0, r1 = {}, {}
        for name, shape, dt in (("before0", [P, P], F32), ("before1", [P, P], F32), ("ones1", [P, P], F32), ("iota", [P, 2 * SLOTS], F32),
                                ("batch_slot", [P, 1], F32), ("router0", [P, E0], F32), ("router1", [P, E1], F32),
                                ("start", [P, E0], F32), ("region", [P, E0], F32), ("edges", [P, NT], F32),
                                ("upto", [P, E0 * E0], F32), ("tile_no", [P, MAX_TILES], F32),
                                ("before0_bf", [P, P], BF16), ("before1_bf", [P, P], BF16), ("ones1_bf", [P, P], BF16),
                                ("ones_bf", [P, P], BF16), ("row_all", [P, NT], F32)):
            r0[name] = sb(name, shape, dt)
        r0.update(w0)
        r1 = dict(r0)
        r0.update(before=r0["before0_bf"], ones=r0["ones_bf"], router=r0["router0"])
        r1.update(before=r0["before1_bf"], ones=r0["ones1_bf"], router=r0["router1"])
        r0["sorted"] = nc.dram_tensor("sorted_rows", (ROWS, D), F32, kind="Internal").ap()
        r0["expert_out"] = nc.dram_tensor("expert_out", (MAX_TILES * P, D), F32, kind="Internal").ap()
        d["more_loads"] = [(r0[n][:, :], d[n]) for n in ("before0", "before1", "ones1", "batch_slot", "router0", "router1")]
        d["more_loads"] += [(r0[n][:, :], d[n].partition_broadcast(P)) for n in ("iota", "start", "region", "edges", "upto", "tile_no")]
        d["casts"] = [(w0["ident_bf"][:, :], w0["ident"][:, :]), (r0["before0_bf"][:, :], r0["before0"][:, :]),
                      (r0["before1_bf"][:, :], r0["before1"][:, :]), (r0["ones1_bf"][:, :], r0["ones1"][:, :])]
        d["ones_bf"] = r0["ones_bf"]
        setup(nc, ctx, d, tg, w0, w1)
        attention(nc, 0, x_all, w0, d, lambda env: router(nc, env, 0, r0))
        experts0(nc, r0, d)
        r1["combineT"] = sb("combineT", [P, NT * 2 * P])
        with ExitStack() as own:
            r1["slotsT"] = own.enter_context(nc.sbuf_tensor("slotsT", [P, E1, B, CAP], F32))

            def hooks(env):
                h = router(nc, env, 1, r1)
                fetched = [env["sem"]("fetched0"), env["sem"]("fetched1")]
                row_now = env["sem"]("row_now_ready")
                added = env["sem"]("ffn_added")
                row = env["sb"]("row_now", [P, 2], I32)
                back = env["sb"]("back", [P, 2, D])

                def fetch(T):
                    wait(nc.gpsimd, added, T.t - 1)
                    nc.gpsimd.tensor_copy(row[:, T.par:T.par + 1], r0["row_all"][:, bass.ds(T.t, 1)]).then_inc(row_now, 1)
                    nc.gpsimd.wait_ge(row_now, T.t + 1)
                    apart(nc.gpsimd)
                    nc.gpsimd.indirect_dma_start(back[:, T.par, :], None, r0["expert_out"],
                                                 bass.IndirectOffsetOnAxis(ap=row[:, T.par:T.par + 1], axis=0)).then_inc(fetched[T.par], 16)

                def before_norm(dve, T):
                    xt = x_all[:, bass.ds(T.t * D, D)]
                    dve.wait_ge(fetched[T.par], (T.half + 1) * 16)
                    nc.vector.scalar_tensor_tensor(xt, back[:, T.par, :], tg[:, 2:3], xt, ALU.mult, ALU.add).then_inc(added, 1)
                    dve.wait_ge(added, T.t + 1)
                    apart(dve)

                h["pool_first"] = [(fetch, -1)]
                h["before_norm"] = before_norm
                return h

            attention(nc, 1, x_all, w1, d, hooks)
            outT = own.enter_context(nc.sbuf_tensor("outT", [P, B, E1, CAP], F32))
            experts1(nc, r1, d, outT)
            collect(nc, r1, tg, x_all, outT, out)


def kernel(**inputs):
    import numpy as np
    import concourse.bacc as bacc
    from concourse import mybir as my
    from concourse.bass_utils import run_bass_kernel_spmd as run

    nc = bacc.Bacc("TRN2", target_bir_lowering=False, num_devices=1)
    i = {k: np.asarray(v) for k, v in inputs.items()}
    T = B * S
    arrays = {
        "x": i["x"].reshape(T, D), "ctx": i["ctx_1024"].reshape(T, D), "mask": i["mask_BxSxS2_ik1"].reshape(T, S),
        "g_xattn": i["g_xattn"], "g_ffn": i["g_ffn"],
        "L0wq": i["L0_xattn_w_q"].T, "L0wk": i["L0_xattn_w_k"].T, "L0wv": i["L0_xattn_w_v"].T, "L0wo": i["L0_xattn_w_o"].T,
        "L0bq": i["L0_xattn_b_q"].reshape(D, 1), "L0bk": i["L0_xattn_b_k"].reshape(D, 1),
        "L0bv": i["L0_xattn_b_v"], "L0bo": i["L0_xattn_b_o"],
        "L1wo": i["L1_xattn_out_proj_weight"], "L1bo": i["L1_xattn_out_proj_bias"],
    }
    for n, name in enumerate(("q", "k", "v")):
        arrays["L1w" + name] = i["L1_xattn_in_proj_weight"][:, n * D:(n + 1) * D]
        bias = i["L1_xattn_in_proj_bias"][n * D:(n + 1) * D]
        arrays["L1b" + name] = bias if name == "v" else bias.reshape(D, 1)
    p = np.arange(P)
    arrays["ident"] = np.eye(P, dtype=np.float32)
    arrays["head_rows"] = (p[:, None] // DK == np.arange(H)[None, :]).astype(np.float32)
    col = np.arange(32)[None, :]
    arrays["ones_blk"] = ((p[:, None] // S == col // DK) | (col >= 2 * DK)).astype(np.float32)
    row, col = p[:, None], p[None, :]
    same = row // S == col // S
    arrays["before0"] = (row < col).astype(np.float32)
    arrays["before1"] = ((row < col) & same).astype(np.float32)
    arrays["ones1"] = same.astype(np.float32)
    arrays["batch_slot"] = (row // S * SLOTS).astype(np.float32)
    arrays["iota"] = np.arange(2 * SLOTS, dtype=np.float32)
    arrays["start"] = arrays["region"] = np.arange(E0, dtype=np.float32) * REGION
    arrays["edges"] = np.arange(NT, dtype=np.float32) * P
    arrays["upto"] = np.tril(np.ones((E0, E0), np.float32)).ravel()
    arrays["tile_no"] = np.arange(MAX_TILES, dtype=np.float32)
    arrays["router0"] = i["L0_ffn_Wg"].T
    arrays["router1"] = i["L1_ffn_w_router"]
    arrays["W1"], arrays["W2"], arrays["b2"] = i["L0_ffn_W1"], i["L0_ffn_W2"], i["L0_ffn_b2"]
    arrays["b1"] = i["L0_ffn_b1"].reshape(E0, NC0, P).transpose(2, 0, 1)
    for name in ("w_fc", "w_gate", "w_proj"):
        arrays[name] = i["L1_ffn_" + name]
    arrays = {k: np.ascontiguousarray(v) for k, v in arrays.items()}
    d = {k: nc.dram_tensor(f"in_{k}", a.shape, my.dt.from_np(a.dtype), kind="ExternalInput").ap() for k, a in arrays.items()}
    out = nc.dram_tensor("out_0", (T, D), my.dt.from_np(np.dtype("float32")), kind="ExternalOutput").ap()
    program(nc, d, out)
    r = run(nc, [{f"in_{k}": a for k, a in arrays.items()}], core_ids=[0])
    return r.results[0]["out_0"].reshape(B, S, D)
```

```python
from contextlib import ExitStack

import concourse.bass as bass
from concourse import mybir

F32 = mybir.dt.float32
BF16 = mybir.dt.bfloat16
I32 = mybir.dt.int32
U32 = mybir.dt.uint32
ALU = mybir.AluOpType
ACT = mybir.ActivationFunctionType
X = mybir.AxisListType.X

B, S, D = 64, 64, 128
H, DK = 16, 8
HP = H // 2
P = 128
NT = B * S // P
E0, HID0 = 8, 512
NC0 = HID0 // P
REGION = B * S + P
MAX_TILES = NT + E0 - 1
ROWS = E0 * REGION + (MAX_TILES - NT) * P
E1, HID1 = 16, 64
CAP = 2 * S // E1
SLOTS = E1 * CAP
EPS = 1e-5
SCALE = DK ** -0.5
MASKED = -1e9
ALL_MASKED = -2.0 ** 100


class Tile:

    def __init__(self, t, par, half):
        self.t, self.par, self.half = t, par, half


def number(t):
    return Tile(t, t % 2, t // 2)


def pipeline(eng, steps, count):
    most = max(skew for _, skew in steps)
    least = min(0, min(skew for _, skew in steps))
    first = most + 2 + most % 2
    last = count + least
    last -= (last - first) % 2

    def alone(n):
        for step, skew in steps:
            if 0 <= n - skew < count:
                step(number(n - skew))

    for n in range(least, first):
        alone(n)
    with eng.Fori(0, (last - first) // 2) as i:
        for u in range(2):
            for step, skew in steps:
                c = first + u - skew
                step(Tile(i * 2 + c, c % 2, i + c // 2))
    for n in range(last, count + most):
        alone(n)


def wait(eng, sem, value):
    if not (isinstance(value, int) and value <= 0):
        eng.wait_ge(sem, value)


def apart(eng):
    eng.nop(nofuse=True)


class Chain:

    def __init__(self, eng, sem, t, n):
        self.eng, self.sem, self.base, self.n, self.k = eng, sem, t * n, n, 0

    def __call__(self, ins, alone=False):
        self.k += 1
        assert self.k <= self.n
        ins.then_inc(self.sem, 1)
        self.eng.wait_ge(self.sem, self.base + self.k)
        if alone:
            apart(self.eng)


def attention(nc, layer, x_all, w, dram, hooks):
    with ExitStack() as ctx:
        def sb(name, shape, dt=F32):
            return ctx.enter_context(nc.sbuf_tensor(f"{name}_{layer}", shape, dt))

        def ps(name, shape, dt=F32):
            return ctx.enter_context(nc.psum_tensor(f"{name}_{layer}", shape, dt))

        def sem(name):
            return ctx.enter_context(nc.semaphore(f"{name}_{layer}"))

        masked = layer == 0
        ctx_in = sb("ctx_in", [P, 2, D])
        mask_in = sb("mask_in", [P, 2, S], I32)
        mask_zero = sb("mask_zero", [P, S])
        mask_all = sb("mask_all", [P, 2])
        mask_bias = sb("mask_bias", [P, 2, S], BF16)
        stats = sb("stats", [P, 6])
        mv = sb("mv", [P, 2, 2])
        rstd = sb("rstd", [P, 2])
        xn = sb("xn", [P, 2, D])
        xnT = sb("xnT", [P, 2, P])
        ctxT = sb("ctxT", [P, 2, 2, 2, S])
        qT = sb("qT", [P, 2, P])
        kT = sb("kT", [P, 2, P])
        k_blk = sb("k_blk", [P, 2, 2, H, S])
        v_blk = sb("v_blk", [P, 2, 2, HP, 32])
        prob = sb("prob", [P, 2, H, S])
        probT = sb("probT", [P, HP, P])
        rden = sb("rden", [P, 2, P])
        avT = sb("avT", [P, 2, P])
        x_bo = sb("x_bo", [P, 2, D])
        maxes = sb("maxes", [P, 2, H])

        S_ps = [ps("S_ps0", [P, HP, S]), ps("S_ps1", [P, HP, S])]
        T_ps = [ps("T_ps0", [P, 4, P]), ps("T_ps1", [P, 4, P])]
        A_ps = ps("A_ps", [P, 4, P])
        O_ps = ps("O_ps", [P, 2, 2, P])
        Y_ps = ps("Y_ps", [P, 512])
        V_ps = Y_ps[:, 256:512].rearrange("p (b a r d) -> p b a r d", b=2, a=HP, r=2)
        R_ps = ps("R_ps", [P, 512])

        loaded = [sem("loaded0"), sem("loaded1")]
        x_ready = sem("x_ready")
        mask_biased = sem("mask_biased")
        ln_stats = sem("ln_stats")
        ln_rstd = sem("ln_rstd")
        xn_ready = sem("xn_ready")
        xo_ready = sem("xo_ready")
        turned = sem("turned")
        turned_out = sem("turned_out")
        qk_ready = sem("qk_ready")
        qk_out = sem("qk_out")
        v_ready = sem("v_ready")
        v_out = sem("v_out")
        kblk_ready = sem("kblk_ready")
        scored = sem("scored")
        shifted = sem("shifted")
        exp_ready = sem("exp_ready")
        probs_turned = sem("probs_turned")
        probT_ready = sem("probT_ready")
        av_ready = sem("av_ready")
        rden_ready = sem("rden_ready")
        divided = sem("divided")
        y_ready = sem("y_ready")
        y_out = sem("y_out")
        a_chain = sem("a_chain")
        m_chain = sem("m_chain")
        b_chain = sem("b_chain")
        zeroed = sem("zeroed")

        block = ctx.enter_context(nc.Block())
        env = dict(ctx=ctx, sb=sb, ps=ps, sem=sem, x_all=x_all, R_ps=R_ps, y_ready=y_ready, y_out=y_out, x_ready=x_ready)
        hook = hooks(env)
        LOADS = 48 if masked else 16

        @block.sync
        def _(sp):
            def load(T):
                wait(sp, turned, T.t - 1)
                sp.dma_start(ctx_in[:, T.par, :], dram["ctx"][bass.ds(T.t * P, P), :]).then_inc(loaded[T.par], 16)
                if masked:
                    wait(sp, mask_biased, T.t - 1)
                    sp.dma_start(x_all[:, bass.ds(T.t * D, D)], dram["x"][bass.ds(T.t * P, P), :]).then_inc(loaded[T.par], 16)
                    sp.dma_start(mask_in[:, T.par, :], dram["mask"][bass.ds(T.t * P, P), :]).then_inc(loaded[T.par], 16)

            pipeline(sp, [(load, 0)] + hook["sync"], NT)
            pass

        @block.gpsimd
        def _(pool):
            nc.gpsimd.memset(v_blk[:, :, :, :, :], 0.0).then_inc(zeroed, 1)

            def std(T):
                pool.wait_ge(ln_stats, T.t + 1)
                nc.gpsimd.tensor_tensor(rstd[:, T.par:T.par + 1], mv[:, T.par, 1:2], w["minus_half"][:, 0:1],
                                        ALU.pow).then_inc(ln_rstd, 1)

            def residual(T):
                pool.wait_ge(xn_ready, T.t + 1)
                wait(pool, y_out, T.t - 1)
                nc.gpsimd.tensor_tensor(x_bo[:, T.par, :], x_all[:, bass.ds(T.t * D, D)], w["bo"][:, :],
                                        ALU.add).then_inc(xo_ready, 1)

            def blocks(T):
                pool.wait_ge(qk_out, 2 * T.t + 2)
                wait(pool, scored, 2 * T.t - 2)
                for b in range(2):
                    last = nc.gpsimd.tensor_tensor(
                        k_blk[:, T.par, b, :, :],
                        kT[:, T.par, b * S:(b + 1) * S].unsqueeze(1).to_broadcast([P, H, S]),
                        w["head_rows"][:, :].unsqueeze(2).to_broadcast([P, H, S]), ALU.mult)
                last.then_inc(kblk_ready, 1)

            pipeline(pool, hook["pool_first"] + [(residual, 3)] + hook["pool"] + [(std, -1), (blocks, 0)], NT)
            hook["pool_end"](pool)

        @block.scalar
        def _(act):
            def turn_out(T):
                act.wait_ge(turned, T.t + 1)
                wait(act, qk_ready, T.t - 1)
                wait(act, v_ready, T.t - 1)
                nc.scalar.copy(ctxT[:, T.par, :, :, :], A_ps[:, 1, :].rearrange("p (b k) -> p b k", b=2)
                               .unsqueeze(2).to_broadcast([P, 2, 2, S])).then_inc(turned_out, 1)
                nc.scalar.copy(xnT[:, T.par, :], A_ps[:, 0, :]).then_inc(turned_out, 1)

            def qk(T):
                act.wait_ge(qk_ready, T.t + 1)
                wait(act, scored, 2 * T.t - 2)
                nc.scalar.activation(qT[:, T.par, :], A_ps[:, 2, :], ACT.Identity, bias=w["bq"][:, 0:1]).then_inc(qk_out, 1)
                nc.scalar.activation(kT[:, T.par, :], A_ps[:, 3, :], ACT.Identity, bias=w["bk"][:, 0:1]).then_inc(qk_out, 1)

            def exps(T):
                for g in range(2):
                    act.wait_ge(shifted, 2 * T.t + g + 1)
                    part = prob[:, T.par, g * HP:(g + 1) * HP, :]
                    nc.scalar.activation(part, part, ACT.Exp, scale=SCALE).then_inc(exp_ready, 1)

            def probs_out(T):
                for g in range(2):
                    act.wait_ge(probs_turned, 2 * T.t + g + 1)
                    wait(act, av_ready, T.t)
                    nc.scalar.copy(probT[:, 4 * g:4 * g + 4, :], T_ps[g][:, :, :]).then_inc(probT_ready, 1)

            pipeline(act, [(turn_out, 0)] + hook["act"] + [(probs_out, 3), (exps, 2), (qk, 0)], NT)

        @block.vector
        def _(dve):
            def stat(T):
                if masked:
                    dve.wait_ge(loaded[T.par], (T.half + 1) * LOADS)
                else:
                    hook["before_norm"](dve, T)
                step = Chain(dve, a_chain, T.t, 2)
                step(nc.vector.bn_stats(stats[:, :], x_all[:, bass.ds(T.t * D, D)]), alone=True)
                step(nc.vector.bn_aggr(mv[:, T.par, :], stats[:, :]))
                nc.vector.tensor_scalar(mv[:, T.par, 1:2], mv[:, T.par, 1:2], EPS, None, ALU.add).then_inc(ln_stats, 1)

            def norm(T):
                dve.wait_ge(ln_rstd, T.t + 1)
                wait(dve, turned, T.t - 1)
                nc.vector.tensor_scalar(xn[:, T.par, :], x_all[:, bass.ds(T.t * D, D)], mv[:, T.par, 0:1],
                                        rstd[:, T.par:T.par + 1], ALU.subtract, ALU.mult).then_inc(xn_ready, 1)

            def mask(T):
                step = Chain(dve, m_chain, T.t, 3)
                step(nc.vector.tensor_scalar(mask_zero[:, :], mask_in[:, T.par, :], 0.0, None, ALU.is_equal))
                step(nc.vector.tensor_reduce(mask_all[:, 0:1], mask_zero[:, :], X, ALU.min))
                step(nc.vector.tensor_scalar(mask_all[:, 1:2], mask_all[:, 0:1], ALL_MASKED, MASKED, ALU.mult, ALU.add))
                wait(dve, scored, 2 * T.t - 2)
                nc.vector.tensor_scalar(mask_bias[:, T.par, :], mask_zero[:, :], mask_all[:, 1:2], None,
                                        ALU.mult).then_inc(mask_biased, 1)

            def values(T):
                dve.wait_ge(v_ready, T.t + 1)
                if isinstance(T.t, int) and T.t == 0:
                    dve.wait_ge(zeroed, 1)
                wait(dve, av_ready, T.t - 1)
                for r in range(2):
                    half = slice(r * S, (r + 1) * S)
                    last = nc.vector.tensor_tensor(
                        v_blk[half, T.par, :, :, r * DK:(r + 1) * DK], V_ps[half, :, :, r, :],
                        w["bv"][half, :].rearrange("p (a r d) -> p a r d", a=HP, r=2)[:, :, r, :]
                        .unsqueeze(1).to_broadcast([S, 2, HP, DK]), ALU.add)
                last.then_inc(v_out, 1)

            def softmax(T):
                step = Chain(dve, b_chain, T.t, 2)
                for g in range(2):
                    heads = slice(g * HP, (g + 1) * HP)
                    dve.wait_ge(scored, 2 * T.t + g + 1)
                    step(nc.vector.tensor_reduce(maxes[:, T.par, heads], S_ps[g][:, :, :], X, ALU.max))
                    wait(dve, probs_turned, 2 * T.t - 2)
                    nc.vector.tensor_tensor(
                        prob[:, T.par, heads, :], S_ps[g][:, :, :],
                        maxes[:, T.par, heads].unsqueeze(2).to_broadcast([P, HP, S]), ALU.subtract).then_inc(shifted, 1)

            def divide(T):
                dve.wait_ge(av_ready, T.t + 1)
                nc.vector.reciprocal(rden[:, :, :], O_ps[:, 1, :, :]).then_inc(rden_ready, 1)
                dve.wait_ge(rden_ready, T.t + 1)
                wait(dve, y_ready, T.t)
                nc.vector.tensor_tensor(avT[:, :, :], O_ps[:, 0, :, :], rden[:, :, :], ALU.mult).then_inc(divided, 1)

            def add(T):
                dve.wait_ge(y_ready, T.t + 1)
                dve.wait_ge(xo_ready, T.t + 1)
                nc.vector.tensor_tensor(x_all[:, bass.ds(T.t * D, D)], Y_ps[:, 0:D], x_bo[:, T.par, :],
                                        ALU.add).then_inc(y_out, 1)

            pipeline(dve, hook["dve_first"] + [(divide, 4), (softmax, 2), (add, 4)] + hook["dve"] + [(values, 1), (stat, -1)]
                     + ([(mask, 0)] if masked else []) + [(norm, -1)], NT)

        @block.tensor
        def _(pe):
            ident = w["ident"]

            def turn(T):
                pe.wait_ge(xn_ready, T.t + 1)
                wait(pe, qk_out, 2 * T.t)
                pe.wait_ge(loaded[T.par], (T.half + 1) * LOADS)
                nc.tensor.transpose(A_ps[:, 1, :], ctx_in[:, T.par, :], ident[:, :])
                nc.tensor.transpose(A_ps[:, 0, :], xn[:, T.par, :], ident[:, :]).then_inc(turned, 1)

            def project(T):
                pe.wait_ge(turned_out, 2 * T.t + 2)
                nc.tensor.matmul(A_ps[:, 2, :], w["wq"][:, :], xnT[:, T.par, :], start=True, stop=True)
                nc.tensor.matmul(A_ps[:, 3, :], w["wk"][:, :], ctxT[:, T.par, :, 0, :], start=True, stop=True).then_inc(qk_ready, 1)

            def project_v(T):
                wait(pe, v_out, T.t)
                wait(pe, y_out, T.t - 2)
                for b in range(2):
                    last = nc.tensor.matmul(V_ps[:, b, :, :, :].rearrange("p a r d -> p (a r d)"),
                                            ctxT[:, T.par, b, :, :].rearrange("p r k -> p (r k)"),
                                            w["wv"][:, :], start=True, stop=True)
                last.then_inc(v_ready, 1)

            def score(T):
                pe.wait_ge(kblk_ready, T.t + 1)
                if masked:
                    pe.wait_ge(mask_biased, T.t + 1)
                for g in range(2):
                    wait(pe, shifted, 2 * T.t + g - 1)
                    if masked:
                        nc.tensor.matmul(S_ps[g][:, :, :], w["ident_bf"][:, :],
                                         mask_bias[:, T.par, :].unsqueeze(1).to_broadcast([P, HP, S]),
                                         start=True, stop=False, skip_group_check=True)
                    for b in range(2):
                        last = nc.tensor.matmul(S_ps[g][b * S:(b + 1) * S, :, :], qT[:, T.par, b * S:(b + 1) * S],
                                                k_blk[:, T.par, b, g * HP:(g + 1) * HP, :],
                                                start=not masked, stop=True, skip_group_check=True)
                    last.then_inc(scored, 1)

            def turn_probs(T):
                for g in range(2):
                    pe.wait_ge(exp_ready, 2 * T.t + g + 1)
                    wait(pe, probT_ready, 2 * T.t + g - 1)
                    for j in range(4):
                        pair = prob[:, T.par, 8 * g + 2 * j:8 * g + 2 * j + 2, :].rearrange("p r k -> p (r k)")
                        last = nc.tensor.transpose(T_ps[g][:, j, :], pair, ident[:, :])
                    last.then_inc(probs_turned, 1)

            def attend(T):
                pe.wait_ge(v_out, T.t + 1)
                wait(pe, divided, T.t)
                for g in range(2):
                    pe.wait_ge(probT_ready, 2 * T.t + g + 1)
                    for b in range(2):
                        for j in range(4):
                            nc.tensor.matmul(O_ps[32 * j:32 * j + 32, 0, g, b * S:(b + 1) * S],
                                             v_blk[:, T.par, b, 4 * g + j, :], probT[:, 4 * g + j, b * S:(b + 1) * S],
                                             start=True, stop=True, skip_group_check=True)
                    for j in range(4):
                        last = nc.tensor.matmul(O_ps[32 * j:32 * j + 32, 1, g, :], w["ones_blk"][:, :],
                                                probT[:, 4 * g + j, :], start=True, stop=True, skip_group_check=True)
                last.then_inc(av_ready, 1)

            def output(T):
                pe.wait_ge(divided, T.t + 1)
                wait(pe, y_out, T.t)
                wait(pe, v_out, min(T.t + 3, NT) if isinstance(T.t, int) else T.t + 3)
                for g in range(2):
                    last = nc.tensor.matmul(Y_ps[:, 0:D], avT[:, g, :], w["wo"][:, g, :],
                                            start=g == 0, stop=g == 1)
                last.then_inc(y_ready, 1)

            pipeline(pe, [(score, 2), (turn, 0)] + hook["pe_turn"] + [(output, 4), (turn_probs, 3)] + hook["pe_logits"]
                     + [(project, 0), (attend, 3)] + hook["pe_ranks"] + [(project_v, 1)], NT)


def router(nc, env, layer, r):
    sb, sem = env["sb"], env["sem"]
    x_all, R_ps, y_out = env["x_all"], env["R_ps"], env["y_out"]
    E = E0 if layer == 0 else E1
    stats = sb("r_stats", [P, 6])
    mv = sb("r_mv", [P, 2, 2])
    rstd = sb("r_rstd", [P, 2])
    xn = sb("r_xn", [P, 2, D])
    xnT = sb("r_xnT", [P, P])
    logits = sb("r_logits", [P, E])
    top = sb("r_top", [P, 8])
    top_at = sb("r_top_at", [P, 8], U32)
    expert = sb("r_expert", [P, 2])
    chosen = sb("r_chosen", [P, 2, E], BF16)
    product = sb("r_product", [P, E])
    place = sb("r_place", [P, E])
    rank = sb("r_rank", [P, 2])
    LOG = R_ps[:, 0:E]
    RANK = R_ps[:, 32:32 + E]
    COUNT = R_ps[:, 64:64 + E]
    XT = R_ps[:, 128:256]

    r_stats = sem("r_stats_ready")
    r_rstd = sem("r_rstd_ready")
    r_xn = sem("r_xn_ready")
    r_turned = sem("r_turned")
    r_xnT = sem("r_xnT_ready")
    r_logits = sem("r_logits_ready")
    r_chosen = sem("r_chosen_ready")
    r_ranked = sem("r_ranked")
    r_done = sem("r_done")
    s_chain = sem("r_s_chain")
    t_chain = sem("r_t_chain")
    p_chain = sem("r_p_chain")
    h = {k: [] for k in ("sync", "pool_first", "pool", "act", "dve_first", "dve", "pe_turn", "pe_logits", "pe_ranks")}
    vec, pool, act, pe = nc.vector, nc.gpsimd, nc.scalar, nc.tensor

    def stat(T):
        step = Chain(vec, s_chain, T.t, 2)
        vec.wait_ge(y_out, T.t + 1)
        apart(vec)
        step(vec.bn_stats(stats[:, :], x_all[:, bass.ds(T.t * D, D)]), alone=True)
        step(vec.bn_aggr(mv[:, T.par, :], stats[:, :]))
        vec.tensor_scalar(mv[:, T.par, 1:2], mv[:, T.par, 1:2], EPS, None, ALU.add).then_inc(r_stats, 1)

    def std(T):
        pool.wait_ge(r_stats, T.t + 1)
        pool.tensor_tensor(rstd[:, T.par:T.par + 1], mv[:, T.par, 1:2], r["minus_half"][:, 0:1], ALU.pow).then_inc(r_rstd, 1)

    def norm(T):
        vec.wait_ge(r_rstd, T.t + 1)
        if layer == 0:
            wait(vec, scattered[T.par], T.half * 16)
        vec.tensor_scalar(xn[:, T.par, :], x_all[:, bass.ds(T.t * D, D)], mv[:, T.par, 0:1], rstd[:, T.par:T.par + 1],
                          ALU.subtract, ALU.mult).then_inc(r_xn, 1)

    def turn(T):
        pe.wait_ge(r_xn, T.t + 1)
        wait(pe, r_done, T.t)
        pe.transpose(XT, xn[:, T.par, :], r["ident"][:, :]).then_inc(r_turned, 1)

    def turn_out(T):
        act.wait_ge(r_turned, T.t + 1)
        act.copy(xnT[:, :], XT).then_inc(r_xnT, 1)

    def logit(T):
        pe.wait_ge(r_xnT, T.t + 1)
        pe.matmul(LOG, xnT[:, :], r["router"][:, :], start=True, stop=True).then_inc(r_logits, 1)

    h["dve_first"] = [(norm, 5)]
    h["act"] = [(turn_out, 5)]
    h["pe_turn"] = [(turn, 5)]
    h["pe_logits"] = [(logit, 5)]
    if layer == 1:
        xn_kept = sem("r_xn_kept")

        def keep(T):
            vec.wait_ge(r_logits, T.t + 1)
            vec.tensor_copy(r["logits"][:, bass.ds(T.t, 1), :].rearrange("p a e -> p (a e)"), LOG).then_inc(r_done, 1)

        def keep_xn(T):
            pool.wait_ge(r_xn, T.t + 1)
            pool.tensor_copy(r["xn"][:, bass.ds(T.t * D, D)], xn[:, T.par, :]).then_inc(xn_kept, 1)

        used = norm

        def norm1(T):
            wait(vec, xn_kept, T.t - 1)
            wait(vec, r_turned, T.t - 1)
            used(T)

        h["dve_first"] = [(norm1, 5)]
        h["dve"] = [(stat, 4), (keep, 5)]
        h["pool"] = [(keep_xn, 5), (std, 4)]
        h["pool_end"] = lambda eng: None
        return h

    row = sb("r_row", [P, 2], I32)
    scattered = [sem("r_scattered0"), sem("r_scattered1")]
    row_ready = sem("r_row_ready")

    def choose(T):
        step = Chain(vec, t_chain, T.t, 4)
        vec.wait_ge(r_logits, T.t + 1)
        step(vec.tensor_copy(logits[:, :], LOG), alone=True)
        step(vec.max(top[:, :], logits[:, :]), alone=True)
        step(vec.max_index(top_at[:, :], top[:, :], logits[:, :]))
        step(vec.tensor_copy(expert[:, :], top_at[:, 0:2]))
        vec.tensor_scalar(chosen[:, 0, :], r["iota"][:, 0:E], expert[:, 0:1], None, ALU.is_equal).then_inc(r_chosen, 1)

    def ranks(T):
        pe.wait_ge(r_chosen, T.t + 1)
        pe.matmul(RANK, r["before"][:, :], chosen[:, 0, :], start=True, stop=True)
        pe.matmul(COUNT, r["ones"][:, :], chosen[:, 0, :], start=True, stop=True).then_inc(r_ranked, 1)

    def rows(T):
        step = Chain(vec, p_chain, T.t, 2)
        vec.wait_ge(r_ranked, T.t + 1)
        step(vec.tensor_tensor(place[:, :], RANK, r["start"][:, :], ALU.add))
        step(vec.tensor_tensor_reduce(product[:, :], place[:, :], chosen[:, 0, :], 1.0, 0.0, ALU.mult, ALU.add,
                                      rank[:, 0:1]))
        vec.tensor_tensor(r["start"][:, :], r["start"][:, :], COUNT, ALU.add).then_inc(r_done, 1)
        wait(vec, scattered[T.par], T.half * 16)
        vec.tensor_copy(row[:, T.par:T.par + 1], rank[:, 0:1]).then_inc(row_ready, 1)
        vec.tensor_copy(r["row_all"][:, bass.ds(T.t, 1)], rank[:, 0:1]).then_inc(row_ready, 1)

    def scatter(T):
        pool.wait_ge(row_ready, 2 * T.t + 1)
        apart(pool)
        pool.indirect_dma_start(r["sorted"], bass.IndirectOffsetOnAxis(ap=row[:, T.par:T.par + 1], axis=0),
                                xn[:, T.par, :], None).then_inc(scattered[T.par], 16)

    def end(eng):
        for s in scattered:
            eng.wait_ge(s, 16 * NT // 2)

    h["dve_first"] = [(rows, 6), (norm, 5)]
    h["dve"] = [(stat, 4), (choose, 5)]
    h["pe_ranks"] = [(ranks, 5)]
    h["pool"] = [(scatter, 6), (std, 4)]
    h["pool_end"] = end
    return h


def assign1(nc, r):
    with ExitStack() as ctx:
        def sb(name, shape, dt=F32):
            return ctx.enter_context(nc.sbuf_tensor("a1_" + name, shape, dt))

        def sem(name):
            return ctx.enter_context(nc.semaphore("a1_" + name))

        ALL = [P, NT, E1]
        most = sb("most", [P, 2, NT])
        same = sb("same", ALL)
        level = sb("level", ALL)
        first = sb("first", [P, 2, NT])
        chosen = sb("chosen", [P, 2, NT, E1])
        chosen_bf = sb("chosen_bf", [P, 2, NT, E1], BF16)
        rest = sb("rest", ALL)
        shifted = sb("shifted", ALL)
        total = sb("total", [P, NT])
        r_total = sb("r_total", [P, NT])
        gap = sb("gap", [P, NT])
        picked = sb("picked", ALL)
        rank = sb("rank", [P, 2, NT])
        base = sb("base", [P, 2, NT])
        over = sb("over", [P, 2, NT])
        one = sb("one", [P, 2, 2 * SLOTS])
        dispatch = sb("dispatch", [P, 2, 2 * SLOTS])
        xn_now = sb("xn_now", [P, 2, D])
        R_ps = [ctx.enter_context(nc.psum_tensor(f"a1_R_ps{n}", [P, NT, E1], F32)) for n in range(2)]
        X_ps = [ctx.enter_context(nc.psum_tensor(f"a1_X_ps{n}", [P, 512], F32)) for n in range(2)]
        chain = sem("chain")
        shift_ready = sem("shift_ready")
        exp_done = sem("exp_done")
        chosen_ready = sem("chosen_ready")
        ranked = sem("ranked")
        matrix = sem("matrix")
        d_chain = sem("d_chain")
        staged = sem("staged")
        moved = sem("moved")
        moved_out = sem("moved_out")
        block = ctx.enter_context(nc.Block())
        vec = nc.vector

        @block.vector
        def _(dve):
            step = Chain(dve, chain, 0, 40)
            experts = r["iota"][:, 0:E1].unsqueeze(1).to_broadcast(ALL)

            def over_experts(ap):
                return ap.unsqueeze(2).to_broadcast(ALL)

            left = r["logits"]
            for k in range(2):
                step(vec.tensor_reduce(most[:, k, :], left[:, :, :], X, ALU.max))
                step(vec.tensor_tensor(same[:, :, :], left[:, :, :], over_experts(most[:, k, :]), ALU.is_equal))
                step(vec.tensor_tensor(level[:, :, :], same[:, :, :], r["from_last"][:, :].unsqueeze(1).to_broadcast(ALL), ALU.mult))
                step(vec.tensor_reduce(first[:, k, :], level[:, :, :], X, ALU.max))
                step(vec.tensor_tensor(chosen[:, k, :, :], level[:, :, :], over_experts(first[:, k, :]), ALU.is_equal))
                vec.tensor_copy(chosen_bf[:, k, :, :], chosen[:, k, :, :]).then_inc(chosen_ready, 1)
                if k == 0:
                    step(vec.scalar_tensor_tensor(rest[:, :, :].rearrange("p t e -> p (t e)"), chosen[:, 0, :, :].rearrange("p t e -> p (t e)"), -3e38,
                                                  left[:, :, :].rearrange("p t e -> p (t e)"), ALU.mult, ALU.add))
                    left = rest
            vec.tensor_tensor(shifted[:, :, :], r["logits"][:, :, :], over_experts(most[:, 0, :]), ALU.subtract).then_inc(shift_ready, 1)
            vec.tensor_tensor(gap[:, :], most[:, 1, :], most[:, 0, :], ALU.subtract).then_inc(shift_ready, 1)
            for k in range(2):
                dve.wait_ge(ranked, k + 1)
                step(vec.tensor_tensor(picked[:, :, :], R_ps[k][:, :, :], chosen[:, k, :, :], ALU.mult))
                step(vec.tensor_reduce(rank[:, k, :], picked[:, :, :], X, ALU.add))
            step(vec.tensor_scalar(base[:, :, :], first[:, :, :], -float(CAP), r["batch_slot"][:, 0:1], ALU.mult, ALU.add))
            step(vec.scalar_tensor_tensor(r["slot"][:, :, :], rank[:, :, :], float(CAP - 1), base[:, :, :], ALU.min, ALU.add))
            step(vec.tensor_scalar(over[:, :, :], rank[:, :, :], float(CAP), 4.0 * SLOTS, ALU.is_ge, ALU.mult))
            step(vec.tensor_tensor(r["sent"][:, :, :], over[:, :, :], r["slot"][:, :, :], ALU.add))
            dve.wait_ge(exp_done, 2)
            step(vec.tensor_reduce(total[:, :], shifted[:, :, :], X, ALU.add))
            step(vec.reciprocal(r["prob"][:, 0, :], total[:, :]))
            step(vec.tensor_tensor(r["prob"][:, 1, :], gap[:, :], r["prob"][:, 0, :], ALU.mult))

            def matrices(T):
                one_done = Chain(dve, d_chain, T.t, 1)
                wait(dve, moved, T.t - 1)
                one_done(vec.tensor_scalar(one[:, T.par, :], r["iota"][:, :], r["sent"][:, 0, bass.ds(T.t, 1)], None, ALU.is_equal))
                vec.scalar_tensor_tensor(dispatch[:, T.par, :], r["iota"][:, :], r["sent"][:, 1, bass.ds(T.t, 1)], one[:, T.par, :],
                                         ALU.is_equal, ALU.add).then_inc(matrix, 1)

            pipeline(dve, [(matrices, 0)], NT)

        @block.gpsimd
        def _(pool):
            def stage(T):
                wait(pool, moved, T.t - 1)
                nc.gpsimd.tensor_copy(xn_now[:, T.par, :], r["xn"][:, bass.ds(T.t * D, D)]).then_inc(staged, 1)

            pipeline(pool, [(stage, 0)], NT)

        @block.scalar
        def _(act):
            act.wait_ge(shift_ready, 2)
            nc.scalar.activation(shifted[:, :, :], shifted[:, :, :], ACT.Exp).then_inc(exp_done, 1)
            nc.scalar.activation(gap[:, :], gap[:, :], ACT.Exp).then_inc(exp_done, 1)

            def out(T):
                act.wait_ge(moved, T.t + 1)
                nc.scalar.copy(r["slotsT"][:, :, bass.ds(T.t * 2, 2), :].rearrange("p e b s -> p b e s"),
                               X_ps[T.par][:, 0:2 * SLOTS].rearrange("p (b e s) -> p b e s", b=2, e=E1)).then_inc(moved_out, 1)

            pipeline(act, [(out, 0)], NT)

        @block.tensor
        def _(pe):
            for k in range(2):
                pe.wait_ge(chosen_ready, k + 1)
                nc.tensor.matmul(R_ps[k][:, :, :], r["before"][:, :], chosen_bf[:, k, :, :], start=True, stop=k == 0).then_inc(ranked, 1 - k) if k == 0 else \
                    nc.tensor.matmul(R_ps[k][:, :, :], r["before"][:, :], chosen_bf[:, k, :, :], start=True, stop=False)
            nc.tensor.matmul(R_ps[1][:, :, :], r["ones"][:, :], chosen_bf[:, 0, :, :], start=False, stop=True).then_inc(ranked, 1)

            def move(T):
                pe.wait_ge(matrix, T.t + 1)
                pe.wait_ge(staged, T.t + 1)
                wait(pe, moved_out, T.t - 1)
                nc.tensor.matmul(X_ps[T.par][:, 0:2 * SLOTS], xn_now[:, T.par, :], dispatch[:, T.par, :], start=True,
                                 stop=True).then_inc(moved, 1)

            pipeline(pe, [(move, 0)], NT)


def experts0(nc, r, f):
    with ExitStack() as ctx:
        def sb(name, shape, dt=F32):
            return ctx.enter_context(nc.sbuf_tensor("f0_" + name, shape, dt))

        def ps(name, shape, dt=F32):
            return ctx.enter_context(nc.psum_tensor("f0_" + name, shape, dt))

        def sem(name):
            return ctx.enter_context(nc.semaphore("f0_" + name))

        w1 = sb("w1", [P, E0, HID0])
        w2 = sb("w2", [P, E0, NC0, D])
        b1 = sb("b1", [P, E0, NC0])
        b2 = sb("b2", [P, E0, D])
        zeros = sb("zeros", [P, D])
        counts = sb("counts", [P, E0])
        filled = sb("filled", [P, E0], I32)
        over = sb("over", [P, E0, NT])
        tiles = sb("tiles", [P, E0])
        ends = sb("ends", [P, E0])
        ends_of = sb("ends_of", [P, E0, E0])
        passed = sb("passed", [P, MAX_TILES, E0])
        behind = sb("behind", [P, MAX_TILES, E0])
        n_passed = sb("n_passed", [P, MAX_TILES])
        n_behind = sb("n_behind", [P, MAX_TILES])
        first = sb("first", [P, MAX_TILES])
        row_tab = sb("row_tab", [P, MAX_TILES], I32)
        expert_tab = sb("expert_tab", [P, MAX_TILES], I32)
        closer = sb("closer", [P, E0])
        beyond = sb("beyond", [P, NT, E0 - 1])
        moved = sb("moved", [P, NT])
        weights_in = sem("weights_in")
        table = sem("table")
        chain = sem("chain")
        zeroed = sem("zeroed")
        rows_zeroed = sem("rows_zeroed")
        rows = sb("rows", [P, 2, D])
        rowsT = sb("rowsT", [P, 2, P])
        w1_now = sb("w1_now", [P, 2, HID0])
        hid = sb("hid", [P, 2, NC0, P])
        done = sb("done", [P, 2, D])
        T_ps = [ps(f"T_ps{n}", [P, 512]) for n in range(2)]
        H_ps = [ps(f"H_ps{n}", [P, NC0, P]) for n in range(2)]
        Y_ps = [ps(f"Y_ps{n}", [P, 512]) for n in range(2)]
        rows_in = [sem("rows_in0"), sem("rows_in1")]
        turned = sem("turned")
        turned_out = sem("turned_out")
        w1_ready = sem("w1_ready")
        hidden = sem("hidden")
        biased = sem("biased")
        gelu_done = sem("gelu_done")
        y_ready = sem("y_ready")
        y_out = sem("y_out")
        stored = [sem("stored0"), sem("stored1")]
        vec, pool, act, pe, sp = nc.vector, nc.gpsimd, nc.scalar, nc.tensor, nc.sync
        block = ctx.enter_context(nc.Block())

        @block.vector
        def _(dve):
            step = Chain(dve, chain, 0, 20)
            vec.memset(zeros[:, :], 0.0).then_inc(zeroed, 1)
            step(vec.tensor_copy(filled[:, :], r["start"][:, :]))
            step(vec.tensor_tensor(counts[:, :], r["start"][:, :], r["region"][:, :], ALU.subtract))
            step(vec.tensor_tensor(over[:, :, :], counts[:, :].unsqueeze(2).to_broadcast([P, E0, NT]),
                                   r["edges"][:, :].unsqueeze(1).to_broadcast([P, E0, NT]), ALU.is_gt))
            step(vec.tensor_reduce(tiles[:, :], over[:, :, :], X, ALU.add))
            step(vec.tensor_tensor(ends_of[:, :, :], tiles[:, :].unsqueeze(1).to_broadcast([P, E0, E0]),
                                   r["upto"][:, :].rearrange("p (a b) -> p a b", a=E0), ALU.mult))
            step(vec.tensor_reduce(ends[:, :], ends_of[:, :, :], X, ALU.add))
            step(vec.tensor_tensor(passed[:, :, :], r["tile_no"][:, :].unsqueeze(2).to_broadcast([P, MAX_TILES, E0]),
                                   ends[:, :].unsqueeze(1).to_broadcast([P, MAX_TILES, E0]), ALU.is_ge))
            step(vec.tensor_tensor(behind[:, :, :], passed[:, :, :],
                                   tiles[:, :].unsqueeze(1).to_broadcast([P, MAX_TILES, E0]), ALU.mult))
            step(vec.tensor_reduce(n_passed[:, :], passed[:, :, :], X, ALU.add))
            step(vec.tensor_reduce(n_behind[:, :], behind[:, :, :], X, ALU.add))
            step(vec.tensor_tensor(first[:, :], r["tile_no"][:, :], n_behind[:, :], ALU.subtract))
            step(vec.tensor_scalar(first[:, :], first[:, :], float(P), None, ALU.mult))
            step(vec.scalar_tensor_tensor(first[:, :], n_passed[:, :], float(REGION), first[:, :], ALU.mult, ALU.add))
            step(vec.tensor_copy(row_tab[:, :], first[:, :]))
            step(vec.tensor_scalar(expert_tab[:, :], n_passed[:, :], float(E0 - 1), None, ALU.min))
            step(vec.tensor_scalar(closer[:, :], tiles[:, :], float(P), -float(REGION), ALU.mult, ALU.add))
            step(vec.tensor_tensor(beyond[:, :, :], r["row_all"][:, :].unsqueeze(2).to_broadcast([P, NT, E0 - 1]),
                                   r["region"][:, 1:E0].unsqueeze(1).to_broadcast([P, NT, E0 - 1]), ALU.is_ge))
            step(vec.tensor_tensor(beyond[:, :, :], beyond[:, :, :],
                                   closer[:, 0:E0 - 1].unsqueeze(1).to_broadcast([P, NT, E0 - 1]), ALU.mult))
            step(vec.tensor_reduce(moved[:, :], beyond[:, :, :], X, ALU.add))
            vec.tensor_tensor(r["row_all"][:, :], r["row_all"][:, :], moved[:, :], ALU.add).then_inc(table, 1)


            def bias(T):
                e = dve.value_load(expert_tab[0:1, bass.ds(T.t, 1)], min_val=0, max_val=E0 - 1)
                dve.wait_ge(hidden, T.t + 1)
                wait(dve, y_ready, T.t - 1)
                vec.tensor_tensor(hid[:, T.par, :, :], H_ps[T.par][:, :, :],
                                  b1[:, bass.ds(e, 1), :].rearrange("p a c -> p (a c)").unsqueeze(2).to_broadcast([P, NC0, P]),
                                  ALU.add).then_inc(biased, 1)

            def finish(T):
                e = dve.value_load(expert_tab[0:1, bass.ds(T.t, 1)], min_val=0, max_val=E0 - 1)
                dve.wait_ge(y_ready, T.t + 1)
                wait(dve, stored[T.par], T.half * 16)
                vec.tensor_tensor(done[:, T.par, :], Y_ps[T.par][:, 0:D],
                                  b2[:, bass.ds(e, 1), :].rearrange("p a c -> p (a c)"), ALU.add).then_inc(y_out, 1)

            dve.wait_ge(weights_in, 16 * 4)
            pipeline(dve, [(bias, 0), (finish, 1)], MAX_TILES)

        @block.sync
        def _(sp):
            for to, what in ((w1, f["W1"].rearrange("e d h -> d e h")), (b1, f["b1"]), (b2, f["b2"].partition_broadcast(P)),
                             (w2, f["W2"].rearrange("e (c p) d -> p e c d", p=P))):
                sp.dma_start(to[:], what).then_inc(weights_in, 16)
            sp.wait_ge(zeroed, 1)
            sp.wait_ge(table, 1)
            for e in range(E0):
                row = sp.value_load(filled[0:1, e:e + 1], min_val=0, max_val=ROWS - P)
                sp.dma_start(r["sorted"][bass.ds(row, P), :], zeros[:, :]).then_inc(rows_zeroed, 16)
            for n in range(MAX_TILES - NT):
                sp.dma_start(r["sorted"][E0 * REGION + n * P:E0 * REGION + (n + 1) * P, :], zeros[:, :]).then_inc(rows_zeroed, 16)
            sp.wait_ge(rows_zeroed, 16 * (E0 + MAX_TILES - NT))

            def load(T):
                row = sp.value_load(row_tab[0:1, bass.ds(T.t, 1)], min_val=0, max_val=ROWS - P)
                wait(sp, turned, T.t - 1)
                sp.dma_start(rows[:, T.par, :], r["sorted"][bass.ds(row, P), :]).then_inc(rows_in[T.par], 16)

            def store(T):
                sp.wait_ge(y_out, T.t + 1)
                sp.dma_start(r["expert_out"][bass.ds(T.t * P, P), :], done[:, T.par, :]).then_inc(stored[T.par], 16)

            pipeline(sp, [(load, 0), (store, 2)], MAX_TILES)
            sp.wait_ge(stored[0], 16 * ((MAX_TILES + 1) // 2))
            sp.wait_ge(stored[1], 16 * (MAX_TILES // 2))

        @block.gpsimd
        def _(pool):
            def weights(T):
                e = pool.value_load(expert_tab[0:1, bass.ds(T.t, 1)], min_val=0, max_val=E0 - 1)
                wait(pool, hidden, T.t - 1)
                pool.tensor_copy(w1_now[:, T.par, :], w1[:, bass.ds(e, 1), :].rearrange("p a c -> p (a c)")).then_inc(w1_ready, 1)

            pool.wait_ge(table, 1)
            pool.wait_ge(weights_in, 16 * 4)
            pipeline(pool, [(weights, 0)], MAX_TILES)

        @block.scalar
        def _(act):
            def turn_out(T):
                act.wait_ge(turned, T.t + 1)
                wait(act, hidden, T.t - 1)
                nc.scalar.copy(rowsT[:, T.par, :], T_ps[T.par][:, 0:P]).then_inc(turned_out, 1)

            def gelu(T):
                act.wait_ge(biased, T.t + 1)
                nc.scalar.activation(hid[:, T.par, :, :], hid[:, T.par, :, :], ACT.Gelu).then_inc(gelu_done, 1)

            pipeline(act, [(turn_out, 0), (gelu, 1)], MAX_TILES)

        @block.tensor
        def _(pe):
            def turn(T):
                pe.wait_ge(rows_in[T.par], (T.half + 1) * 16)
                wait(pe, turned_out, T.t - 1)
                nc.tensor.transpose(T_ps[T.par][:, 0:P], rows[:, T.par, :], r["ident"][:, :]).then_inc(turned, 1)

            def up(T):
                pe.wait_ge(turned_out, T.t + 1)
                pe.wait_ge(w1_ready, T.t + 1)
                wait(pe, biased, T.t - 1)
                for n in range(NC0):
                    last = nc.tensor.matmul(H_ps[T.par][:, n, :], w1_now[:, T.par, n * P:(n + 1) * P], rowsT[:, T.par, :],
                                            start=True, stop=True)
                last.then_inc(hidden, 1)

            def down(T):
                e = pe.value_load(expert_tab[0:1, bass.ds(T.t, 1)], min_val=0, max_val=E0 - 1)
                pe.wait_ge(gelu_done, T.t + 1)
                wait(pe, y_out, T.t - 1)
                for n in range(NC0):
                    last = nc.tensor.matmul(Y_ps[T.par][:, 0:D], hid[:, T.par, n, :],
                                            w2[:, bass.ds(e, 1), n, :].rearrange("p a c -> p (a c)"),
                                            start=n == 0, stop=n == NC0 - 1)
                last.then_inc(y_ready, 1)

            pe.wait_ge(table, 1)
            pe.wait_ge(weights_in, 16 * 4)
            pipeline(pe, [(turn, 0), (up, 0), (down, 1)], MAX_TILES)


def experts1(nc, r, f, outT):
    N = B * CAP
    with ExitStack() as ctx:
        def sb(name, shape, dt=F32):
            return ctx.enter_context(nc.sbuf_tensor("f1_" + name, shape, dt))

        def sem(name):
            return ctx.enter_context(nc.semaphore("f1_" + name))

        gate = sb("gate", [P, E1, HID1])
        fc = sb("fc", [P, E1, HID1])
        proj = sb("proj", [P, E1, D])
        silu = sb("silu", [P, 2, N])
        hid = sb("hid", [P, 2, N])
        G_ps = [ctx.enter_context(nc.psum_tensor(f"f1_G_ps{n}", [P, N], F32)) for n in range(2)]
        F_ps = [ctx.enter_context(nc.psum_tensor(f"f1_F_ps{n}", [P, N], F32)) for n in range(2)]
        O_ps = [ctx.enter_context(nc.psum_tensor(f"f1_O_ps{n}", [P, N], F32)) for n in range(2)]
        weights_in = sem("weights_in")
        zeroed = sem("zeroed")
        up = sem("up")
        silu_done = sem("silu_done")
        hid_ready = sem("hid_ready")
        down = sem("down")
        out_done = sem("out_done")
        block = ctx.enter_context(nc.Block())
        PAIRS = E1 // 2

        @block.sync
        def _(sp):
            sp.dma_start(gate[:, :, :], f["w_gate"].rearrange("e d h -> d e h")).then_inc(weights_in, 16)
            sp.dma_start(fc[:, :, :], f["w_fc"].rearrange("e d h -> d e h")).then_inc(weights_in, 16)
            sp.wait_ge(zeroed, 1)
            for half in range(2):
                sp.dma_start(proj[half * HID1:(half + 1) * HID1, half:E1:2, :],
                             f["w_proj"].rearrange("(a two) h d -> two h a d", two=2)[half]).then_inc(weights_in, 16)

        @block.vector
        def _(dve):
            nc.vector.memset(proj[:, :, :], 0.0).then_inc(zeroed, 1)
            for q in range(PAIRS):
                dve.wait_ge(silu_done, q + 1)
                wait(dve, down, 2 * (q - 1))
                nc.vector.tensor_tensor(hid[:, q % 2, :], F_ps[q % 2][:, :], silu[:, q % 2, :], ALU.mult).then_inc(hid_ready, 1)

        @block.scalar
        def _(act):
            def out(e):
                act.wait_ge(down, e + 1)
                nc.scalar.copy(outT[:, :, e, :], O_ps[e % 2][:, :].rearrange("p (b s) -> p b s", s=CAP)).then_inc(out_done, 1)

            for q in range(PAIRS + 1):
                if q < PAIRS:
                    act.wait_ge(up, q + 1)
                    wait(act, hid_ready, q - 1)
                    nc.scalar.activation(silu[:, q % 2, :], G_ps[q % 2][:, :], ACT.Silu).then_inc(silu_done, 1)
                if q > 0:
                    out(2 * q - 2)
                    out(2 * q - 1)

        @block.tensor
        def _(pe):
            pe.wait_ge(weights_in, 64)
            for q in range(PAIRS + 1):
                if q < PAIRS:
                    wait(pe, hid_ready, q - 1)
                    for w, to in ((gate, G_ps), (fc, F_ps)):
                        for half in range(2):
                            last = nc.tensor.matmul(to[q % 2][half * HID1:(half + 1) * HID1, :], w[:, 2 * q + half, :],
                                                    r["slotsT"][:, 2 * q + half, :, :].rearrange("p b s -> p (b s)"), start=True, stop=True,
                                                    skip_group_check=True)
                    last.then_inc(up, 1)
                if q > 0:
                    pe.wait_ge(hid_ready, q)
                    for e in (2 * q - 2, 2 * q - 1):
                        wait(pe, out_done, e - 1)
                        nc.tensor.matmul(O_ps[e % 2][:, :], proj[:, e, :], hid[:, (q - 1) % 2, :], start=True,
                                         stop=True).then_inc(down, 1)


def collect(nc, r, tg, x_all, outT, out):
    with ExitStack() as ctx:
        def sb(name, shape, dt=F32):
            return ctx.enter_context(nc.sbuf_tensor("c_" + name, shape, dt))

        def sem(name):
            return ctx.enter_context(nc.semaphore("c_" + name))

        slots_now = sb("slots_now", [P, 2, 2 * SLOTS])
        one = sb("one", [P, 2, 2, 2 * SLOTS])
        combine = sb("combine", [P, 2, 2 * SLOTS])
        combine_now = sb("combine_now", [P, 2, 2, P])
        c_chain = sem("c_chain")
        matrix = sem("matrix")
        slots = sb("slots", [P, 2, 2, D])
        final = sb("final", [P, 2, D])
        T_ps = [ctx.enter_context(nc.psum_tensor(f"c_T_ps{n}", [P, 512], F32)) for n in range(2)]
        Y_ps = [ctx.enter_context(nc.psum_tensor(f"c_Y_ps{n}", [P, 512], F32)) for n in range(2)]
        staged = sem("staged")
        turned = sem("turned")
        turned_out = sem("turned_out")
        y_ready = sem("y_ready")
        y_out = sem("y_out")
        stored = [sem("stored0"), sem("stored1")]
        block = ctx.enter_context(nc.Block())

        @block.gpsimd
        def _(pool):
            def stage(T):
                wait(pool, turned, T.t - 1)
                nc.gpsimd.tensor_copy(slots_now[:, T.par, :], outT[:, bass.ds(2 * T.t, 2), :, :].rearrange("p b e s -> p (b e s)")).then_inc(staged, 1)

            pipeline(pool, [(stage, 0)], NT)

        @block.scalar
        def _(act):
            def turn_out(T):
                act.wait_ge(turned, T.t + 1)
                wait(act, y_ready, T.t - 1)
                nc.scalar.copy(slots[:, T.par, :, :].rearrange("p b k -> p (b k)"), T_ps[T.par][:, 0:256])
                nc.scalar.copy(combine_now[:, T.par, :, :].rearrange("p b k -> p (b k)"), T_ps[T.par][:, 256:512]).then_inc(turned_out, 1)

            pipeline(act, [(turn_out, 0)], NT)

        @block.tensor
        def _(pe):
            def turn(T):
                pe.wait_ge(staged, T.t + 1)
                wait(pe, turned_out, T.t - 1)
                pe.wait_ge(matrix, T.t + 1)
                for b in range(2):
                    nc.tensor.transpose(T_ps[T.par][:, b * P:(b + 1) * P], slots_now[:, T.par, b * P:(b + 1) * P],
                                        r["ident"][:, :])
                    last = nc.tensor.transpose(T_ps[T.par][:, (2 + b) * P:(3 + b) * P], combine[:, T.par, b * P:(b + 1) * P],
                                               r["ident"][:, :])
                last.then_inc(turned, 1)

            def weigh(T):
                pe.wait_ge(turned_out, T.t + 1)
                wait(pe, y_out, T.t - 1)
                for b in range(2):
                    last = nc.tensor.matmul(Y_ps[T.par][:, 0:D], combine_now[:, T.par, b, :], slots[:, T.par, b, :],
                                            start=b == 0, stop=b == 1)
                last.then_inc(y_ready, 1)

            pipeline(pe, [(turn, 0), (weigh, 1)], NT)

        @block.vector
        def _(dve):
            def divide(T):
                dve.wait_ge(av_ready, T.t + 1)
                nc.vector.reciprocal(rden[:, :, :], O_ps[:, 1, :, :]).then_inc(rden_ready, 1)
                dve.wait_ge(rden_ready, T.t + 1)
                wait(dve, y_ready, T.t)
                nc.vector.tensor_tensor(avT[:, :, :], O_ps[:, 0, :, :], rden[:, :, :], ALU.mult).then_inc(divided, 1)

            def add(T):
                dve.wait_ge(y_ready, T.t + 1)
                wait(dve, stored[T.par], T.half * 16)
                nc.vector.scalar_tensor_tensor(final[:, T.par, :], Y_ps[T.par][:, 0:D], tg[:, 3:4],
                                               x_all[:, bass.ds(T.t * D, D)], ALU.mult, ALU.add).then_inc(y_out, 1)

            def matrices(T):
                step = Chain(dve, c_chain, T.t, 2)
                wait(dve, turned, T.t - 1)
                for k in range(2):
                    step(nc.vector.tensor_scalar(one[:, T.par, k, :], r["iota"][:, :], r["slot"][:, k, bass.ds(T.t, 1)],
                                                 r["prob"][:, k, bass.ds(T.t, 1)], ALU.is_equal, ALU.mult))
                nc.vector.tensor_tensor(combine[:, T.par, :], one[:, T.par, 0, :], one[:, T.par, 1, :], ALU.add).then_inc(matrix, 1)

            pipeline(dve, [(matrices, 0), (add, 2)], NT)

        @block.sync
        def _(sp):
            def store(T):
                sp.wait_ge(y_out, T.t + 1)
                sp.dma_start(out[bass.ds(T.t * P, P), :], final[:, T.par, :]).then_inc(stored[T.par], 16)

            pipeline(sp, [(store, 0)], NT)
            for s in stored:
                sp.wait_ge(s, 16 * NT // 2)


def setup(nc, ctx, d, tg, w0, w1):
    with ExitStack() as own:
        def sem(name):
            return own.enter_context(nc.semaphore(name))

        gates = own.enter_context(nc.sbuf_tensor("gates", [P, 4], F32))
        gates_in = sem("gates_in")
        loaded = sem("weights_in")
        tanh_done = sem("tanh_done")
        wo_zeroed = sem("wo_zeroed")
        casts = sem("casts")
        block = own.enter_context(nc.Block())
        loads = []
        for w, q in ((w0, "L0"), (w1, "L1")):
            loads += [(w["wq"][:, :], d[q + "wq"]), (w["wk"][:, :], d[q + "wk"]), (w["wv"][:, :], d[q + "wv"]),
                      (w["bq"][:, :], d[q + "bq"]), (w["bk"][:, :], d[q + "bk"]),
                      (w["bv"][:, :], d[q + "bv"].partition_broadcast(P)), (w["bo"][:, :], d[q + "bo"].partition_broadcast(P))]
            for j in range(4):
                loads.append((w["wo"][32 * j:32 * j + 16, :, :],
                              d[q + "wo"].rearrange("(g j r) o -> j r g o", g=2, j=4)[j]))
        loads += [(w0["ident"][:, :], d["ident"]), (w0["head_rows"][:, :], d["head_rows"]), (w0["ones_blk"][:, :], d["ones_blk"])]
        loads += d["more_loads"]

        @block.sync
        def _(sp):
            sp.dma_start(gates[:, 0:2], d["g_xattn"].partition_broadcast(P)).then_inc(gates_in, 16)
            sp.dma_start(gates[:, 2:4], d["g_ffn"].partition_broadcast(P)).then_inc(gates_in, 16)
            sp.wait_ge(wo_zeroed, 2)
            for to, what in loads:
                sp.dma_start(to, what).then_inc(loaded, 16)

        @block.scalar
        def _(act):
            act.wait_ge(gates_in, 32)
            nc.scalar.activation(tg[:, :], gates[:, :], ACT.Tanh).then_inc(tanh_done, 1)

        @block.vector
        def _(dve):
            nc.vector.memset(w0["wo"][:, :, :], 0.0).then_inc(wo_zeroed, 1)
            nc.vector.memset(w1["wo"][:, :, :], 0.0).then_inc(wo_zeroed, 1)
            nc.vector.memset(w0["minus_half"][:, :], -0.5)
            nc.vector.memset(d["ones_bf"][:, :], 1.0)
            dve.wait_ge(loaded, 16 * len(loads))
            dve.wait_ge(tanh_done, 1)
            for n, w in enumerate((w0, w1)):
                nc.vector.tensor_scalar(w["wo"][:, :, :], w["wo"][:, :, :], tg[:, n:n + 1], None, ALU.mult)
                nc.vector.tensor_scalar(w["bo"][:, :], w["bo"][:, :], tg[:, n:n + 1], None, ALU.mult)
            for to, what in d["casts"]:
                nc.vector.tensor_copy(to, what)


def program(nc, d, out):
    with ExitStack() as ctx:
        def sb(name, shape, dt=F32):
            return ctx.enter_context(nc.sbuf_tensor(name, shape, dt))

        x_all = sb("x_all", [P, NT * D])
        tg = sb("tg", [P, 4])
        w0, w1 = {}, {}
        for q, w in (("L0", w0), ("L1", w1)):
            for name, shape in (("wq", [P, D]), ("wk", [P, D]), ("wv", [P, D]), ("wo", [P, 2, D]),
                                ("bq", [P, 1]), ("bk", [P, 1]), ("bv", [P, D]), ("bo", [P, D])):
                w[name] = sb(q + name, shape)
        for name, shape, dt in (("ident", [P, P], F32), ("head_rows", [P, H], F32), ("ones_blk", [P, 32], F32),
                                ("minus_half", [P, 1], F32), ("ident_bf", [P, P], BF16)):
            w0[name] = w1[name] = sb(name, shape, dt)
        r0, r1 = {}, {}
        for name, shape, dt in (("before0", [P, P], F32), ("before1", [P, P], F32), ("ones1", [P, P], F32), ("iota", [P, 2 * SLOTS], F32), ("from_last", [P, E1], F32),
                                ("batch_slot", [P, 1], F32), ("router0", [P, E0], F32), ("router1", [P, E1], F32),
                                ("start", [P, E0], F32), ("region", [P, E0], F32), ("edges", [P, NT], F32),
                                ("upto", [P, E0 * E0], F32), ("tile_no", [P, MAX_TILES], F32),
                                ("before0_bf", [P, P], BF16), ("before1_bf", [P, P], BF16), ("ones1_bf", [P, P], BF16),
                                ("ones_bf", [P, P], BF16), ("row_all", [P, NT], F32)):
            r0[name] = sb(name, shape, dt)
        r0.update(w0)
        r1 = dict(r0)
        r0.update(before=r0["before0_bf"], ones=r0["ones_bf"], router=r0["router0"])
        r1.update(before=r0["before1_bf"], ones=r0["ones1_bf"], router=r0["router1"])
        r0["sorted"] = nc.dram_tensor("sorted_rows", (ROWS, D), F32, kind="Internal").ap()
        r0["expert_out"] = nc.dram_tensor("expert_out", (MAX_TILES * P, D), F32, kind="Internal").ap()
        d["more_loads"] = [(r0[n][:, :], d[n]) for n in ("before0", "before1", "ones1", "batch_slot", "router0", "router1")]
        d["more_loads"] += [(r0[n][:, :], d[n].partition_broadcast(P)) for n in ("iota", "from_last", "start", "region", "edges", "upto", "tile_no")]
        d["casts"] = [(w0["ident_bf"][:, :], w0["ident"][:, :]), (r0["before0_bf"][:, :], r0["before0"][:, :]),
                      (r0["before1_bf"][:, :], r0["before1"][:, :]), (r0["ones1_bf"][:, :], r0["ones1"][:, :])]
        d["ones_bf"] = r0["ones_bf"]
        setup(nc, ctx, d, tg, w0, w1)
        attention(nc, 0, x_all, w0, d, lambda env: router(nc, env, 0, r0))
        experts0(nc, r0, d)
        for name in ("slot", "sent", "prob"):
            r1[name] = sb(name, [P, 2, NT])
        r1["logits"] = sb("logits1", [P, NT, E1])
        with ExitStack() as own:
            r1["slotsT"] = own.enter_context(nc.sbuf_tensor("slotsT", [P, E1, B, CAP], F32))

            def hooks(env):
                h = router(nc, env, 1, r1)
                fetched = [env["sem"]("fetched0"), env["sem"]("fetched1")]
                row_now = env["sem"]("row_now_ready")
                added = env["sem"]("ffn_added")
                row = env["sb"]("row_now", [P, 2], I32)
                back = env["sb"]("back", [P, 2, D])

                def fetch(T):
                    wait(nc.gpsimd, added, T.t - 1)
                    nc.gpsimd.tensor_copy(row[:, T.par:T.par + 1], r0["row_all"][:, bass.ds(T.t, 1)]).then_inc(row_now, 1)
                    nc.gpsimd.wait_ge(row_now, T.t + 1)
                    apart(nc.gpsimd)
                    nc.gpsimd.indirect_dma_start(back[:, T.par, :], None, r0["expert_out"],
                                                 bass.IndirectOffsetOnAxis(ap=row[:, T.par:T.par + 1], axis=0)).then_inc(fetched[T.par], 16)

                def before_norm(dve, T):
                    xt = x_all[:, bass.ds(T.t * D, D)]
                    dve.wait_ge(fetched[T.par], (T.half + 1) * 16)
                    nc.vector.scalar_tensor_tensor(xt, back[:, T.par, :], tg[:, 2:3], xt, ALU.mult, ALU.add).then_inc(added, 1)
                    dve.wait_ge(added, T.t + 1)
                    apart(dve)

                h["pool_first"] = [(fetch, -2)]
                h["before_norm"] = before_norm
                return h

            with ExitStack() as kept:
                r1["xn"] = kept.enter_context(nc.sbuf_tensor("xn_all", [P, NT * D], F32))
                attention(nc, 1, x_all, w1, d, hooks)
                assign1(nc, r1)
            outT = own.enter_context(nc.sbuf_tensor("outT", [P, B, E1, CAP], F32))
            experts1(nc, r1, d, outT)
            collect(nc, r1, tg, x_all, outT, out)


def kernel(**inputs):
    import numpy as np
    import concourse.bacc as bacc
    from concourse import mybir as my
    from concourse.bass_utils import run_bass_kernel_spmd as run

    nc = bacc.Bacc("TRN2", target_bir_lowering=False, num_devices=1)
    i = {k: np.asarray(v) for k, v in inputs.items()}
    T = B * S
    arrays = {
        "x": i["x"].reshape(T, D), "ctx": i["ctx_1024"].reshape(T, D), "mask": i["mask_BxSxS2_ik1"].reshape(T, S),
        "g_xattn": i["g_xattn"], "g_ffn": i["g_ffn"],
        "L0wq": i["L0_xattn_w_q"].T, "L0wk": i["L0_xattn_w_k"].T, "L0wv": i["L0_xattn_w_v"].T, "L0wo": i["L0_xattn_w_o"].T,
        "L0bq": i["L0_xattn_b_q"].reshape(D, 1), "L0bk": i["L0_xattn_b_k"].reshape(D, 1),
        "L0bv": i["L0_xattn_b_v"], "L0bo": i["L0_xattn_b_o"],
        "L1wo": i["L1_xattn_out_proj_weight"], "L1bo": i["L1_xattn_out_proj_bias"],
    }
    for n, name in enumerate(("q", "k", "v")):
        arrays["L1w" + name] = i["L1_xattn_in_proj_weight"][:, n * D:(n + 1) * D]
        bias = i["L1_xattn_in_proj_bias"][n * D:(n + 1) * D]
        arrays["L1b" + name] = bias if name == "v" else bias.reshape(D, 1)
    p = np.arange(P)
    arrays["ident"] = np.eye(P, dtype=np.float32)
    arrays["head_rows"] = (p[:, None] // DK == np.arange(H)[None, :]).astype(np.float32)
    col = np.arange(32)[None, :]
    arrays["ones_blk"] = ((p[:, None] // S == col // DK) | (col >= 2 * DK)).astype(np.float32)
    row, col = p[:, None], p[None, :]
    same = row // S == col // S
    arrays["before0"] = (row < col).astype(np.float32)
    arrays["before1"] = ((row < col) & same).astype(np.float32)
    arrays["ones1"] = same.astype(np.float32)
    arrays["batch_slot"] = (row // S * SLOTS + E1 * CAP).astype(np.float32)
    arrays["from_last"] = E1 - np.arange(E1, dtype=np.float32)
    arrays["iota"] = np.arange(2 * SLOTS, dtype=np.float32)
    arrays["start"] = arrays["region"] = np.arange(E0, dtype=np.float32) * REGION
    arrays["edges"] = np.arange(NT, dtype=np.float32) * P
    arrays["upto"] = np.tril(np.ones((E0, E0), np.float32)).ravel()
    arrays["tile_no"] = np.arange(MAX_TILES, dtype=np.float32)
    arrays["router0"] = i["L0_ffn_Wg"].T
    arrays["router1"] = i["L1_ffn_w_router"]
    arrays["W1"], arrays["W2"], arrays["b2"] = i["L0_ffn_W1"], i["L0_ffn_W2"], i["L0_ffn_b2"]
    arrays["b1"] = i["L0_ffn_b1"].reshape(E0, NC0, P).transpose(2, 0, 1)
    for name in ("w_fc", "w_gate", "w_proj"):
        arrays[name] = i["L1_ffn_" + name]
    arrays = {k: np.ascontiguousarray(v) for k, v in arrays.items()}
    d = {k: nc.dram_tensor(f"in_{k}", a.shape, my.dt.from_np(a.dtype), kind="ExternalInput").ap() for k, a in arrays.items()}
    out = nc.dram_tensor("out_0", (T, D), my.dt.from_np(np.dtype("float32")), kind="ExternalOutput").ap()
    program(nc, d, out)
    r = run(nc, [{f"in_{k}": a for k, a in arrays.items()}], core_ids=[0])
    return r.results[0]["out_0"].reshape(B, S, D)
```

```python
from contextlib import ExitStack

import concourse.bass as bass
from concourse import mybir

F32 = mybir.dt.float32
BF16 = mybir.dt.bfloat16
I32 = mybir.dt.int32
U32 = mybir.dt.uint32
ALU = mybir.AluOpType
ACT = mybir.ActivationFunctionType
X = mybir.AxisListType.X

B, S, D = 64, 64, 128
H, DK = 16, 8
HP = H // 2
P = 128
NT = B * S // P
E0, HID0 = 8, 512
NC0 = HID0 // P
REGION = B * S + P
MAX_TILES = NT + E0 - 1
ROWS = E0 * REGION + (MAX_TILES - NT) * P
E1, HID1 = 16, 64
CAP = 2 * S // E1
SLOTS = E1 * CAP
EPS = 1e-5
SCALE = DK ** -0.5
MASKED = -1e9
ALL_MASKED = -2.0 ** 100


class Tile:

    def __init__(self, t, par, half):
        self.t, self.par, self.half = t, par, half


def number(t):
    return Tile(t, t % 2, t // 2)


def pipeline(eng, steps, count):
    most = max(skew for _, skew in steps)
    least = min(0, min(skew for _, skew in steps))
    first = most + 2 + most % 2
    last = count + least
    last -= (last - first) % 2

    def alone(n):
        for step, skew in steps:
            if 0 <= n - skew < count:
                step(number(n - skew))

    for n in range(least, first):
        alone(n)
    with eng.Fori(0, (last - first) // 2) as i:
        for u in range(2):
            for step, skew in steps:
                c = first + u - skew
                step(Tile(i * 2 + c, c % 2, i + c // 2))
    for n in range(last, count + most):
        alone(n)


def wait(eng, sem, value):
    if not (isinstance(value, int) and value <= 0):
        eng.wait_ge(sem, value)


def apart(eng):
    eng.nop(nofuse=True)


class Chain:

    def __init__(self, eng, sem, t, n):
        self.eng, self.sem, self.base, self.n, self.k = eng, sem, t * n, n, 0

    def __call__(self, ins, alone=False):
        self.k += 1
        assert self.k <= self.n
        ins.then_inc(self.sem, 1)
        self.eng.wait_ge(self.sem, self.base + self.k)
        if alone:
            apart(self.eng)


def attention(nc, layer, x_all, w, dram, hooks):
    with ExitStack() as ctx:
        def sb(name, shape, dt=F32):
            return ctx.enter_context(nc.sbuf_tensor(f"{name}_{layer}", shape, dt))

        def ps(name, shape, dt=F32):
            return ctx.enter_context(nc.psum_tensor(f"{name}_{layer}", shape, dt))

        def sem(name):
            return ctx.enter_context(nc.semaphore(f"{name}_{layer}"))

        masked = layer == 0
        ctx_in = sb("ctx_in", [P, 2, D])
        mask_in = sb("mask_in", [P, 2, S], I32)
        mask_zero = sb("mask_zero", [P, 2, S])
        mask_all = sb("mask_all", [P, 2, 2])
        mask_bias = sb("mask_bias", [P, 2, S], BF16)
        stats = sb("stats", [P, 6])
        mv = sb("mv", [P, 2, 2])
        rstd = sb("rstd", [P, 2])
        xn = sb("xn", [P, 2, D])
        xnT = sb("xnT", [P, 2, P])
        ctxT = sb("ctxT", [P, 2, 2, 2, S])
        qT = sb("qT", [P, 2, P])
        kT = sb("kT", [P, 2, P])
        k_blk = sb("k_blk", [P, 2, 2, H, S])
        v_blk = sb("v_blk", [P, 2, 2, 2, 16 + 4 * 32])
        prob = sb("prob", [P, 2, H, S])
        probT = sb("probT", [P, HP, P])
        rden = sb("rden", [P, P])
        avT = sb("avT", [P, P])
        x_bo = sb("x_bo", [P, 2, D])
        maxes = sb("maxes", [P, 2, H])

        S_ps = [ps("S_ps0", [P, HP, S]), ps("S_ps1", [P, HP, S])]
        T_ps = [ps("T_ps0", [P, 4, P]), ps("T_ps1", [P, 4, P])]
        A_ps = ps("A_ps", [P, 4, P])
        O_ps = ps("O_ps", [P, 2, P])
        Y_ps = ps("Y_ps", [P, 512])
        V_ps = Y_ps[:, 256:512].rearrange("p (b a r d) -> p b a r d", b=2, a=HP, r=2)
        R_ps = ps("R_ps", [P, 512])

        loaded = [sem("loaded0"), sem("loaded1")]
        x_ready = sem("x_ready")
        mask_biased = sem("mask_biased")
        ln_stats = sem("ln_stats")
        ln_rstd = sem("ln_rstd")
        xn_ready = sem("xn_ready")
        xo_ready = sem("xo_ready")
        turned = sem("turned")
        turned_out = sem("turned_out")
        qk_ready = sem("qk_ready")
        qk_out = sem("qk_out")
        v_ready = sem("v_ready")
        v_out = sem("v_out")
        kblk_ready = sem("kblk_ready")
        scored = sem("scored")
        shifted = sem("shifted")
        exp_ready = sem("exp_ready")
        probs_turned = sem("probs_turned")
        probT_ready = sem("probT_ready")
        av_ready = sem("av_ready")
        rden_ready = sem("rden_ready")
        divided = sem("divided")
        y_ready = sem("y_ready")
        y_out = sem("y_out")
        bn_done = sem("bn_done")
        eps_added = sem("eps_added")
        m_chain = sem("m_chain")
        b_chain = sem("b_chain")
        zeroed = sem("zeroed")

        block = ctx.enter_context(nc.Block())
        env = dict(ctx=ctx, sb=sb, ps=ps, sem=sem, x_all=x_all, R_ps=R_ps, y_ready=y_ready, y_out=y_out, x_ready=x_ready)
        hook = hooks(env)
        LOADS = 48 if masked else 16

        @block.sync
        def _(sp):
            def load(T):
                wait(sp, turned, T.t - 1)
                sp.dma_start(ctx_in[:, T.par, :], dram["ctx"][bass.ds(T.t * P, P), :]).then_inc(loaded[T.par], 16)
                if masked:
                    wait(sp, mask_biased, T.t - 1)
                    sp.dma_start(x_all[:, bass.ds(T.t * D, D)], dram["x"][bass.ds(T.t * P, P), :]).then_inc(loaded[T.par], 16)
                    sp.dma_start(mask_in[:, T.par, :], dram["mask"][bass.ds(T.t * P, P), :]).then_inc(loaded[T.par], 16)

                if isinstance(T.t, int) and T.t == 1:
                    for to, what, done in hook["experts"]:
                        sp.dma_start(to, what).then_inc(done, 16)

            pipeline(sp, [(load, 0)], NT)

        @block.gpsimd
        def _(pool):
            nc.gpsimd.memset(v_blk[:, :, :, :, :], 0.0).then_inc(zeroed, 1)

            def std(T):
                pool.wait_ge(ln_stats, T.t + 1)
                nc.gpsimd.tensor_tensor(mv[:, T.par, 1:2], mv[:, T.par, 1:2], w["eps"][:, 0:1], ALU.add).then_inc(eps_added, 1)
                pool.wait_ge(eps_added, T.t + 1)
                nc.gpsimd.tensor_tensor(rstd[:, T.par:T.par + 1], mv[:, T.par, 1:2], w["minus_half"][:, 0:1],
                                        ALU.pow).then_inc(ln_rstd, 1)

            def residual(T):
                pool.wait_ge(xn_ready, T.t + 1)
                wait(pool, y_out, T.t - 1)
                nc.gpsimd.tensor_tensor(x_bo[:, T.par, :], x_all[:, bass.ds(T.t * D, D)], w["bo"][:, :],
                                        ALU.add).then_inc(xo_ready, 1)

            def blocks(T):
                pool.wait_ge(qk_out, 2 * T.t + 2)
                wait(pool, scored, 2 * T.t - 2)
                for b in range(2):
                    last = nc.gpsimd.tensor_tensor(
                        k_blk[:, T.par, b, :, :],
                        kT[:, T.par, b * S:(b + 1) * S].unsqueeze(1).to_broadcast([P, H, S]),
                        w["head_rows"][:, :].unsqueeze(2).to_broadcast([P, H, S]), ALU.mult)
                last.then_inc(kblk_ready, 1)

            pipeline(pool, hook["pool_first"] + [(residual, 3)] + hook["pool"] + [(std, -1), (blocks, 0)], NT)
            hook["pool_end"](pool)

        @block.scalar
        def _(act):
            def turn_out(T):
                act.wait_ge(turned, T.t + 1)
                wait(act, qk_ready, T.t - 1)
                wait(act, v_ready, T.t - 1)
                nc.scalar.copy(ctxT[:, T.par, :, :, :], A_ps[:, 1, :].rearrange("p (b k) -> p b k", b=2)
                               .unsqueeze(2).to_broadcast([P, 2, 2, S])).then_inc(turned_out, 1)
                nc.scalar.copy(xnT[:, T.par, :], A_ps[:, 0, :]).then_inc(turned_out, 1)

            def values(T):
                act.wait_ge(v_ready, T.t + 1)
                if isinstance(T.t, int) and T.t == 0:
                    act.wait_ge(zeroed, 1)
                wait(act, av_ready, T.t - 1)
                for r in range(2):
                    half = slice(r * S, (r + 1) * S)
                    last = nc.scalar.copy(
                        v_blk[half, T.par, :, :, 16:].rearrange("p b g (j w) -> p (b g) j w", w=32)[:, :, :, r * DK:(r + 1) * DK],
                        V_ps[half, :, :, r, :].rearrange("p b (g j) d -> p (b g) j d", g=2))
                last.then_inc(v_out, 1)

            def qk(T):
                act.wait_ge(qk_ready, T.t + 1)
                wait(act, scored, 2 * T.t - 2)
                nc.scalar.activation(qT[:, T.par, :], A_ps[:, 2, :], ACT.Identity, bias=w["bq"][:, 0:1]).then_inc(qk_out, 1)
                nc.scalar.activation(kT[:, T.par, :], A_ps[:, 3, :], ACT.Identity, bias=w["bk"][:, 0:1]).then_inc(qk_out, 1)

            def exps(T):
                for g in range(2):
                    act.wait_ge(shifted, 2 * T.t + g + 1)
                    part = prob[:, T.par, g * HP:(g + 1) * HP, :]
                    nc.scalar.activation(part, part, ACT.Exp, scale=SCALE).then_inc(exp_ready, 1)

            def probs_out(T):
                for g in range(2):
                    act.wait_ge(probs_turned, 2 * T.t + g + 1)
                    wait(act, av_ready, T.t)
                    nc.scalar.copy(probT[:, 4 * g:4 * g + 4, :], T_ps[g][:, :, :]).then_inc(probT_ready, 1)

            pipeline(act, [(turn_out, 0)] + hook["act"] + [(probs_out, 3), (exps, 2), (qk, 0), (values, 1)], NT)

        @block.vector
        def _(dve):
            def stat(T):
                if masked:
                    dve.wait_ge(loaded[T.par], (T.half + 1) * LOADS)
                else:
                    hook["before_norm"](dve, T)
                nc.vector.bn_stats(stats[:, :], x_all[:, bass.ds(T.t * D, D)]).then_inc(bn_done, 1)
                if masked:
                    nc.vector.tensor_scalar(mask_zero[:, T.par, :], mask_in[:, T.par, :], 0.0, None,
                                            ALU.is_equal).then_inc(m_chain, 1)
                dve.wait_ge(bn_done, T.t + 1)
                apart(dve)
                nc.vector.bn_aggr(mv[:, T.par, :], stats[:, :]).then_inc(ln_stats, 1)
                if masked:
                    dve.wait_ge(m_chain, 3 * T.t + 1)
                    nc.vector.tensor_reduce(mask_all[:, T.par, 0:1], mask_zero[:, T.par, :], X, ALU.min).then_inc(m_chain, 1)
                    dve.wait_ge(m_chain, 3 * T.t + 2)
                    nc.vector.tensor_scalar(mask_all[:, T.par, 1:2], mask_all[:, T.par, 0:1], ALL_MASKED, MASKED,
                                            ALU.mult, ALU.add).then_inc(m_chain, 1)

            def norm(T):
                dve.wait_ge(ln_rstd, T.t + 1)
                wait(dve, turned, T.t - 1)
                nc.vector.tensor_scalar(xn[:, T.par, :], x_all[:, bass.ds(T.t * D, D)], mv[:, T.par, 0:1],
                                        rstd[:, T.par:T.par + 1], ALU.subtract, ALU.mult).then_inc(xn_ready, 1)

            def mask(T):
                dve.wait_ge(m_chain, 3 * T.t + 3)
                wait(dve, scored, 2 * T.t - 2)
                nc.vector.tensor_scalar(mask_bias[:, T.par, :], mask_zero[:, T.par, :], mask_all[:, T.par, 1:2], None,
                                        ALU.mult).then_inc(mask_biased, 1)

            def softmax(T):
                step = Chain(dve, b_chain, T.t, 2)
                for g in range(2):
                    heads = slice(g * HP, (g + 1) * HP)
                    dve.wait_ge(scored, 2 * T.t + g + 1)
                    step(nc.vector.tensor_reduce(maxes[:, T.par, heads], S_ps[g][:, :, :], X, ALU.max))
                    wait(dve, probs_turned, 2 * T.t - 2)
                    nc.vector.tensor_tensor(
                        prob[:, T.par, heads, :], S_ps[g][:, :, :],
                        maxes[:, T.par, heads].unsqueeze(2).to_broadcast([P, HP, S]), ALU.subtract).then_inc(shifted, 1)

            def divide(T):
                dve.wait_ge(av_ready, T.t + 1)
                nc.vector.reciprocal(rden[:, :], O_ps[:, 1, :]).then_inc(rden_ready, 1)
                dve.wait_ge(rden_ready, T.t + 1)
                wait(dve, y_ready, T.t)
                nc.vector.tensor_tensor(avT[:, :], O_ps[:, 0, :], rden[:, :], ALU.mult).then_inc(divided, 1)

            def add(T):
                dve.wait_ge(y_ready, T.t + 1)
                dve.wait_ge(xo_ready, T.t + 1)
                nc.vector.tensor_tensor(x_all[:, bass.ds(T.t * D, D)], Y_ps[:, 0:D], x_bo[:, T.par, :],
                                        ALU.add).then_inc(y_out, 1)

            pipeline(dve, [(divide, 4), (norm, 0)] + hook["dve_first"] + hook["dve_rows"] + [(softmax, 2), (add, 4)] + hook["dve"] + [(stat, -1)]
                     + ([(mask, 0)] if masked else []), NT)

        @block.tensor
        def _(pe):
            ident = w["ident"]

            def turn(T):
                pe.wait_ge(xn_ready, T.t + 1)
                wait(pe, qk_out, 2 * T.t)
                pe.wait_ge(loaded[T.par], (T.half + 1) * LOADS)
                nc.tensor.transpose(A_ps[:, 1, :], ctx_in[:, T.par, :], ident[:, :])
                nc.tensor.transpose(A_ps[:, 0, :], xn[:, T.par, :], ident[:, :]).then_inc(turned, 1)

            def project(T):
                pe.wait_ge(turned_out, 2 * T.t + 2)
                nc.tensor.matmul(A_ps[:, 2, :], w["wq"][:, :], xnT[:, T.par, :], start=True, stop=True)
                nc.tensor.matmul(A_ps[:, 3, :], w["wk"][:, :], ctxT[:, T.par, :, 0, :], start=True, stop=True).then_inc(qk_ready, 1)

            def project_v(T):
                wait(pe, v_out, T.t)
                wait(pe, y_out, T.t - 2)
                for b in range(2):
                    last = nc.tensor.matmul(V_ps[:, b, :, :, :].rearrange("p a r d -> p (a r d)"),
                                            ctxT[:, T.par, b, :, :].rearrange("p r k -> p (r k)"),
                                            w["wv"][:, :], start=True, stop=True)
                last.then_inc(v_ready, 1)

            def score(T):
                pe.wait_ge(kblk_ready, T.t + 1)
                if masked:
                    pe.wait_ge(mask_biased, T.t + 1)
                for g in range(2):
                    wait(pe, shifted, 2 * T.t + g - 1)
                    if masked:
                        nc.tensor.matmul(S_ps[g][:, :, :], w["ident_bf"][:, :],
                                         mask_bias[:, T.par, :].unsqueeze(1).to_broadcast([P, HP, S]),
                                         start=True, stop=False, skip_group_check=True)
                    for b in range(2):
                        last = nc.tensor.matmul(S_ps[g][b * S:(b + 1) * S, :, :], qT[:, T.par, b * S:(b + 1) * S],
                                                k_blk[:, T.par, b, g * HP:(g + 1) * HP, :],
                                                start=not masked, stop=True, skip_group_check=True)
                    last.then_inc(scored, 1)

            def turn_probs(T):
                for g in range(2):
                    pe.wait_ge(exp_ready, 2 * T.t + g + 1)
                    wait(pe, probT_ready, 2 * T.t + g - 1)
                    for j in range(4):
                        pair = prob[:, T.par, 8 * g + 2 * j:8 * g + 2 * j + 2, :].rearrange("p r k -> p (r k)")
                        last = nc.tensor.transpose(T_ps[g][:, j, :], pair, ident[:, :])
                    last.then_inc(probs_turned, 1)

            def attend(T):
                pe.wait_ge(v_out, T.t + 1)
                wait(pe, divided, T.t)
                for g in range(2):
                    pe.wait_ge(probT_ready, 2 * T.t + g + 1)
                    at = 16 * (1 - g)
                    for b in range(2):
                        for j in range(4):
                            nc.tensor.matmul(O_ps[32 * j:32 * j + 32, 0, b * S:(b + 1) * S],
                                             v_blk[:, T.par, b, g, at + 32 * j:at + 32 * j + 32],
                                             probT[:, 4 * g + j, b * S:(b + 1) * S],
                                             start=g == 0 and b == 0, stop=g == 1, skip_group_check=True)
                    for j in range(4):
                        last = nc.tensor.matmul(O_ps[32 * j:32 * j + 32, 1, :], w["ones_blk"][:, at:at + 32],
                                                probT[:, 4 * g + j, :], start=False, stop=g == 1, skip_group_check=True)
                last.then_inc(av_ready, 1)

            def output(T):
                pe.wait_ge(divided, T.t + 1)
                wait(pe, y_out, T.t)
                wait(pe, v_out, min(T.t + 3, NT) if isinstance(T.t, int) else T.t + 3)
                nc.tensor.matmul(Y_ps[:, 0:D], avT[:, :], w["wo"][:, :], start=True, stop=True).then_inc(y_ready, 1)

            pipeline(pe, hook["pe_ranks"] + [(score, 2), (turn, 0)] + hook["pe_turn"] + [(turn_probs, 3), (output, 4)] + hook["pe_logits"]
                     + [(project, 0), (attend, 3), (project_v, 1)], NT)


def router(nc, env, layer, r):
    sb, sem = env["sb"], env["sem"]
    x_all, R_ps, y_out = env["x_all"], env["R_ps"], env["y_out"]
    E = E0 if layer == 0 else E1
    stats = sb("r_stats", [P, 6])
    mv = sb("r_mv", [P, 2, 2])
    rstd = sb("r_rstd", [P, 2])
    xn = sb("r_xn", [P, 2, D])
    xnT = sb("r_xnT", [P, P])
    logits = sb("r_logits", [P, E])
    top = sb("r_top", [P, 8])
    top_at = sb("r_top_at", [P, 8], U32)
    expert = sb("r_expert", [P, 2])
    chosen = sb("r_chosen", [P, 2, E], BF16)
    product = sb("r_product", [P, E])
    place = sb("r_place", [P, E])
    rank = sb("r_rank", [P, 2])
    LOG = R_ps[:, 0:E]
    RANK = R_ps[:, 32:32 + E]
    COUNT = R_ps[:, 64:64 + E]
    XT = R_ps[:, 128:256]

    r_stats = sem("r_stats_ready")
    r_rstd = sem("r_rstd_ready")
    r_xn = sem("r_xn_ready")
    r_turned = sem("r_turned")
    r_xnT = sem("r_xnT_ready")
    r_logits = sem("r_logits_ready")
    r_chosen = sem("r_chosen_ready")
    r_ranked = sem("r_ranked")
    r_done = sem("r_done")
    r_bn_done = sem("r_bn_done")
    r_eps_added = sem("r_eps_added")
    t_chain = sem("r_t_chain")
    p_chain = sem("r_p_chain")
    h = {k: [] for k in ("experts", "pool_first", "pool", "act", "dve_first", "dve_rows", "dve", "pe_turn", "pe_logits", "pe_ranks")}
    vec, pool, act, pe = nc.vector, nc.gpsimd, nc.scalar, nc.tensor

    def stat(T):
        vec.wait_ge(y_out, T.t + 1)
        apart(vec)
        vec.bn_stats(stats[:, :], x_all[:, bass.ds(T.t * D, D)]).then_inc(r_bn_done, 1)
        vec.wait_ge(r_bn_done, T.t + 1)
        apart(vec)
        vec.bn_aggr(mv[:, T.par, :], stats[:, :]).then_inc(r_stats, 1)

    def std(T):
        pool.wait_ge(r_stats, T.t + 1)
        pool.tensor_tensor(mv[:, T.par, 1:2], mv[:, T.par, 1:2], r["eps"][:, 0:1], ALU.add).then_inc(r_eps_added, 1)
        pool.wait_ge(r_eps_added, T.t + 1)
        pool.tensor_tensor(rstd[:, T.par:T.par + 1], mv[:, T.par, 1:2], r["minus_half"][:, 0:1], ALU.pow).then_inc(r_rstd, 1)

    def norm(T):
        vec.wait_ge(r_rstd, T.t + 1)
        if layer == 0:
            wait(vec, scattered[T.par], T.half * 16)
        vec.tensor_scalar(xn[:, T.par, :], x_all[:, bass.ds(T.t * D, D)], mv[:, T.par, 0:1], rstd[:, T.par:T.par + 1],
                          ALU.subtract, ALU.mult).then_inc(r_xn, 1)

    def turn(T):
        pe.wait_ge(r_xn, T.t + 1)
        wait(pe, r_done, T.t)
        pe.transpose(XT, xn[:, T.par, :], r["ident"][:, :]).then_inc(r_turned, 1)

    def turn_out(T):
        act.wait_ge(r_turned, T.t + 1)
        act.copy(xnT[:, :], XT).then_inc(r_xnT, 1)

    def logit(T):
        pe.wait_ge(r_xnT, T.t + 1)
        pe.matmul(LOG, xnT[:, :], r["router"][:, :], start=True, stop=True).then_inc(r_logits, 1)

    h["dve_first"] = [(norm, 5)]
    h["act"] = [(turn_out, 5)]
    h["pe_turn"] = [(turn, 5)]
    h["pe_logits"] = [(logit, 5)]
    if layer == 1:
        xn_kept = sem("r_xn_kept")

        def keep(T):
            vec.wait_ge(r_logits, T.t + 1)
            vec.tensor_copy(r["logits"][:, bass.ds(T.t, 1), :].rearrange("p a e -> p (a e)"), LOG).then_inc(r_done, 1)

        def keep_xn(T):
            pool.wait_ge(r_xn, T.t + 1)
            pool.tensor_copy(r["xn"][:, bass.ds(T.t * D, D)], xn[:, T.par, :]).then_inc(xn_kept, 1)

        def norm1(T):
            wait(vec, xn_kept, T.t - 1)
            norm(T)

        h["dve_first"] = [(norm1, 5)]
        h["dve"] = [(stat, 4), (keep, 5)]
        h["pool"] = [(keep_xn, 5), (std, 4)]
        h["pool_end"] = lambda eng: None
        return h

    row = sb("r_row", [P, 2], I32)
    scattered = [sem("r_scattered0"), sem("r_scattered1")]
    row_ready = sem("r_row_ready")

    def choose(T):
        step = Chain(vec, t_chain, T.t, 4)
        vec.wait_ge(r_logits, T.t + 1)
        step(vec.tensor_copy(logits[:, :], LOG), alone=True)
        step(vec.max(top[:, :], logits[:, :]), alone=True)
        step(vec.max_index(top_at[:, :], top[:, :], logits[:, :]))
        step(vec.tensor_copy(expert[:, :], top_at[:, 0:2]))
        vec.tensor_scalar(chosen[:, 0, :], r["iota"][:, 0:E], expert[:, 0:1], None, ALU.is_equal).then_inc(r_chosen, 1)

    def ranks(T):
        pe.wait_ge(r_chosen, T.t + 1)
        pe.matmul(RANK, r["before"][:, :], chosen[:, 0, :], start=True, stop=True)
        pe.matmul(COUNT, r["ones"][:, :], chosen[:, 0, :], start=True, stop=True).then_inc(r_ranked, 1)

    def rows(T):
        step = Chain(vec, p_chain, T.t, 2)
        vec.wait_ge(r_ranked, T.t + 1)
        step(vec.tensor_tensor(place[:, :], RANK, r["start"][:, :], ALU.add))
        step(vec.tensor_tensor_reduce(product[:, :], place[:, :], chosen[:, 0, :], 1.0, 0.0, ALU.mult, ALU.add,
                                      rank[:, 0:1]))
        vec.tensor_tensor(r["start"][:, :], r["start"][:, :], COUNT, ALU.add).then_inc(r_done, 1)
        wait(vec, scattered[T.par], T.half * 16)
        vec.tensor_copy(row[:, T.par:T.par + 1], rank[:, 0:1]).then_inc(row_ready, 1)
        vec.tensor_copy(r["row_all"][:, bass.ds(T.t, 1)], rank[:, 0:1]).then_inc(row_ready, 1)

    def scatter(T):
        pool.wait_ge(row_ready, 2 * T.t + 1)
        apart(pool)
        pool.indirect_dma_start(r["sorted"], bass.IndirectOffsetOnAxis(ap=row[:, T.par:T.par + 1], axis=0),
                                xn[:, T.par, :], None).then_inc(scattered[T.par], 16)

    def end(eng):
        for s in scattered:
            eng.wait_ge(s, 16 * NT // 2)

    h["dve_first"] = [(norm, 5)]
    h["dve_rows"] = [(rows, 6)]
    h["dve"] = [(stat, 4), (choose, 5)]
    h["pe_ranks"] = [(ranks, 6)]
    h["pool"] = [(scatter, 6), (std, 4)]
    h["pool_end"] = end
    return h


def assign1(nc, r, tg):
    with ExitStack() as ctx:
        def sb(name, shape, dt=F32):
            return ctx.enter_context(nc.sbuf_tensor("a1_" + name, shape, dt))

        def sem(name):
            return ctx.enter_context(nc.semaphore("a1_" + name))

        ALL = [P, NT, E1]
        most = sb("most", [P, 2, NT])
        same = sb("same", ALL)
        level = sb("level", ALL)
        first = sb("first", [P, 2, NT])
        chosen = sb("chosen", [P, 2, NT, E1])
        chosen_bf = sb("chosen_bf", [P, 2, NT, E1], BF16)
        rest = sb("rest", ALL)
        shifted = sb("shifted", ALL)
        total = sb("total", [P, NT])
        r_total = sb("r_total", [P, NT])
        gap = sb("gap", [P, NT])
        picked = sb("picked", ALL)
        rank = sb("rank", [P, 2, NT])
        base = sb("base", [P, 2, NT])
        over = sb("over", [P, 2, NT])
        one = sb("one", [P, 2, 2 * SLOTS])
        dispatch = sb("dispatch", [P, 2, 2 * SLOTS])
        xn_now = sb("xn_now", [P, 2, D])
        R_ps = [ctx.enter_context(nc.psum_tensor(f"a1_R_ps{n}", [P, NT, E1], F32)) for n in range(2)]
        X_ps = [ctx.enter_context(nc.psum_tensor(f"a1_X_ps{n}", [P, 512], F32)) for n in range(2)]
        chain = sem("chain")
        shift_ready = sem("shift_ready")
        exp_done = sem("exp_done")
        chosen_ready = sem("chosen_ready")
        ranked = sem("ranked")
        matrix = sem("matrix")
        one_ready = sem("one_ready")
        staged = sem("staged")
        moved = sem("moved")
        moved_out = sem("moved_out")
        block = ctx.enter_context(nc.Block())
        vec = nc.vector

        @block.vector
        def _(dve):
            step = Chain(dve, chain, 0, 40)
            experts = r["iota"][:, 0:E1].unsqueeze(1).to_broadcast(ALL)

            def over_experts(ap):
                return ap.unsqueeze(2).to_broadcast(ALL)

            left = r["logits"]
            for k in range(2):
                step(vec.tensor_reduce(most[:, k, :], left[:, :, :], X, ALU.max))
                step(vec.tensor_tensor(same[:, :, :], left[:, :, :], over_experts(most[:, k, :]), ALU.is_equal))
                step(vec.tensor_tensor(level[:, :, :], same[:, :, :], r["from_last"][:, :].unsqueeze(1).to_broadcast(ALL), ALU.mult))
                step(vec.tensor_reduce(first[:, k, :], level[:, :, :], X, ALU.max))
                step(vec.tensor_tensor(chosen[:, k, :, :], level[:, :, :], over_experts(first[:, k, :]), ALU.is_equal))
                vec.tensor_copy(chosen_bf[:, k, :, :], chosen[:, k, :, :]).then_inc(chosen_ready, 1)
                if k == 0:
                    step(vec.scalar_tensor_tensor(rest[:, :, :].rearrange("p t e -> p (t e)"), chosen[:, 0, :, :].rearrange("p t e -> p (t e)"), -3e38,
                                                  left[:, :, :].rearrange("p t e -> p (t e)"), ALU.mult, ALU.add))
                    left = rest
            vec.tensor_tensor(shifted[:, :, :], r["logits"][:, :, :], over_experts(most[:, 0, :]), ALU.subtract).then_inc(shift_ready, 1)
            vec.tensor_tensor(gap[:, :], most[:, 1, :], most[:, 0, :], ALU.subtract).then_inc(shift_ready, 1)
            for k in range(2):
                dve.wait_ge(ranked, k + 1)
                step(vec.tensor_tensor(picked[:, :, :], R_ps[k][:, :, :], chosen[:, k, :, :], ALU.mult))
                step(vec.tensor_reduce(rank[:, k, :], picked[:, :, :], X, ALU.add))
            step(vec.tensor_scalar(base[:, :, :], first[:, :, :], -float(CAP), r["batch_slot"][:, 0:1], ALU.mult, ALU.add))
            step(vec.scalar_tensor_tensor(r["slot"][:, :, :], rank[:, :, :], float(CAP - 1), base[:, :, :], ALU.min, ALU.add))
            step(vec.tensor_scalar(over[:, :, :], rank[:, :, :], float(CAP), 4.0 * SLOTS, ALU.is_ge, ALU.mult))
            step(vec.tensor_tensor(r["sent"][:, :, :], over[:, :, :], r["slot"][:, :, :], ALU.add))
            dve.wait_ge(exp_done, 2)
            step(vec.tensor_reduce(total[:, :], shifted[:, :, :], X, ALU.add))
            step(vec.reciprocal(r["prob"][:, 0, :], total[:, :]))
            step(vec.tensor_scalar(r["prob"][:, 0, :], r["prob"][:, 0, :], tg[:, 3:4], None, ALU.mult))
            step(vec.tensor_copy(r["prob"][:, 1, :], gap[:, :]))

            def first_choice(T):
                wait(dve, matrix, T.t - 1)
                vec.tensor_scalar(one[:, T.par, :], r["iota"][:, :], r["sent"][:, 0, bass.ds(T.t, 1)], None,
                                  ALU.is_equal).then_inc(one_ready, 1)

            def both(T):
                dve.wait_ge(one_ready, T.t + 1)
                wait(dve, moved, T.t - 1)
                vec.scalar_tensor_tensor(dispatch[:, T.par, :], r["iota"][:, :], r["sent"][:, 1, bass.ds(T.t, 1)], one[:, T.par, :],
                                         ALU.is_equal, ALU.add).then_inc(matrix, 1)

            pipeline(dve, [(first_choice, 0), (both, 1)], NT)

        @block.gpsimd
        def _(pool):
            def stage(T):
                wait(pool, moved, T.t - 1)
                nc.gpsimd.tensor_copy(xn_now[:, T.par, :], r["xn"][:, bass.ds(T.t * D, D)]).then_inc(staged, 1)

            pipeline(pool, [(stage, 0)], NT)

        @block.scalar
        def _(act):
            act.wait_ge(shift_ready, 2)
            nc.scalar.activation(shifted[:, :, :], shifted[:, :, :], ACT.Exp).then_inc(exp_done, 1)
            nc.scalar.activation(gap[:, :], gap[:, :], ACT.Exp).then_inc(exp_done, 1)

            def out(T):
                act.wait_ge(moved, T.t + 1)
                nc.scalar.copy(r["slotsT"][:, :, bass.ds(T.t * 2, 2), :].rearrange("p e b s -> p b e s"),
                               X_ps[T.par][:, 0:2 * SLOTS].rearrange("p (b e s) -> p b e s", b=2, e=E1)).then_inc(moved_out, 1)

            pipeline(act, [(out, 0)], NT)

        @block.tensor
        def _(pe):
            for k in range(2):
                pe.wait_ge(chosen_ready, k + 1)
                last = nc.tensor.matmul(R_ps[k][:, :, :], r["before"][:, :], chosen_bf[:, k, :, :], start=True, stop=k == 0)
                if k == 0:
                    last.then_inc(ranked, 1)
            nc.tensor.matmul(R_ps[1][:, :, :], r["ones"][:, :], chosen_bf[:, 0, :, :], start=False, stop=True).then_inc(ranked, 1)

            def move(T):
                pe.wait_ge(matrix, T.t + 1)
                pe.wait_ge(staged, T.t + 1)
                wait(pe, moved_out, T.t - 1)
                nc.tensor.matmul(X_ps[T.par][:, 0:2 * SLOTS], xn_now[:, T.par, :], dispatch[:, T.par, :], start=True,
                                 stop=True).then_inc(moved, 1)

            pipeline(pe, [(move, 0)], NT)


def experts0(nc, r):
    with ExitStack() as ctx:
        def sb(name, shape, dt=F32):
            return ctx.enter_context(nc.sbuf_tensor("f0_" + name, shape, dt))

        def ps(name, shape, dt=F32):
            return ctx.enter_context(nc.psum_tensor("f0_" + name, shape, dt))

        def sem(name):
            return ctx.enter_context(nc.semaphore("f0_" + name))

        w1, w2, b1, b2, weights_in = (r["f0"][n] for n in ("w1", "w2", "b1", "b2", "in"))
        zeros = sb("zeros", [P, D])
        counts = sb("counts", [P, E0])
        filled = sb("filled", [P, E0], I32)
        over = sb("over", [P, E0, NT])
        tiles = sb("tiles", [P, E0])
        ends = sb("ends", [P, E0])
        ends_of = sb("ends_of", [P, E0, E0])
        passed = sb("passed", [P, MAX_TILES, E0])
        behind = sb("behind", [P, MAX_TILES, E0])
        n_passed = sb("n_passed", [P, MAX_TILES])
        n_behind = sb("n_behind", [P, MAX_TILES])
        first = sb("first", [P, MAX_TILES])
        row_tab = sb("row_tab", [P, MAX_TILES], I32)
        expert_tab = sb("expert_tab", [P, MAX_TILES], I32)
        closer = sb("closer", [P, E0])
        beyond = sb("beyond", [P, NT, E0 - 1])
        moved = sb("moved", [P, NT])
        table = sem("table")
        chain = sem("chain")
        zeroed = sem("zeroed")
        rows_zeroed = sem("rows_zeroed")
        rows = sb("rows", [P, 2, D])
        rowsT = sb("rowsT", [P, 2, P])
        w1_now = sb("w1_now", [P, 2, HID0])
        hid = sb("hid", [P, 2, NC0, P])
        done = sb("done", [P, 2, D])
        T_ps = [ps(f"T_ps{n}", [P, 512]) for n in range(2)]
        H_ps = [ps(f"H_ps{n}", [P, NC0, P]) for n in range(2)]
        Y_ps = [ps(f"Y_ps{n}", [P, 512]) for n in range(2)]
        rows_in = [sem("rows_in0"), sem("rows_in1")]
        turned = sem("turned")
        turned_out = sem("turned_out")
        w1_ready = sem("w1_ready")
        hidden = sem("hidden")
        biased = sem("biased")
        gelu_done = sem("gelu_done")
        y_ready = sem("y_ready")
        y_out = sem("y_out")
        stored = [sem("stored0"), sem("stored1")]
        vec, pool, act, pe, sp = nc.vector, nc.gpsimd, nc.scalar, nc.tensor, nc.sync
        block = ctx.enter_context(nc.Block())

        @block.vector
        def _(dve):
            step = Chain(dve, chain, 0, 20)
            vec.memset(zeros[:, :], 0.0).then_inc(zeroed, 1)
            step(vec.tensor_copy(filled[:, :], r["start"][:, :]))
            step(vec.tensor_tensor(counts[:, :], r["start"][:, :], r["region"][:, :], ALU.subtract))
            step(vec.tensor_tensor(over[:, :, :], counts[:, :].unsqueeze(2).to_broadcast([P, E0, NT]),
                                   r["edges"][:, :].unsqueeze(1).to_broadcast([P, E0, NT]), ALU.is_gt))
            step(vec.tensor_reduce(tiles[:, :], over[:, :, :], X, ALU.add))
            step(vec.tensor_tensor(ends_of[:, :, :], tiles[:, :].unsqueeze(1).to_broadcast([P, E0, E0]),
                                   r["upto"][:, :].rearrange("p (a b) -> p a b", a=E0), ALU.mult))
            step(vec.tensor_reduce(ends[:, :], ends_of[:, :, :], X, ALU.add))
            step(vec.tensor_tensor(passed[:, :, :], r["tile_no"][:, :].unsqueeze(2).to_broadcast([P, MAX_TILES, E0]),
                                   ends[:, :].unsqueeze(1).to_broadcast([P, MAX_TILES, E0]), ALU.is_ge))
            step(vec.tensor_tensor(behind[:, :, :], passed[:, :, :],
                                   tiles[:, :].unsqueeze(1).to_broadcast([P, MAX_TILES, E0]), ALU.mult))
            step(vec.tensor_reduce(n_passed[:, :], passed[:, :, :], X, ALU.add))
            step(vec.tensor_reduce(n_behind[:, :], behind[:, :, :], X, ALU.add))
            step(vec.tensor_tensor(first[:, :], r["tile_no"][:, :], n_behind[:, :], ALU.subtract))
            step(vec.tensor_scalar(first[:, :], first[:, :], float(P), None, ALU.mult))
            step(vec.scalar_tensor_tensor(first[:, :], n_passed[:, :], float(REGION), first[:, :], ALU.mult, ALU.add))
            step(vec.tensor_copy(row_tab[:, :], first[:, :]))
            step(vec.tensor_scalar(expert_tab[:, :], n_passed[:, :], float(E0 - 1), None, ALU.min))
            step(vec.tensor_scalar(closer[:, :], tiles[:, :], float(P), -float(REGION), ALU.mult, ALU.add))
            step(vec.tensor_tensor(beyond[:, :, :], r["row_all"][:, :].unsqueeze(2).to_broadcast([P, NT, E0 - 1]),
                                   r["region"][:, 1:E0].unsqueeze(1).to_broadcast([P, NT, E0 - 1]), ALU.is_ge))
            step(vec.tensor_tensor(beyond[:, :, :], beyond[:, :, :],
                                   closer[:, 0:E0 - 1].unsqueeze(1).to_broadcast([P, NT, E0 - 1]), ALU.mult))
            step(vec.tensor_reduce(moved[:, :], beyond[:, :, :], X, ALU.add))
            vec.tensor_tensor(r["row_all"][:, :], r["row_all"][:, :], moved[:, :], ALU.add).then_inc(table, 1)


            def bias(T):
                e = dve.value_load(expert_tab[0:1, bass.ds(T.t, 1)], min_val=0, max_val=E0 - 1)
                dve.wait_ge(hidden, T.t + 1)
                wait(dve, y_ready, T.t - 1)
                vec.tensor_tensor(hid[:, T.par, :, :], H_ps[T.par][:, :, :],
                                  b1[:, bass.ds(e, 1), :].rearrange("p a c -> p (a c)").unsqueeze(2).to_broadcast([P, NC0, P]),
                                  ALU.add).then_inc(biased, 1)

            def finish(T):
                e = dve.value_load(expert_tab[0:1, bass.ds(T.t, 1)], min_val=0, max_val=E0 - 1)
                dve.wait_ge(y_ready, T.t + 1)
                wait(dve, stored[T.par], T.half * 16)
                vec.tensor_tensor(done[:, T.par, :], Y_ps[T.par][:, 0:D],
                                  b2[:, bass.ds(e, 1), :].rearrange("p a c -> p (a c)"), ALU.add).then_inc(y_out, 1)

            dve.wait_ge(weights_in, 16 * 4)
            pipeline(dve, [(bias, 1), (finish, 3)], MAX_TILES)

        @block.sync
        def _(sp):
            sp.wait_ge(zeroed, 1)
            sp.dma_start(r["sorted"][E0 * REGION:ROWS, :].rearrange("(n p) d -> p n d", p=P),
                         zeros[:, :].unsqueeze(1).to_broadcast([P, MAX_TILES - NT, D])).then_inc(rows_zeroed, 16)
            sp.wait_ge(chain, 1)
            for e in range(0, E0, 2):
                row = sp.value_load(filled[0:1, e:e + 1], min_val=0, max_val=ROWS - P)
                sp.dma_start(r["sorted"][bass.ds(row, P), :], zeros[:, :]).then_inc(rows_zeroed, 16)
            sp.wait_ge(table, 1)
            sp.wait_ge(rows_zeroed, 16 * (E0 + 1))

            def load(T):
                row = sp.value_load(row_tab[0:1, bass.ds(T.t, 1)], min_val=0, max_val=ROWS - P)
                wait(sp, turned, T.t - 1)
                sp.dma_start(rows[:, T.par, :], r["sorted"][bass.ds(row, P), :]).then_inc(rows_in[T.par], 16)

            def store(T):
                sp.wait_ge(y_out, T.t + 1)
                sp.dma_start(r["expert_out"][bass.ds(T.t * P, P), :], done[:, T.par, :]).then_inc(stored[T.par], 16)

            pipeline(sp, [(load, 0), (store, 6)], MAX_TILES)
            sp.wait_ge(stored[0], 16 * ((MAX_TILES + 1) // 2))
            sp.wait_ge(stored[1], 16 * (MAX_TILES // 2))

        @block.gpsimd
        def _(pool):
            def weights(T):
                e = pool.value_load(expert_tab[0:1, bass.ds(T.t, 1)], min_val=0, max_val=E0 - 1)
                wait(pool, hidden, T.t - 1)
                pool.tensor_copy(w1_now[:, T.par, :], w1[:, bass.ds(e, 1), :].rearrange("p a c -> p (a c)")).then_inc(w1_ready, 1)

            pool.wait_ge(table, 1)
            pool.wait_ge(weights_in, 16 * 4)
            pipeline(pool, [(weights, 0)], MAX_TILES)

        @block.scalar
        def _(act):
            def turn_out(T):
                act.wait_ge(turned, T.t + 1)
                wait(act, hidden, T.t - 1)
                nc.scalar.copy(rowsT[:, T.par, :], T_ps[T.par][:, 0:P]).then_inc(turned_out, 1)

            def gelu(T):
                act.wait_ge(biased, T.t + 1)
                nc.scalar.activation(hid[:, T.par, :, :], hid[:, T.par, :, :], ACT.Gelu).then_inc(gelu_done, 1)

            act.wait_ge(zeroed, 1)
            act.wait_ge(chain, 1)
            for e in range(1, E0, 2):
                row = act.value_load(filled[0:1, e:e + 1], min_val=0, max_val=ROWS - P)
                act.dma_start(r["sorted"][bass.ds(row, P), :], zeros[:, :]).then_inc(rows_zeroed, 16)
            pipeline(act, [(gelu, 2), (turn_out, 0)], MAX_TILES)

        @block.tensor
        def _(pe):
            def turn(T):
                pe.wait_ge(rows_in[T.par], (T.half + 1) * 16)
                wait(pe, turned_out, T.t - 1)
                nc.tensor.transpose(T_ps[T.par][:, 0:P], rows[:, T.par, :], r["ident"][:, :]).then_inc(turned, 1)

            def up(T):
                pe.wait_ge(turned_out, T.t + 1)
                pe.wait_ge(w1_ready, T.t + 1)
                wait(pe, biased, T.t - 1)
                for n in range(NC0):
                    last = nc.tensor.matmul(H_ps[T.par][:, n, :], w1_now[:, T.par, n * P:(n + 1) * P], rowsT[:, T.par, :],
                                            start=True, stop=True)
                last.then_inc(hidden, 1)

            def down(T):
                e = pe.value_load(expert_tab[0:1, bass.ds(T.t, 1)], min_val=0, max_val=E0 - 1)
                pe.wait_ge(gelu_done, T.t + 1)
                wait(pe, y_out, T.t - 1)
                for n in range(NC0):
                    last = nc.tensor.matmul(Y_ps[T.par][:, 0:D], hid[:, T.par, n, :],
                                            w2[:, bass.ds(e, 1), n, :].rearrange("p a c -> p (a c)"),
                                            start=n == 0, stop=n == NC0 - 1)
                last.then_inc(y_ready, 1)

            pe.wait_ge(table, 1)
            pe.wait_ge(weights_in, 16 * 4)
            pipeline(pe, [(turn, 0), (up, 1), (down, 3)], MAX_TILES)


def experts1(nc, r, outT):
    N = B * CAP
    with ExitStack() as ctx:
        def sb(name, shape, dt=F32):
            return ctx.enter_context(nc.sbuf_tensor("f1_" + name, shape, dt))

        def sem(name):
            return ctx.enter_context(nc.semaphore("f1_" + name))

        gate, fc, proj, weights_in = (r["f1"][n] for n in ("gate", "fc", "proj", "in"))
        silu = sb("silu", [P, 2, N])
        hid = sb("hid", [P, 2, N])
        G_ps = [ctx.enter_context(nc.psum_tensor(f"f1_G_ps{n}", [P, N], F32)) for n in range(2)]
        F_ps = [ctx.enter_context(nc.psum_tensor(f"f1_F_ps{n}", [P, N], F32)) for n in range(2)]
        O_ps = [ctx.enter_context(nc.psum_tensor(f"f1_O_ps{n}", [P, N], F32)) for n in range(2)]
        up = sem("up")
        silu_done = sem("silu_done")
        hid_ready = sem("hid_ready")
        down = sem("down")
        out_done = sem("out_done")
        block = ctx.enter_context(nc.Block())
        PAIRS = E1 // 2

        @block.vector
        def _(dve):
            for q in range(PAIRS):
                dve.wait_ge(silu_done, q + 1)
                wait(dve, down, 2 * (q - 1))
                nc.vector.tensor_tensor(hid[:, q % 2, :], F_ps[q % 2][:, :], silu[:, q % 2, :], ALU.mult).then_inc(hid_ready, 1)

        @block.scalar
        def _(act):
            def out(e):
                act.wait_ge(down, e + 1)
                nc.scalar.copy(outT[:, :, e, :], O_ps[e % 2][:, :].rearrange("p (b s) -> p b s", s=CAP)).then_inc(out_done, 1)

            for q in range(PAIRS + 1):
                if q < PAIRS:
                    act.wait_ge(up, q + 1)
                    wait(act, hid_ready, q - 1)
                    nc.scalar.activation(silu[:, q % 2, :], G_ps[q % 2][:, :], ACT.Silu).then_inc(silu_done, 1)
                if q > 0:
                    out(2 * q - 2)
                    out(2 * q - 1)

        @block.tensor
        def _(pe):
            pe.wait_ge(weights_in, 16 * 4)
            for q in range(PAIRS + 1):
                if q < PAIRS:
                    wait(pe, hid_ready, q - 1)
                    for w, to in ((gate, G_ps), (fc, F_ps)):
                        for half in range(2):
                            last = nc.tensor.matmul(to[q % 2][half * HID1:(half + 1) * HID1, :], w[:, 2 * q + half, :],
                                                    r["slotsT"][:, 2 * q + half, :, :].rearrange("p b s -> p (b s)"), start=True, stop=True,
                                                    skip_group_check=True)
                    last.then_inc(up, 1)
                if q > 0:
                    pe.wait_ge(hid_ready, q)
                    for e in (2 * q - 2, 2 * q - 1):
                        wait(pe, out_done, e - 1)
                        nc.tensor.matmul(O_ps[e % 2][:, :], proj[:, e, :], hid[:, (q - 1) % 2, :], start=True,
                                         stop=True).then_inc(down, 1)


def collect(nc, r, x_all, outT, out):
    with ExitStack() as ctx:
        def sb(name, shape, dt=F32):
            return ctx.enter_context(nc.sbuf_tensor("c_" + name, shape, dt))

        def sem(name):
            return ctx.enter_context(nc.semaphore("c_" + name))

        slots_now = sb("slots_now", [P, 2, 2 * SLOTS])
        one = sb("one", [P, 2, 2 * SLOTS])
        combine = sb("combine", [P, 2, 2 * SLOTS])
        combine_now = sb("combine_now", [P, 2, 2, P])
        one_ready = sem("one_ready")
        matrix = sem("matrix")
        slots = sb("slots", [P, 2, 2, D])
        final = sb("final", [P, 2, D])
        T_ps = [ctx.enter_context(nc.psum_tensor(f"c_T_ps{n}", [P, 512], F32)) for n in range(2)]
        Y_ps = [ctx.enter_context(nc.psum_tensor(f"c_Y_ps{n}", [P, 512], F32)) for n in range(2)]
        staged = sem("staged")
        turned = sem("turned")
        turned_out = sem("turned_out")
        y_ready = sem("y_ready")
        y_out = sem("y_out")
        stored = [sem("stored0"), sem("stored1")]
        block = ctx.enter_context(nc.Block())

        @block.gpsimd
        def _(pool):
            def stage(T):
                wait(pool, turned, T.t - 1)
                nc.gpsimd.tensor_copy(slots_now[:, T.par, :], outT[:, bass.ds(2 * T.t, 2), :, :].rearrange("p b e s -> p (b e s)")).then_inc(staged, 1)

            pipeline(pool, [(stage, 0)], NT)

        @block.scalar
        def _(act):
            def turn_out(T):
                act.wait_ge(turned, T.t + 1)
                wait(act, y_ready, T.t - 1)
                nc.scalar.copy(slots[:, T.par, :, :].rearrange("p b k -> p (b k)"), T_ps[T.par][:, 0:256])
                nc.scalar.copy(combine_now[:, T.par, :, :].rearrange("p b k -> p (b k)"), T_ps[T.par][:, 256:512]).then_inc(turned_out, 1)

            pipeline(act, [(turn_out, 0)], NT)

        @block.tensor
        def _(pe):
            def turn(T):
                pe.wait_ge(staged, T.t + 1)
                wait(pe, turned_out, T.t - 1)
                pe.wait_ge(matrix, T.t + 1)
                for b in range(2):
                    nc.tensor.transpose(T_ps[T.par][:, b * P:(b + 1) * P], slots_now[:, T.par, b * P:(b + 1) * P],
                                        r["ident"][:, :])
                    last = nc.tensor.transpose(T_ps[T.par][:, (2 + b) * P:(3 + b) * P], combine[:, T.par, b * P:(b + 1) * P],
                                               r["ident"][:, :])
                last.then_inc(turned, 1)

            def weigh(T):
                pe.wait_ge(turned_out, T.t + 1)
                wait(pe, y_out, T.t - 1)
                for b in range(2):
                    last = nc.tensor.matmul(Y_ps[T.par][:, 0:D], combine_now[:, T.par, b, :], slots[:, T.par, b, :],
                                            start=b == 0, stop=b == 1)
                last.then_inc(y_ready, 1)

            pipeline(pe, [(turn, 0), (weigh, 1)], NT)

        @block.vector
        def _(dve):
            def add(T):
                dve.wait_ge(y_ready, T.t + 1)
                wait(dve, stored[T.par], T.half * 16)
                nc.vector.scalar_tensor_tensor(final[:, T.par, :], Y_ps[T.par][:, 0:D], r["prob"][:, 0, bass.ds(T.t, 1)],
                                               x_all[:, bass.ds(T.t * D, D)], ALU.mult, ALU.add).then_inc(y_out, 1)

            def second_choice(T):
                wait(dve, matrix, T.t - 1)
                nc.vector.tensor_scalar(one[:, T.par, :], r["iota"][:, :], r["slot"][:, 1, bass.ds(T.t, 1)],
                                        r["prob"][:, 1, bass.ds(T.t, 1)], ALU.is_equal, ALU.mult).then_inc(one_ready, 1)

            def both(T):
                dve.wait_ge(one_ready, T.t + 1)
                wait(dve, turned, T.t - 1)
                nc.vector.scalar_tensor_tensor(combine[:, T.par, :], r["iota"][:, :], r["slot"][:, 0, bass.ds(T.t, 1)],
                                               one[:, T.par, :], ALU.is_equal, ALU.add).then_inc(matrix, 1)

            pipeline(dve, [(second_choice, 0), (both, 1), (add, 3)], NT)

        @block.sync
        def _(sp):
            def store(T):
                sp.wait_ge(y_out, T.t + 1)
                sp.dma_start(out[bass.ds(T.t * P, P), :], final[:, T.par, :]).then_inc(stored[T.par], 16)

            pipeline(sp, [(store, 0)], NT)
            for s in stored:
                sp.wait_ge(s, 16 * NT // 2)


def setup(nc, d, tg, w0, w1, columns, rows):
    with ExitStack() as own:
        def sem(name):
            return own.enter_context(nc.semaphore(name))

        bv_rows = own.enter_context(nc.sbuf_tensor("bv_rows", [P, 2, P], F32))
        B_ps = [own.enter_context(nc.psum_tensor(f"B_ps{n}", [P, 512], F32)) for n in range(2)]
        bv_laid = sem("bv_laid")
        bv_wo = sem("bv_wo")
        bo_added = sem("bo_added")
        rows_in = sem("rows_in")
        loaded = sem("weights_in")
        tanh_done = sem("tanh_done")
        block = own.enter_context(nc.Block())
        @block.sync
        def _(sp):
            sp.dma_start(rows[:, :], d["rows"].partition_broadcast(P)).then_inc(rows_in, 16)
            sp.dma_start(columns[1][:, :], d["columns1"]).then_inc(loaded, 16)

        @block.gpsimd
        def _(pool):
            for what in d["zeros"]:
                nc.gpsimd.memset(what[:, :, :], 0.0)

        @block.scalar
        def _(act):
            act.dma_start(columns[0][:, :], d["columns0"]).then_inc(loaded, 16)
            act.wait_ge(rows_in, 16)
            nc.scalar.activation(tg[:, :], w0["gates"][:, :], ACT.Tanh).then_inc(tanh_done, 1)

        @block.tensor
        def _(pe):
            for n, w in enumerate((w0, w1)):
                pe.wait_ge(bv_laid, n + 1)
                nc.tensor.matmul(B_ps[n][:, 0:D], bv_rows[:, n, :], w["wo"][:, :], start=True,
                                 stop=True).then_inc(bv_wo, 1)

        @block.vector
        def _(dve):
            nc.vector.memset(w0["minus_half"][:, :], -0.5)
            nc.vector.memset(w0["eps"][:, :], EPS)
            nc.vector.memset(d["ones_bf"][:, :], 1.0)
            dve.wait_ge(loaded, 16 * 2)
            dve.wait_ge(tanh_done, 1)
            for n, w in enumerate((w0, w1)):
                nc.vector.tensor_copy(bv_rows[:, n, :], w["bv"].to_broadcast([P, P])).then_inc(bv_laid, 1)
            for n, w in enumerate((w0, w1)):
                dve.wait_ge(bv_wo, n + 1)
                nc.vector.tensor_tensor(w["bo"][:, :], w["bo"][:, :], B_ps[n][:, 0:D], ALU.add).then_inc(bo_added, 1)
                dve.wait_ge(bo_added, n + 1)
                nc.vector.tensor_scalar(w["wo"][:, :], w["wo"][:, :], tg[:, n:n + 1], None, ALU.mult)
                nc.vector.tensor_scalar(w["bo"][:, :], w["bo"][:, :], tg[:, n:n + 1], None, ALU.mult)
            for to, what in d["casts"]:
                nc.vector.tensor_copy(to, what)


IN_COLUMNS = [[("wq", D), ("wk", D), ("wv", D), ("wo", D), ("bq", 1), ("bk", 1), ("bv", 1), ("ident", P), ("head_rows", H),
               ("ones_blk", 48), ("before0", P), ("before1", P), ("ones1", P), ("batch_slot", 1), ("router0", E0),
               ("router1", E1)],
              [("wq", D), ("wk", D), ("wv", D), ("wo", D), ("bq", 1), ("bk", 1), ("bv", 1)]]
IN_ROWS = [("gates", 4), ("bo0", D), ("bo1", D), ("iota", 2 * SLOTS), ("from_last", E1),
           ("start", E0), ("region", E0), ("edges", NT), ("upto", E0 * E0), ("tile_no", MAX_TILES)]


def width(parts):
    return sum(n for _, n in parts)


def cut(whole, parts):
    out, at = {}, 0
    for name, n in parts:
        out[name] = whole[:, at:at + n]
        at += n
    return out


def program(nc, d, out):
    with ExitStack() as ctx:
        def sb(name, shape, dt=F32):
            return ctx.enter_context(nc.sbuf_tensor(name, shape, dt))

        x_all = sb("x_all", [P, NT * D])
        tg = sb("tg", [P, 4])
        rows = sb("row_constants", [P, width(IN_ROWS)])
        columns = [sb(f"columns{n}", [P, width(IN_COLUMNS[n])]) for n in range(2)]
        w0 = cut(columns[0], IN_COLUMNS[0])
        w0.update(cut(rows, IN_ROWS))
        w1 = dict(w0)
        w1.update(cut(columns[1], IN_COLUMNS[1]))
        w0.update(bo=w0["bo0"], minus_half=sb("minus_half", [P, 1]), eps=sb("eps", [P, 1]), ident_bf=sb("ident_bf", [P, P], BF16))
        w1.update(bo=w0["bo1"], minus_half=w0["minus_half"], eps=w0["eps"])
        r0 = dict(w0)
        for name, shape, dt in (("before0_bf", [P, P], BF16), ("before1_bf", [P, P], BF16), ("ones1_bf", [P, P], BF16),
                                ("ones_bf", [P, P], BF16), ("row_all", [P, NT], F32)):
            r0[name] = sb(name, shape, dt)
        r1 = dict(r0)
        r0.update(before=r0["before0_bf"], ones=r0["ones_bf"], router=r0["router0"])
        r1.update(before=r0["before1_bf"], ones=r0["ones1_bf"], router=r0["router1"])
        r0["sorted"] = nc.dram_tensor("sorted_rows", (ROWS, D), F32, kind="Internal").ap()
        r0["expert_out"] = nc.dram_tensor("expert_out", (MAX_TILES * P, D), F32, kind="Internal").ap()
        d["casts"] = [(w0["ident_bf"][:, :], w0["ident"][:, :]), (r0["before0_bf"][:, :], r0["before0"][:, :]),
                      (r0["before1_bf"][:, :], r0["before1"][:, :]), (r0["ones1_bf"][:, :], r0["ones1"][:, :])]
        d["ones_bf"] = r0["ones_bf"]
        f1 = r1["f1"] = {"in": ctx.enter_context(nc.semaphore("f1_weights_in"))}
        for name, shape in (("gate", [P, E1, HID1]), ("fc", [P, E1, HID1]), ("proj", [P, E1, D])):
            f1[name] = sb("f1_" + name, shape)
        d["zeros"] = [f1["proj"]]
        setup(nc, d, tg, w0, w1, columns, rows)
        with ExitStack() as own:
            f0 = r0["f0"] = {"in": own.enter_context(nc.semaphore("f0_weights_in"))}
            for name, shape in (("w1", [P, E0, HID0]), ("w2", [P, E0, NC0, D]), ("b1", [P, E0, NC0]), ("b2", [P, E0, D])):
                f0[name] = own.enter_context(nc.sbuf_tensor("f0_" + name, shape, F32))

            def hooks0(env):
                h = router(nc, env, 0, r0)
                h["experts"] = [(f0["w1"][:, :, :], d["W1"].rearrange("e d h -> d e h"), f0["in"]),
                                (f0["b1"][:, :, :], d["b1"], f0["in"]),
                                (f0["b2"][:, :, :], d["b2"].partition_broadcast(P), f0["in"]),
                                (f0["w2"][:, :, :, :], d["W2"].rearrange("e (c p) d -> p e c d", p=P), f0["in"])]
                return h

            attention(nc, 0, x_all, w0, d, hooks0)
            experts0(nc, r0)
        for name in ("slot", "sent", "prob"):
            r1[name] = sb(name, [P, 2, NT])
        r1["logits"] = sb("logits1", [P, NT, E1])
        with ExitStack() as own:
            r1["slotsT"] = own.enter_context(nc.sbuf_tensor("slotsT", [P, E1, B, CAP], F32))

            def hooks(env):
                h = router(nc, env, 1, r1)
                fetched = [env["sem"]("fetched0"), env["sem"]("fetched1")]
                row_now = env["sem"]("row_now_ready")
                added = env["sem"]("ffn_added")
                row = env["sb"]("row_now", [P, 2], I32)
                back = env["sb"]("back", [P, 2, D])

                def fetch(T):
                    wait(nc.gpsimd, added, T.t - 1)
                    nc.gpsimd.tensor_copy(row[:, T.par:T.par + 1], r0["row_all"][:, bass.ds(T.t, 1)]).then_inc(row_now, 1)
                    nc.gpsimd.wait_ge(row_now, T.t + 1)
                    apart(nc.gpsimd)
                    nc.gpsimd.indirect_dma_start(back[:, T.par, :], None, r0["expert_out"],
                                                 bass.IndirectOffsetOnAxis(ap=row[:, T.par:T.par + 1], axis=0)).then_inc(fetched[T.par], 16)

                def before_norm(dve, T):
                    xt = x_all[:, bass.ds(T.t * D, D)]
                    dve.wait_ge(fetched[T.par], (T.half + 1) * 16)
                    nc.vector.scalar_tensor_tensor(xt, back[:, T.par, :], tg[:, 2:3], xt, ALU.mult, ALU.add).then_inc(added, 1)
                    dve.wait_ge(added, T.t + 1)
                    apart(dve)

                h["experts"] = [(f1["gate"][:, :, :], d["w_gate"].rearrange("e d h -> d e h"), f1["in"]),
                                (f1["fc"][:, :, :], d["w_fc"].rearrange("e d h -> d e h"), f1["in"])]
                h["experts"] += [(f1["proj"][half * HID1:(half + 1) * HID1, half:E1:2, :],
                                  d["w_proj"].rearrange("(a two) h d -> two h a d", two=2)[half], f1["in"]) for half in range(2)]
                h["pool_first"] = [(fetch, -2)]
                h["before_norm"] = before_norm
                return h

            with ExitStack() as kept:
                r1["xn"] = kept.enter_context(nc.sbuf_tensor("xn_all", [P, NT * D], F32))
                attention(nc, 1, x_all, w1, d, hooks)
                assign1(nc, r1, tg)
            outT = own.enter_context(nc.sbuf_tensor("outT", [P, B, E1, CAP], F32))
            experts1(nc, r1, outT)
            collect(nc, r1, x_all, outT, out)


def kernel(**inputs):
    import numpy as np
    import concourse.bacc as bacc
    from concourse import mybir as my
    from concourse.bass_utils import run_bass_kernel_spmd as run

    nc = bacc.Bacc("TRN2", target_bir_lowering=False, num_devices=1)
    i = {k: np.asarray(v) for k, v in inputs.items()}
    T = B * S
    arrays = {
        "x": i["x"].reshape(T, D), "ctx": i["ctx_1024"].reshape(T, D), "mask": i["mask_BxSxS2_ik1"].reshape(T, S),
    }
    parts = [{}, {}, {"gates": np.concatenate([i["g_xattn"].ravel(), i["g_ffn"].ravel()])}]

    def by_partition(a):
        return a.reshape(2, 4, 2 * DK, -1).transpose(1, 0, 2, 3).reshape(P, -1)

    for n, (q, k, v, o) in enumerate((
            (i["L0_xattn_w_q"].T, i["L0_xattn_w_k"].T, i["L0_xattn_w_v"].T, i["L0_xattn_w_o"].T),
            tuple(i["L1_xattn_in_proj_weight"][:, m * D:(m + 1) * D] for m in range(3)) + (i["L1_xattn_out_proj_weight"],))):
        parts[n].update(wq=q, wk=k, wv=v, wo=by_partition(o))
    bias = i["L1_xattn_in_proj_bias"]
    parts[0].update(bq=i["L0_xattn_b_q"], bk=i["L0_xattn_b_k"], bv=by_partition(i["L0_xattn_b_v"]))
    parts[1].update(bq=bias[:D], bk=bias[D:2 * D], bv=by_partition(bias[2 * D:]))
    parts[2].update(bo0=i["L0_xattn_b_o"], bo1=i["L1_xattn_out_proj_bias"])
    columns, rows = parts[0], parts[2]
    p = np.arange(P)
    columns["ident"] = np.eye(P, dtype=np.float32)
    columns["head_rows"] = (p[:, None] // DK == np.arange(H)[None, :]).astype(np.float32)
    col = np.arange(48)[None, :] - 16
    columns["ones_blk"] = ((p[:, None] // S == col // DK) & (col >= 0)).astype(np.float32)
    row, col = p[:, None], p[None, :]
    same = row // S == col // S
    columns["before0"] = (row < col).astype(np.float32)
    columns["before1"] = ((row < col) & same).astype(np.float32)
    columns["ones1"] = same.astype(np.float32)
    columns["batch_slot"] = (row // S * SLOTS + E1 * CAP).astype(np.float32)
    rows["from_last"] = E1 - np.arange(E1, dtype=np.float32)
    rows["iota"] = np.arange(2 * SLOTS, dtype=np.float32)
    rows["start"] = rows["region"] = np.arange(E0, dtype=np.float32) * REGION
    rows["edges"] = np.arange(NT, dtype=np.float32) * P
    rows["upto"] = np.tril(np.ones((E0, E0), np.float32)).ravel()
    rows["tile_no"] = np.arange(MAX_TILES, dtype=np.float32)
    columns["router0"] = i["L0_ffn_Wg"].T
    columns["router1"] = i["L1_ffn_w_router"]
    for n in range(2):
        arrays[f"columns{n}"] = np.concatenate([parts[n][name].reshape(P, k) for name, k in IN_COLUMNS[n]], axis=1)
    arrays["rows"] = np.concatenate([rows[name].reshape(k) for name, k in IN_ROWS])
    arrays["W1"], arrays["W2"], arrays["b2"] = i["L0_ffn_W1"], i["L0_ffn_W2"], i["L0_ffn_b2"]
    arrays["b1"] = i["L0_ffn_b1"].reshape(E0, NC0, P).transpose(2, 0, 1)
    for name in ("w_fc", "w_gate", "w_proj"):
        arrays[name] = i["L1_ffn_" + name]
    arrays = {k: np.ascontiguousarray(v) for k, v in arrays.items()}
    d = {k: nc.dram_tensor(f"in_{k}", a.shape, my.dt.from_np(a.dtype), kind="ExternalInput").ap() for k, a in arrays.items()}
    out = nc.dram_tensor("out_0", (T, D), my.dt.from_np(np.dtype("float32")), kind="ExternalOutput").ap()
    program(nc, d, out)
    r = run(nc, [{f"in_{k}": a for k, a in arrays.items()}], core_ids=[0])
    return r.results[0]["out_0"].reshape(B, S, D)
```
